# Optimizing a Trainium2 kernel written in Bass

```python
import numpy as np
import jax
import jax.numpy as jnp

def _softmax(x, axis=-1):
    return jax.nn.softmax(x, axis=axis)

def _gelu(x):
    return jax.nn.gelu(x, approximate=True)

def _silu(x):
    return jax.nn.silu(x)

def _sigmoid(x):
    return jax.nn.sigmoid(x)

def _layernorm(x, axis=-1, eps=1e-05):
    m = jnp.mean(x, axis=axis, keepdims=True)
    v = jnp.var(x, axis=axis, keepdims=True)
    return (x - m) / jnp.sqrt(v + eps)

def _scatter_add(tgt, idx, src, axis=0):
    return tgt.at[idx].add(src)

def _segment_sum(src, seg, n):
    return jax.ops.segment_sum(src, seg, n)
kernel_name = 'mk_recurrent_d2_jaxref_r8_dbd1b8'

def setup_inputs(seed: int=0):
    np.random.seed(seed)
    _w = jnp.asarray

    def _L0_attn_setup():
        import jax, jax.numpy as jnp
        import numpy as np
        H = 256
        NH = 32
        HD = H // NH
        key = jax.random.key(seed)
        ks = jax.random.split(key, 9)
        s = 1.0 / np.sqrt(H)
        return {'hidden_states': jax.random.normal(ks[0], (2, 256, H), dtype=jnp.float32), 'wq': jax.random.uniform(ks[1], (H, H), jnp.float32, -s, s), 'bq': jnp.zeros((H,), jnp.float32), 'wk': jax.random.uniform(ks[2], (H, H), jnp.float32, -s, s), 'bk': jnp.zeros((H,), jnp.float32), 'wv': jax.random.uniform(ks[3], (H, H), jnp.float32, -s, s), 'bv': jnp.zeros((H,), jnp.float32), 'wo': jax.random.uniform(ks[4], (H, H), jnp.float32, -s, s), 'bo': jnp.zeros((H,), jnp.float32)}
    _L0_attn_in = _L0_attn_setup()

    def _L0_ffn_setup():
        import jax, jax.numpy as jnp
        import numpy as np
        D = 256
        F = 176
        E = 8
        K = 2
        FS = 352
        B, S = (2, 128)
        key = jax.random.key(seed)
        ks = jax.random.split(key, 9)
        sc = 0.02
        return {'x': jax.random.normal(ks[0], (B, S, D), dtype=jnp.float32), 'Wr': jax.random.normal(ks[1], (E, D), dtype=jnp.float32) * sc, 'Wg': jax.random.normal(ks[2], (E, F, D), dtype=jnp.float32) * sc, 'Wu': jax.random.normal(ks[3], (E, F, D), dtype=jnp.float32) * sc, 'Wd': jax.random.normal(ks[4], (E, D, F), dtype=jnp.float32) * sc, 'Wsg': jax.random.normal(ks[5], (FS, D), dtype=jnp.float32) * sc, 'Wsu': jax.random.normal(ks[6], (FS, D), dtype=jnp.float32) * sc, 'Wsd': jax.random.normal(ks[7], (D, FS), dtype=jnp.float32) * sc}
    _L0_ffn_in = _L0_ffn_setup()

    def _L1_attn_setup():
        import jax, jax.numpy as jnp
        import numpy as np
        H = 16
        DK = 128
        DV = 128
        M = 64
        EPS = 1e-05
        CLAMP = 32.0
        ROPE_BASE = 10000.0

        def _rope(x, cos, sin):
            x1, x2 = jnp.split(x, 2, axis=-1)
            return jnp.concatenate([x1 * cos - x2 * sin, x2 * cos + x1 * sin], axis=-1)
        key = jax.random.key(seed)
        ks = jax.random.split(key, 9)
        B, T, D = (1, 256, 256)
        sc = 0.02
        return {'hidden_states': jax.random.normal(ks[0], (B, T, D), jnp.float32), 'Wq': jax.random.normal(ks[1], (H * DK, D), jnp.float32) * sc, 'Wk': jax.random.normal(ks[2], (H * DK, D), jnp.float32) * sc, 'Wv': jax.random.normal(ks[3], (H * DV, D), jnp.float32) * sc, 'Wg': jax.random.normal(ks[4], (H * DV, D), jnp.float32) * sc, 'Wo': jax.random.normal(ks[5], (D, H * DV), jnp.float32) * sc, 'Ws1': jax.random.normal(ks[6], (16, D), jnp.float32) * sc, 'Ws2': jax.random.normal(ks[7], (H * M, 16), jnp.float32) * sc, 'bs2': jnp.zeros((H * M,), jnp.float32), 'g_norm_weight': jnp.ones((DV,), jnp.float32)}
    _L1_attn_in = _L1_attn_setup()

    def _L1_ffn_setup():
        import jax, jax.numpy as jnp
        import numpy as np
        from jax import lax
        H = 256
        I = 176
        E = 16
        K = 4
        ISH = 2 * I
        B, S = (4, 256)

        def _router(xf, rg_w, ru_w, extra_scale, extra_bias):
            g = xf @ rg_w.T
            u = xf @ ru_w.T
            scores = jnp.abs(u * jax.nn.silu(g))
            probs = jax.nn.softmax(scores.astype(jnp.float32), axis=-1)
            biased = probs + extra_bias[None, :]
            _, idx = lax.top_k(biased, K)
            orig = 1.0 + probs * extra_scale[None, :]
            w = jnp.take_along_axis(orig, idx, axis=1).astype(xf.dtype)
            return (w, idx)
        key = jax.random.key(seed)
        ks = jax.random.split(key, 12)
        sc = 0.02
        return {'x': jax.random.normal(ks[0], (B, S, H), dtype=jnp.float32), 'rg_w': jax.random.normal(ks[1], (E, H), dtype=jnp.float32) * sc, 'ru_w': jax.random.normal(ks[2], (E, H), dtype=jnp.float32) * sc, 'extra_scale': jnp.zeros((E,), dtype=jnp.float32), 'extra_bias': jnp.zeros((E,), dtype=jnp.float32), 'Wg': jax.random.normal(ks[3], (E, I, H), dtype=jnp.float32) * sc, 'Wu': jax.random.normal(ks[4], (E, I, H), dtype=jnp.float32) * sc, 'Wd': jax.random.normal(ks[5], (E, H, I), dtype=jnp.float32) * sc, 'Sg': jax.random.normal(ks[6], (ISH, H), dtype=jnp.float32) * sc, 'Su': jax.random.normal(ks[7], (ISH, H), dtype=jnp.float32) * sc, 'Sd': jax.random.normal(ks[8], (H, ISH), dtype=jnp.float32) * sc}
    _L1_ffn_in = _L1_ffn_setup()
    _d = {'L0_attn_hidden_states': _L0_attn_in['hidden_states'], 'L0_attn_wq': _L0_attn_in['wq'], 'L0_attn_bq': _L0_attn_in['bq'], 'L0_attn_wk': _L0_attn_in['wk'], 'L0_attn_bk': _L0_attn_in['bk'], 'L0_attn_wv': _L0_attn_in['wv'], 'L0_attn_bv': _L0_attn_in['bv'], 'L0_attn_wo': _L0_attn_in['wo'], 'L0_attn_bo': _L0_attn_in['bo'], 'L0_ffn_Wr': _L0_ffn_in['Wr'], 'L0_ffn_Wg': _L0_ffn_in['Wg'], 'L0_ffn_Wu': _L0_ffn_in['Wu'], 'L0_ffn_Wd': _L0_ffn_in['Wd'], 'L0_ffn_Wsg': _L0_ffn_in['Wsg'], 'L0_ffn_Wsu': _L0_ffn_in['Wsu'], 'L0_ffn_Wsd': _L0_ffn_in['Wsd'], 'L1_attn_Wq': _L1_attn_in['Wq'], 'L1_attn_Wk': _L1_attn_in['Wk'], 'L1_attn_Wv': _L1_attn_in['Wv'], 'L1_attn_Wg': _L1_attn_in['Wg'], 'L1_attn_Wo': _L1_attn_in['Wo'], 'L1_attn_Ws1': _L1_attn_in['Ws1'], 'L1_attn_Ws2': _L1_attn_in['Ws2'], 'L1_attn_bs2': _L1_attn_in['bs2'], 'L1_attn_g_norm_weight': _L1_attn_in['g_norm_weight'], 'L1_ffn_rg_w': _L1_ffn_in['rg_w'], 'L1_ffn_ru_w': _L1_ffn_in['ru_w'], 'L1_ffn_extra_scale': _L1_ffn_in['extra_scale'], 'L1_ffn_extra_bias': _L1_ffn_in['extra_bias'], 'L1_ffn_Wg': _L1_ffn_in['Wg'], 'L1_ffn_Wu': _L1_ffn_in['Wu'], 'L1_ffn_Wd': _L1_ffn_in['Wd'], 'L1_ffn_Sg': _L1_ffn_in['Sg'], 'L1_ffn_Su': _L1_ffn_in['Su'], 'L1_ffn_Sd': _L1_ffn_in['Sd']}
    _x0 = _d['L0_attn_hidden_states']
    _d['L0_attn_hidden_states'] = jax.random.normal(jax.random.fold_in(jax.random.key(seed), 1), (8, 256, 256), dtype=_x0.dtype)
    del _x0
    return _d

def reference(L0_attn_hidden_states, L0_attn_wq, L0_attn_bq, L0_attn_wk, L0_attn_bk, L0_attn_wv, L0_attn_bv, L0_attn_wo, L0_attn_bo, L0_ffn_Wr, L0_ffn_Wg, L0_ffn_Wu, L0_ffn_Wd, L0_ffn_Wsg, L0_ffn_Wsu, L0_ffn_Wsd, L1_attn_Wq, L1_attn_Wk, L1_attn_Wv, L1_attn_Wg, L1_attn_Wo, L1_attn_Ws1, L1_attn_Ws2, L1_attn_bs2, L1_attn_g_norm_weight, L1_ffn_rg_w, L1_ffn_ru_w, L1_ffn_extra_scale, L1_ffn_extra_bias, L1_ffn_Wg, L1_ffn_Wu, L1_ffn_Wd, L1_ffn_Sg, L1_ffn_Su, L1_ffn_Sd):

    def _L0_attn_ref(hidden_states, wq, bq, wk, bk, wv, bv, wo, bo):
        import jax, jax.numpy as jnp
        import numpy as np
        H = 256
        NH = 32
        HD = H // NH
        B, S, _ = hidden_states.shape

        def heads(x):
            return x.reshape(B, S, NH, HD).transpose(0, 2, 1, 3)
        q = heads(hidden_states @ wq.T + bq)
        k = heads(hidden_states @ wk.T + bk)
        v = heads(hidden_states @ wv.T + bv)
        scores = jnp.einsum('bhqd,bhkd->bhqk', q, k) / np.sqrt(HD).astype(np.float32)
        causal = jnp.tril(jnp.ones((S, S), dtype=bool))
        scores = jnp.where(causal, scores, -jnp.inf)
        attn = jax.nn.softmax(scores, axis=-1)
        out = jnp.einsum('bhqk,bhkd->bhqd', attn, v)
        out = out.transpose(0, 2, 1, 3).reshape(B, S, H)
        return out @ wo.T + bo

    def _L0_ffn_ref(x, Wr, Wg, Wu, Wd, Wsg, Wsu, Wsd):
        import jax, jax.numpy as jnp
        import numpy as np
        D = 256
        F = 176
        E = 8
        K = 2
        FS = 352
        B, S = (2, 128)
        silu = jax.nn.silu
        sg = silu(jnp.einsum('bsd,fd->bsf', x, Wsg))
        su = jnp.einsum('bsd,fd->bsf', x, Wsu)
        shared_out = jnp.einsum('bsf,df->bsd', sg * su, Wsd)
        logits = jnp.einsum('bsd,ed->bse', x, Wr)
        scores = jax.nn.softmax(logits, axis=-1)
        topk_scores, topk_idx = jax.lax.top_k(scores, K)
        w_full = jnp.sum(jax.nn.one_hot(topk_idx, E, dtype=x.dtype) * topk_scores[..., None], axis=-2)
        g = silu(jnp.einsum('bsd,efd->bsef', x, Wg))
        u = jnp.einsum('bsd,efd->bsef', x, Wu)
        out_e = jnp.einsum('bsef,edf->bsed', g * u, Wd)
        routed_out = jnp.einsum('bsed,bse->bsd', out_e, w_full)
        return routed_out + shared_out

    def _L1_attn_ref(hidden_states, Wq, Wk, Wv, Wg, Wo, Ws1, Ws2, bs2, g_norm_weight):
        import jax, jax.numpy as jnp
        import numpy as np
        H = 16
        DK = 128
        DV = 128
        M = 64
        EPS = 1e-05
        CLAMP = 32.0
        ROPE_BASE = 10000.0

        def _rope(x, cos, sin):
            x1, x2 = jnp.split(x, 2, axis=-1)
            return jnp.concatenate([x1 * cos - x2 * sin, x2 * cos + x1 * sin], axis=-1)
        B, T, D = hidden_states.shape
        hs = hidden_states
        q = (hs @ Wq.T).reshape(B, T, H, DK)
        k = (hs @ Wk.T).reshape(B, T, H, DK)
        pos = jnp.arange(T, dtype=jnp.float32)
        inv_freq = 1.0 / ROPE_BASE ** (jnp.arange(0, DK, 2, dtype=jnp.float32) / DK)
        ang = pos[:, None] * inv_freq[None, :]
        cos = jnp.cos(ang)[None, :, None, :]
        sin = jnp.sin(ang)[None, :, None, :]
        q = _rope(q, cos, sin).transpose(0, 2, 1, 3)
        k = _rope(k, cos, sin).transpose(0, 2, 1, 3)
        v = (hs @ Wv.T).reshape(B, T, H, DV).transpose(0, 2, 1, 3)
        s = hs @ Ws1.T @ Ws2.T + bs2
        s = jnp.clip(s, -CLAMP, CLAMP).reshape(B, T, H, M).transpose(0, 2, 1, 3)
        z = jax.lax.cumlogsumexp(s, axis=2)
        es = jnp.exp(s)
        enz = jnp.exp(-z)
        scale = DK ** (-0.5)
        mask = jnp.tril(jnp.ones((T, T), dtype=bool))
        A = jnp.einsum('bhtd,bhjd->bhtj', q, k) * scale
        A = jnp.where(mask, A, 0.0)
        ok = enz * jnp.einsum('bhtj,bhjm->bhtm', A, es)
        qv = jax.nn.softmax(ok, axis=-1)
        W2 = jnp.einsum('bhtm,bhjm->bhtj', qv * enz, es)
        W2 = jnp.where(mask, W2, 0.0)
        o = jnp.einsum('bhtj,bhjd->bhtd', W2, v)
        o = o.transpose(0, 2, 1, 3)
        g = (hs @ Wg.T).reshape(B, T, H, DV)
        o_n = o * jax.lax.rsqrt(jnp.mean(o * o, axis=-1, keepdims=True) + EPS) * g_norm_weight
        o_g = o_n * (g * jax.nn.sigmoid(g))
        return o_g.reshape(B, T, H * DV) @ Wo.T

    def _L1_ffn_ref(x, rg_w, ru_w, extra_scale, extra_bias, Wg, Wu, Wd, Sg, Su, Sd):
        import jax, jax.numpy as jnp
        import numpy as np
        from jax import lax
        H = 256
        I = 176
        E = 16
        K = 4
        ISH = 2 * I
        B, S = (4, 256)

        def _router(xf, rg_w, ru_w, extra_scale, extra_bias):
            g = xf @ rg_w.T
            u = xf @ ru_w.T
            scores = jnp.abs(u * jax.nn.silu(g))
            probs = jax.nn.softmax(scores.astype(jnp.float32), axis=-1)
            biased = probs + extra_bias[None, :]
            _, idx = lax.top_k(biased, K)
            orig = 1.0 + probs * extra_scale[None, :]
            w = jnp.take_along_axis(orig, idx, axis=1).astype(xf.dtype)
            return (w, idx)
        shape = x.shape
        xf = x.reshape(-1, H)
        w, idx = _router(xf, rg_w, ru_w, extra_scale, extra_bias)
        coeff = jnp.einsum('tk,tke->te', w, jax.nn.one_hot(idx, E, dtype=w.dtype))

        def step(y, ew):
            wg, wu, wd, c = ew
            h = jax.nn.silu(xf @ wg.T) * (xf @ wu.T)
            return (y + h @ wd.T * c[:, None], None)
        y0 = jnp.zeros_like(xf)
        y, _ = lax.scan(step, y0, (Wg, Wu, Wd, coeff.T))
        z = jax.nn.silu(xf @ Sg.T) * (xf @ Su.T) @ Sd.T
        return (y + z).reshape(shape)
    x = L0_attn_hidden_states
    xn = _layernorm(x, axis=-1)
    s = _L0_attn_ref(xn, L0_attn_wq, L0_attn_bq, L0_attn_wk, L0_attn_bk, L0_attn_wv, L0_attn_bv, L0_attn_wo, L0_attn_bo)
    g = _silu(_L0_ffn_ref(xn, L0_ffn_Wr, L0_ffn_Wg, L0_ffn_Wu, L0_ffn_Wd, L0_ffn_Wsg, L0_ffn_Wsu, L0_ffn_Wsd))
    x = x + s * g
    xn = _layernorm(x, axis=-1)
    s = _L1_attn_ref(xn, L1_attn_Wq, L1_attn_Wk, L1_attn_Wv, L1_attn_Wg, L1_attn_Wo, L1_attn_Ws1, L1_attn_Ws2, L1_attn_bs2, L1_attn_g_norm_weight)
    g = _silu(_L1_ffn_ref(xn, L1_ffn_rg_w, L1_ffn_ru_w, L1_ffn_extra_scale, L1_ffn_extra_bias, L1_ffn_Wg, L1_ffn_Wu, L1_ffn_Wd, L1_ffn_Sg, L1_ffn_Su, L1_ffn_Sd))
    x = x + s * g
    return x

_drawn_inputs = setup_inputs


def setup_inputs(seed=0):
    import zlib

    import numpy as np

    out = dict(_drawn_inputs(seed))
    spreads = {'L0_attn_bq': (0.0, 0.8),
     'L0_attn_bk': (0.0, 0.8),
     'L0_attn_bv': (0.0, 0.8),
     'L0_attn_bo': (0.0, 0.8),
     'L1_attn_bs2': (0.0, 0.8),
     'L1_attn_g_norm_weight': (1.0, 0.6),
     'L1_ffn_extra_scale': (0.0, 0.8),
     'L1_ffn_extra_bias': (0.0, 0.8)}
    factors = {'L0_attn_wq': 8.0,
     'L0_attn_wk': 8.0,
     'L0_attn_wv': 8.0,
     'L0_attn_wo': 8.0,
     'L0_ffn_Wr': 8.0,
     'L0_ffn_Wg': 8.0,
     'L0_ffn_Wu': 8.0,
     'L0_ffn_Wd': 8.0,
     'L0_ffn_Wsg': 8.0,
     'L0_ffn_Wsu': 8.0,
     'L0_ffn_Wsd': 8.0,
     'L1_attn_Wq': 8.0,
     'L1_attn_Wk': 8.0,
     'L1_attn_Wv': 8.0,
     'L1_attn_Wg': 8.0,
     'L1_attn_Wo': 8.0,
     'L1_attn_Ws1': 8.0,
     'L1_attn_Ws2': 8.0,
     'L1_ffn_rg_w': 8.0,
     'L1_ffn_ru_w': 8.0,
     'L1_ffn_Wg': 8.0,
     'L1_ffn_Wu': 8.0,
     'L1_ffn_Wd': 8.0,
     'L1_ffn_Sg': 8.0,
     'L1_ffn_Su': 8.0,
     'L1_ffn_Sd': 8.0}
    for name, (base, spread) in spreads.items():
        noise = np.random.default_rng([zlib.crc32(name.encode()), seed]).standard_normal(out[name].shape)
        drawn = base * np.exp(spread * noise) if base else spread * noise
        out[name] = jnp.asarray(drawn.astype(out[name].dtype))
    for name, factor in factors.items():
        out[name] = (out[name] * factor).astype(out[name].dtype)
    return out
```

```python
from contextlib import ExitStack

import numpy as np

import concourse.bass as bass
from concourse import mybir

F32 = mybir.dt.float32
BF16 = mybir.dt.bfloat16
ALU = mybir.AluOpType
ACT = mybir.ActivationFunctionType
AX = mybir.AxisListType

P = 128
BATCH, SEQ, D = 8, 256, 256
TOK = BATCH * SEQ
KC = D // P
TILES = TOK // P
CH = 512
TURNS = TOK // CH
CT = CH // P
ST = SEQ // P
EPS = 1e-5
NEG = -1.0e30

NH0, HD0 = 32, 8
HPQ = 4
PAIRS = NH0 // 2
SLOTS = 2 * PAIRS
BLK = 3 * P
RING = 3
LAG = 2

E0, F0, K0, FS0 = 8, 176, 2, 352
E1, F1, K1, FS1 = 16, 176, 4, 352
NT0 = -(-(E0 * F0 + FS0) // P)
NT1 = -(-(E1 * F1 + FS1) // P)
WT = 2 * KC * P + D

NH1, DK, M = 16, 128, 64
HW = KC * (DK + DK + 2 * DK)
R1 = 16
SCALE1 = DK ** -0.5
CLAMP = 32.0
PAIR1 = NH1 // 2

W0Q, W0F = 0, 4 * KC * D
W1O = NH1 * HW
WCOLS = W1O + NH1 * D
assert W0F + NT0 * WT <= WCOLS and NT1 * WT <= WCOLS


def w1_head(h):
    return (NH1 - 1 - h) * HW


class Count:

    def __init__(self, sem, per):
        self.sem, self.per = sem, per

    def at(self, turn, n):
        return turn * self.per + n


def build(nc, A, out, phases=3):
    with ExitStack() as ctx:
        def sb(name, shape, dt=F32):
            return ctx.enter_context(nc.sbuf_tensor(name, shape, dt))

        def sem(name):
            return ctx.enter_context(nc.semaphore(name))

        def count(name, per):
            return Count(sem(name), per)

        ps = ctx.enter_context(nc.psum_tensor("ps", [P, 8, 512], F32))

        x_res = sb("x_res", [P, TILES, D])
        weights = sb("weights", [P, WCOLS])
        ident = sb("ident", [P, P])
        causal = sb("causal", [P, BLK])
        sel0 = sb("sel0", [3 * (E0 + 1), NT0 * P], BF16)
        sel1 = sb("sel1", [3 * (E1 + 1), NT1 * P], BF16)
        cols = sb("cols", [P, 16])
        bkm = sb("bkm", [P, HPQ])
        bqs = sb("bqs", [P, KC])
        router0 = sb("router0", [P, KC, E0])
        lower0 = sb("lower0", [P, E0 * E0])
        lower1 = sb("lower1", [P, E1 * E1])
        router1 = sb("router1", [P, KC, 2 * E1])
        expert_rows = sb("expert_rows", [P, 2, E1])
        minus_half = sb("minus_half", [P, 64])
        rope = sb("rope", [P, 2, SEQ])
        tri = sb("tri", [P, P])
        ones = sb("ones", [P, P])
        keep_a = sb("keep_a", [P, BLK])
        keep_w = sb("keep_w", [P, BLK])
        s1w = sb("s1w", [P, KC, R1])
        s2w = sb("s2w", [R1, NH1 * M])
        s2b = sb("s2b", [P, NH1 * M])
        g_norm = sb("g_norm", [P, DK])
        g_half = sb("g_half", [P, DK])
        LEFT = (nc.sbuf_bytes_remaining // 4) - 64
        work = sb("work", [P, LEFT])
        sT1 = work[:, LEFT - KC * TOK:LEFT].rearrange("p (k t) -> p k t", k=KC)
        room = {"layer0": LEFT, "slots": LEFT - KC * TOK, "experts": LEFT - KC * TOK}
        used = {"layer0": 0, "slots": 0, "experts": 0}

        def carve(loop, *shape, parts=P, dt=F32):
            n = int(np.prod(shape))
            words = n if dt is F32 else (n + 1) // 2
            at = used[loop]
            used[loop] += words
            assert used[loop] <= room[loop], (loop, used[loop], room[loop])
            ap = work[0:parts, at:at + words]
            if dt is not F32:
                ap = ap.bitcast(dt)
            if len(shape) == 1:
                return ap
            names = "abcd"[:len(shape)]
            return ap.rearrange(f"p ({' '.join(names)}) -> p {' '.join(names)}",
                                **dict(zip(names, shape)))

        MASK = cols[:, 0:4]
        BQ, BK, BV, BO = (cols[:, 4 + 2 * i:6 + 2 * i] for i in range(4))

        x_loaded, consts_loaded, w0_loaded = sem("x_loaded"), sem("consts_loaded"), sem("w0_loaded")
        f0_loaded = sem("f0_loaded")
        casts_done, bias_done, pow_rows = sem("casts_done"), sem("bias_done"), sem("pow_rows")

        class MoE:

            def __init__(self, loop, experts, top, tiles, sel, lower, per_token):
                self.loop, self.E, self.top, self.NT, self.sel, self.lower = loop, experts, top, tiles, sel, lower
                self.per_token = per_token
                n = loop
                self.logits_done = count(n + "_logits_done", 1)
                self.tokens_done = count(n + "_tokens_done", 1)
                self.coef_turned = count(n + "_coef_turned", 1)
                self.gate_up_done = count(n + "_gate_up_done", tiles)
                self.coef_done = count(n + "_coef_done", tiles)
                self.down_done = count(n + "_down_done", tiles)
                self.delta_turned = count(n + "_delta_turned", 1)
                self.logits_copied = count(n + "_logits_copied", 1)
                self.router_act = count(n + "_router_act", 1 if per_token == 1 else 2)
                self.coef_copied = count(n + "_coef_copied", 1)
                self.tanh_done = count(n + "_tanh_done", tiles)
                self.out_tanh = count(n + "_out_tanh", KC)
                self.router_step = count(n + "_router_step", 11 if per_token == 1 else 17)
                self.coef_ready = count(n + "_coef_ready", 1)
                self.half_step = count(n + "_half_step", 2 * tiles)
                self.hidden_ready = count(n + "_hidden_ready", tiles)
                self.out_step = count(n + "_out_step", KC)
                self.delta_ready = count(n + "_delta_ready", 1)
                self.x_ready = count(n + "_x_ready", 2)
                self.split_step = count(n + "_split_step", 6)
                self.split_ready = count(n + "_split_ready", 1)
                E, c = experts, carve
                self.lg_sb = c(loop, CH)
                self.tok = [c(loop, CT, E) for _ in range(3)]
                self.cmp = [c(loop, CT, E, E) for _ in range(2)]
                self.small = c(loop, 4, CT)
                self.coef = c(loop, CT, E + 1)
                self.part = c(loop, CT, 3, E + 1)
                self.rest = c(loop, CT, E + 1)
                self.narrow = c(loop, CT * (E + 1) + 1, dt=BF16)[:, 0:CT * (E + 1)].rearrange(
                    "p (a b) -> p a b", a=CT)
                self.coefT = c(loop, CH, dt=BF16)
                self.th = c(loop, 2, CH)
                self.half = c(loop, CH)
                self.both = c(loop, CH)
                self.hidden = c(loop, 2, CH)
                self.out_th = c(loop, KC, CH)
                self.delta = self.out_th

            def w(self, j):
                w0 = (W0F if self.loop == "layer0" else 0) + j * WT
                return weights[:, w0:w0 + WT]

            def gate_w(self, j, kc):
                return self.w(j)[:, kc * P:(kc + 1) * P]

            def up_w(self, j, kc):
                return self.w(j)[:, (KC + kc) * P:(KC + kc + 1) * P]

            def down_w(self, j, mt):
                return self.w(j)[:, 2 * KC * P + mt * P:2 * KC * P + (mt + 1) * P]

            def pe_logits(self, pe, t, xT, rw):
                n = self.E * self.per_token
                for kc in range(KC):
                    last = pe.matmul(ps[0:n, 6, :], rw[:, kc, :], xT[:, kc, :], start=kc == 0, stop=kc == KC - 1)
                last.then_inc(self.logits_done.sem, 1)

            def pe_gate_up(self, pe, t, j, xT):
                b = j % 2
                if j >= 2:
                    pe.wait_ge(self.hidden_ready.sem, self.hidden_ready.at(t, j - 1))
                for kc in range(KC):
                    pe.matmul(ps[:, 2 + b, :], self.gate_w(j, kc), xT[:, kc, :], start=kc == 0, stop=kc == KC - 1)
                for kc in range(KC):
                    last = pe.matmul(ps[:, 4 + b, :], self.up_w(j, kc), xT[:, kc, :], start=kc == 0, stop=kc == KC - 1)
                last.then_inc(self.gate_up_done.sem, 1)

            def pe_router(self, pe, t):
                n = self.E * self.per_token
                pe.wait_ge(self.logits_copied.sem, self.logits_copied.at(t, 1))
                for c in range(CT):
                    last = pe.matmul(ps[:, 7, c * n:(c + 1) * n], self.lg_sb[0:n, c * P:(c + 1) * P], ident[0:n, 0:n],
                                     start=True, stop=True)
                last.then_inc(self.tokens_done.sem, 1)

            def pe_coef(self, pe, t):
                n = 3 * (self.E + 1)
                pe.wait_ge(self.split_ready.sem, self.split_ready.at(t, 1))
                for c in range(CT):
                    last = pe.matmul(ps[0:n, 6, c * P:(c + 1) * P],
                                     self.part[:, c, :, :].rearrange("p a b -> p (a b)"), ident[:, :],
                                     start=True, stop=True)
                last.then_inc(self.coef_turned.sem, 1)

            def pe_spread(self, pe, t, j):
                n = 3 * (self.E + 1)
                if j == 0:
                    pe.wait_ge(self.coef_copied.sem, self.coef_copied.at(t, 1))
                pe.matmul(ps[:, j % 2, :], self.sel[:, j * P:(j + 1) * P], self.coefT[0:n, :],
                          start=True, stop=True).then_inc(self.coef_done.sem, 1)

            def pe_down(self, pe, t, j):
                pe.wait_ge(self.hidden_ready.sem, self.hidden_ready.at(t, j + 1))
                for mt in range(KC):
                    last = pe.matmul(ps[:, 6 + mt, :], self.down_w(j, mt), self.hidden[:, j % 2, :],
                                     start=j == 0, stop=j == self.NT - 1)
                last.then_inc(self.down_done.sem, 1)

            def pe_all(self, pe, t, xT, rw, loaded):
                self.pe_logits(pe, t, xT, rw)
                loaded(0)
                self.pe_gate_up(pe, t, 0, xT)
                loaded(1)
                self.pe_gate_up(pe, t, 1, xT)
                self.pe_router(pe, t)
                self.pe_coef(pe, t)
                self.pe_spread(pe, t, 0)
                self.pe_spread(pe, t, 1)
                self.pe_down(pe, t, 0)
                for j in range(2, self.NT):
                    loaded(j)
                    self.pe_gate_up(pe, t, j, xT)
                    self.pe_spread(pe, t, j)
                    self.pe_down(pe, t, j - 1)
                self.pe_down(pe, t, self.NT - 1)
                pe.wait_ge(self.delta_ready.sem, self.delta_ready.at(t, 1))
                for c in range(CT):
                    for mt in range(KC):
                        last = pe.transpose(ps[:, c // 2, (c % 2) * D + mt * P:(c % 2) * D + (mt + 1) * P],
                                            self.delta[:, mt, c * P:(c + 1) * P], ident[:, :])
                last.then_inc(self.delta_turned.sem, 1)

            def act_all(self, act, t):
                n = self.E * self.per_token
                act.wait_ge(self.logits_done.sem, self.logits_done.at(t, 1))
                act.copy(self.lg_sb[0:n, :], ps[0:n, 6, :]).then_inc(self.logits_copied.sem, 1)
                E = self.E
                lg = ps[:, 7, 0:CT * n].rearrange("p (c n) -> p c n", c=CT)
                if self.per_token == 2:
                    act.wait_ge(self.tokens_done.sem, self.tokens_done.at(t, 1))
                    act.activation(self.tok[0], lg[:, :, 0:E], ACT.Tanh, scale=0.5).then_inc(self.router_act.sem, 1)
                    act.wait_ge(self.router_step.sem, self.router_step.at(t, 5))
                    act.activation(self.tok[1], self.tok[0], ACT.Exp, scale=0.5).then_inc(self.router_act.sem, 1)
                else:
                    act.wait_ge(self.router_step.sem, self.router_step.at(t, 2))
                    act.activation(self.tok[1], self.tok[0], ACT.Exp).then_inc(self.router_act.sem, 1)

                def tanh(j):
                    act.wait_ge(self.gate_up_done.sem, self.gate_up_done.at(t, j + 1))
                    if j >= 2:
                        act.wait_ge(self.hidden_ready.sem, self.hidden_ready.at(t, j - 1))
                    act.activation(self.th[:, j % 2, :], ps[:, 2 + j % 2, :], ACT.Tanh, scale=0.5)\
                       .then_inc(self.tanh_done.sem, 1)

                tanh(0)
                tanh(1)
                act.wait_ge(self.coef_turned.sem, self.coef_turned.at(t, 1))
                act.copy(self.coefT[0:3 * (E + 1), :], ps[0:3 * (E + 1), 6, :]).then_inc(self.coef_copied.sem, 1)
                for j in range(2, self.NT):
                    tanh(j)
                act.wait_ge(self.down_done.sem, self.down_done.at(t, self.NT))
                for mt in range(KC):
                    act.activation(self.out_th[:, mt, :], ps[:, 6 + mt, :], ACT.Tanh, scale=0.5)\
                       .then_inc(self.out_tanh.sem, 1)

            def pool_all(self, pool, t):
                n = [0]
                zero = zeros.unsqueeze(2).broadcast_to([P, CT, self.E + 1])

                def step(ins):
                    n[0] += 1
                    ins.then_inc(self.split_step.sem, 1)
                    pool.wait_ge(self.split_step.sem, self.split_step.at(t, n[0]))

                pool.wait_ge(self.coef_ready.sem, self.coef_ready.at(t, 1))
                step(pool.tensor_tensor(self.narrow, self.coef, zero, ALU.add))
                step(pool.tensor_tensor(self.part[:, :, 0, :], self.narrow, zero, ALU.add))
                step(pool.tensor_tensor(self.rest, self.coef, self.part[:, :, 0, :], ALU.subtract))
                step(pool.tensor_tensor(self.narrow, self.rest, zero, ALU.add))
                step(pool.tensor_tensor(self.part[:, :, 1, :], self.narrow, zero, ALU.add))
                step(pool.tensor_tensor(self.coef, self.rest, self.part[:, :, 1, :], ALU.subtract))
                pool.tensor_tensor(self.part[:, :, 2, :], self.coef, zero, ALU.add).then_inc(self.split_ready.sem, 1)
                assert n[0] == self.split_step.per

            def dve_router(self, dve, t):
                E, n = self.E, [0]
                a, b, c = self.tok
                gt, eq = self.cmp
                mx, sm, inv = (self.small[:, i, :] for i in range(3))
                row = [P, CT, E]
                cube = [P, CT, E, E]

                def step(ins):
                    n[0] += 1
                    ins.then_inc(self.router_step.sem, 1)
                    dve.wait_ge(self.router_step.sem, self.router_step.at(t, n[0]))

                dve.wait_ge(self.tokens_done.sem, self.tokens_done.at(t, 1))
                lg = ps[:, 7, 0:CT * E * self.per_token].rearrange("p (c n) -> p c n", c=CT)
                if self.per_token == 2:
                    dve.wait_ge(self.router_act.sem, self.router_act.at(t, 1))
                    step(dve.scalar_tensor_tensor(b, a, 1.0, lg[:, :, 0:E], ALU.add, ALU.mult))
                    step(dve.tensor_tensor(c, b, lg[:, :, E:2 * E], ALU.mult))
                    step(dve.scalar_tensor_tensor(b, c, -1.0, c, ALU.mult, ALU.max))
                    lg = b
                step(dve.tensor_reduce(mx, lg, AX.X, ALU.max))
                step(dve.tensor_tensor(a, lg, mx.unsqueeze(2).broadcast_to(row), ALU.subtract))
                dve.wait_ge(self.router_act.sem, self.router_act.at(t, self.per_token))
                step(dve.tensor_reduce(sm, b, AX.X, ALU.add))
                step(dve.reciprocal(inv, sm))
                step(dve.tensor_tensor(a, b, inv.unsqueeze(2).broadcast_to(row), ALU.mult))
                rank_of = a
                if self.per_token == 2:
                    step(dve.tensor_tensor(c, a, expert_rows[:, 1, :].unsqueeze(1).broadcast_to(row), ALU.add))
                    rank_of = c
                    step(dve.tensor_tensor(b, a, expert_rows[:, 0, :].unsqueeze(1).broadcast_to(row), ALU.mult))
                    step(dve.tensor_scalar(a, b, 1.0, None, ALU.add))
                mine = rank_of.unsqueeze(3).broadcast_to(cube)
                other = rank_of.unsqueeze(2).broadcast_to(cube)
                low = self.lower[:, :].rearrange("p (e f) -> p e f", e=E).unsqueeze(1).broadcast_to(cube)
                step(dve.tensor_tensor(gt, other, mine, ALU.is_gt))
                step(dve.tensor_tensor(eq, other, mine, ALU.is_equal))
                step(dve.tensor_tensor(eq, eq, low, ALU.mult))
                step(dve.tensor_tensor(gt, gt, eq, ALU.add))
                step(dve.tensor_reduce(b, gt, AX.X, ALU.add))
                step(dve.tensor_scalar(c, b, self.top - 0.5, 0.5, ALU.is_lt, ALU.mult))
                dve.tensor_tensor(self.coef[:, :, 0:E], c, a, ALU.mult).then_inc(self.coef_ready.sem, 1)
                assert n[0] == self.router_step.per, n[0]

            def dve_all(self, dve, t, sT, x_now):
                dve.memset(self.coef[:, :, self.E:self.E + 1], 0.5)
                self.dve_router(dve, t)
                for j in range(self.NT):
                    b = j % 2
                    dve.wait_ge(self.tanh_done.sem, self.tanh_done.at(t, j + 1))
                    dve.scalar_tensor_tensor(self.half, self.th[:, b, :], 1.0, ps[:, 2 + b, :], ALU.add, ALU.mult)\
                       .then_inc(self.half_step.sem, 1)
                    dve.wait_ge(self.half_step.sem, self.half_step.at(t, 2 * j + 1))
                    dve.tensor_tensor(self.both, self.half, ps[:, 4 + b, :], ALU.mult).then_inc(self.half_step.sem, 1)
                    dve.wait_ge(self.half_step.sem, self.half_step.at(t, 2 * j + 2))
                    dve.wait_ge(self.coef_done.sem, self.coef_done.at(t, j + 1))
                    if j >= 2:
                        dve.wait_ge(self.down_done.sem, self.down_done.at(t, j - 1))
                    dve.tensor_tensor(self.hidden[:, b, :], self.both, ps[:, b, :], ALU.mult)\
                       .then_inc(self.hidden_ready.sem, 1)
                for mt in range(KC):
                    dve.wait_ge(self.out_tanh.sem, self.out_tanh.at(t, mt + 1))
                    dve.scalar_tensor_tensor(self.out_th[:, mt, :], self.out_th[:, mt, :], 1.0, ps[:, 6 + mt, :],
                                             ALU.add, ALU.mult).then_inc(self.out_step.sem, 1)
                dve.wait_ge(self.out_step.sem, self.out_step.at(t, KC))
                dve.tensor_tensor(self.delta, self.out_th, sT, ALU.mult).then_inc(self.delta_ready.sem, 1)
                dve.wait_ge(self.delta_turned.sem, self.delta_turned.at(t, 1))
                for c in range(CT // 2):
                    xs = x_now(2 * c, 2)
                    dve.scalar_tensor_tensor(xs, ps[:, c, :].rearrange("p (a d) -> p a d", a=2), 0.5, xs,
                                             ALU.mult, ALU.add).then_inc(self.x_ready.sem, 1)

        class Norm:
            def __init__(self, loop, tiles):
                self.T = tiles
                self.stats_done = count(loop + "_stats_done", tiles)
                self.mean_done = count(loop + "_mean_done", tiles)
                self.var_done = count(loop + "_var_done", 1)
                self.rstd_done = count(loop + "_rstd_done", 1)
                self.xn_ready = count(loop + "_xn_ready", tiles)
                self.xn_turned = count(loop + "_xn_turned", 1)
                self.xT_ready = count(loop + "_xT_ready", KC)
                self.stats = carve(loop, tiles, 6)
                self.mean = carve(loop, tiles, 2)
                self.var = carve(loop, tiles)
                self.rstd = carve(loop, tiles)
                self.xn = carve(loop, tiles, D)
                self.xT = carve(loop, KC, tiles * P)

            def dve_all(self, dve, t, x_now):
                T = self.T
                for c in range(T):
                    dve.bn_stats(self.stats[:, c, :], x_now(c, 1).rearrange("p a d -> p (a d)"))\
                       .then_inc(self.stats_done.sem, 1)
                dve.wait_ge(self.stats_done.sem, self.stats_done.at(t, T))
                dve.memset(self.rstd, 0.0)
                for c in range(T):
                    dve.bn_aggr(self.mean[:, c, :], self.stats[:, c, :]).then_inc(self.mean_done.sem, 1)
                dve.wait_ge(self.rstd_done.sem, self.rstd_done.at(t, 1))
                for c in range(T):
                    dve.tensor_scalar(self.xn[:, c, :], x_now(c, 1).rearrange("p a d -> p (a d)"),
                                      self.mean[:, c, 0:1], self.rstd[:, c:c + 1], ALU.subtract, ALU.mult)\
                       .then_inc(self.xn_ready.sem, 1)

            def pool_all(self, pool, t):
                T = self.T
                pool.wait_ge(self.mean_done.sem, self.mean_done.at(t, T))
                pool.tensor_tensor(self.var, self.mean[:, :, 1], eps_row[:, 0:T], ALU.add).then_inc(self.var_done.sem, 1)
                pool.wait_ge(self.var_done.sem, self.var_done.at(t, 1))
                pool.tensor_tensor(self.rstd, self.var, minus_half[:, 0:T], ALU.pow).then_inc(self.rstd_done.sem, 1)

            def pe_all(self, pe, t):
                pe.wait_ge(self.xn_ready.sem, self.xn_ready.at(t, self.T))
                for kc in range(KC):
                    for c in range(self.T):
                        last = pe.transpose(ps[:, kc, c * P:(c + 1) * P], self.xn[:, c, kc * P:(kc + 1) * P], ident[:, :])
                last.then_inc(self.xn_turned.sem, 1)

            def act_all(self, act, t):
                act.wait_ge(self.xn_turned.sem, self.xn_turned.at(t, 1))
                for kc in range(KC):
                    act.copy(self.xT[:, kc, :], ps[:, kc, 0:self.T * P]).then_inc(self.xT_ready.sem, 1)

        eps_row, eps_dk, zeros = minus_half[:, 16:32], minus_half[:, 32:32 + ST * 2], minus_half[:, 48:49]

        norm0 = Norm("layer0", CT)
        qT = carve("layer0", KC, CH)
        kTm = carve("layer0", HPQ, KC, CH)
        v0 = carve("layer0", CT, D)
        prob = carve("layer0", RING, 2, BLK)
        probT = carve("layer0", 2, 2, BLK)
        nmax = carve("layer0", RING, ST, 2)
        total = carve("layer0", 2, ST, NH0)
        inv0 = carve("layer0", ST, NH0)
        o0 = carve("layer0", ST, D)
        oT0 = carve("layer0", KC, CH)
        sT0 = carve("layer0", KC, CH)
        moe0 = MoE("layer0", E0, K0, NT0, sel0, lower0, 1)

        HEADS2 = 2 * SLOTS
        q_done, k_done, v_done = count("q_done", KC), count("k_done", KC), count("v_done", 2)
        qT_ready, v_ready = count("qT_ready", KC), count("v_ready", 2)
        keys_dve, keys_act = count("keys_dve", HPQ), count("keys_act", HPQ)
        scores_done = count("scores_done", HEADS2)
        masked, max_ready = count("masked", SLOTS), count("max_ready", 2 * SLOTS)
        exp_done = count("exp_done", HEADS2)
        prob_turned = count("prob_turned", HEADS2)
        probT_dve, probT_act = count("probT_dve", SLOTS), count("probT_act", SLOTS)
        pv_done = count("pv_done", HEADS2)
        inv_ready, o_ready = count("inv_ready", 2), count("o_ready", 2 * ST)
        o_turned, oT_ready = count("o_turned", 2), count("oT_ready", 2 * KC)
        out_done, sT_ready = count("out_done", KC), count("sT_ready", KC)

        def w0(which, kc, a, b):
            at = W0Q + (which * KC + kc) * D
            return weights[:, at + a:at + b]

        def pair_of(s):
            w = s % PAIRS
            return s // PAIRS, w // (PAIRS // 2), (w % (PAIRS // 2)) // 2, (2 * (w % 2), 2 * (w % 2) + 1)

        def head_of(n):
            bb, mt, j, rows = pair_of(n // 2)
            return mt * (NH0 // KC) + rows[n % 2] * HPQ + j

        def pe_layer0(pe, t):
            norm0.pe_all(pe, t)
            pe.wait_ge(norm0.xT_ready.sem, norm0.xT_ready.at(t, KC))
            xT = norm0.xT
            for mt in range(KC):
                for which, bank, done in ((0, 2 + mt, q_done), (1, 4 + mt, k_done)):
                    for kc in range(KC):
                        last = pe.matmul(ps[:, bank, :], w0(which, kc, mt * P, (mt + 1) * P), xT[:, kc, :],
                                         start=kc == 0, stop=kc == KC - 1)
                    last.then_inc(done.sem, 1)
            for c in range(CT):
                for kc in range(KC):
                    last = pe.matmul(ps[:, 6 + c // 2, (c % 2) * D:(c % 2 + 1) * D], xT[:, kc, c * P:(c + 1) * P],
                                     w0(2, kc, 0, D), start=kc == 0, stop=kc == KC - 1)
                if c % 2:
                    last.then_inc(v_done.sem, 1)

            def scores(s, hh):
                bb, mt, j, rows = pair_of(s)
                bank, r, q0 = 2 * (s % 2) + hh, rows[hh], bb * SEQ
                if s == 0 and hh == 0:
                    pe.wait_ge(qT_ready.sem, qT_ready.at(t, KC))
                    pe.wait_ge(keys_dve.sem, keys_dve.at(t, HPQ))
                if s == PAIRS // 2 and hh == 0:
                    pe.wait_ge(keys_act.sem, keys_act.at(t, HPQ))
                if s >= 2 and hh == 0:
                    pe.wait_ge(masked.sem, masked.at(t, s - 1))
                q = qT[32 * r:32 * r + 32, mt, :]
                k = kTm[32 * r:32 * r + 32, j, mt, :]
                pe.matmul(ps[:, bank, 0:P], q[:, q0:q0 + P], k[:, q0:q0 + P], start=True, stop=True)
                pe.matmul(ps[:, bank, P:BLK], q[:, q0 + P:q0 + SEQ], k[:, q0:q0 + SEQ], start=True, stop=True)\
                  .then_inc(scores_done.sem, 1)

            def turn(s, hh):
                copied = (probT_dve, probT_act)[hh]
                pe.wait_ge(exp_done.sem, exp_done.at(t, 2 * s + hh + 1))
                if s == 0 and hh == 0:
                    pe.wait_ge(keys_act.sem, keys_act.at(t, HPQ))
                if s:
                    pe.wait_ge(copied.sem, copied.at(t, s))
                for k in range(3):
                    last = pe.transpose(ps[:, 4 + hh, k * P:(k + 1) * P], prob[:, s % RING, hh, k * P:(k + 1) * P],
                                        ident[:, :])
                last.then_inc(prob_turned.sem, 1)

            def pv(s, hh):
                bb, h = s // PAIRS, head_of(2 * s + hh)
                copied = (probT_dve, probT_act)[hh]
                if s == 0 and hh == 0:
                    pe.wait_ge(v_ready.sem, v_ready.at(t, 2))
                pe.wait_ge(copied.sem, copied.at(t, s + 1))
                hs = slice(h * HD0, (h + 1) * HD0)
                pt = probT[:, s % 2, hh, :]
                pe.matmul(ps[:, 6 + bb, h * HD0:(h + 1) * HD0], pt[:, 0:P], v0[:, ST * bb, hs], start=True, stop=True)
                for k in range(2):
                    last = pe.matmul(ps[:, 6 + bb, D + h * HD0:D + (h + 1) * HD0], pt[:, (k + 1) * P:(k + 2) * P],
                                     v0[:, ST * bb + k, hs], start=k == 0, stop=k == 1)
                last.then_inc(pv_done.sem, 1)

            def turn_out(bb):
                pe.wait_ge(o_ready.sem, o_ready.at(t, ST * (bb + 1)))
                for mt in range(KC):
                    for c in range(ST):
                        last = pe.transpose(ps[:, 6 + bb, mt * SEQ + c * P:mt * SEQ + (c + 1) * P],
                                            o0[:, c, mt * P:(mt + 1) * P], ident[:, :])
                last.then_inc(o_turned.sem, 1)

            for s in range(SLOTS + LAG + 1):
                for hh in range(2):
                    if s < SLOTS:
                        scores(s, hh)
                for hh in range(2):
                    if LAG <= s < SLOTS + LAG:
                        turn(s - LAG, hh)
                for hh in range(2):
                    if s > LAG:
                        pv(s - LAG - 1, hh)
                if s == PAIRS + LAG + 3:
                    turn_out(0)
            turn_out(1)
            pe.wait_ge(oT_ready.sem, oT_ready.at(t, 2 * KC))
            for mt in range(KC):
                for kc in range(KC):
                    last = pe.matmul(ps[:, mt, :], w0(3, kc, mt * P, (mt + 1) * P), oT0[:, kc, :],
                                     start=kc == 0, stop=kc == KC - 1)
                last.then_inc(out_done.sem, 1)

        def act_layer0(act, t):
            norm0.act_all(act, t)

            def queries(mt):
                act.wait_ge(q_done.sem, q_done.at(t, mt + 1))
                act.activation(qT[:, mt, :], ps[:, 2 + mt, :], ACT.Identity, bias=bqs[:, mt:mt + 1],
                               scale=HD0 ** -0.5).then_inc(qT_ready.sem, 1)

            queries(0)
            queries(1)
            act.wait_ge(k_done.sem, k_done.at(t, 2))
            for j in range(HPQ):
                act.activation(kTm[:, j, 1, :], ps[:, 5, :], ACT.Identity, bias=bkm[:, j:j + 1],
                               scale=MASK[:, j:j + 1]).then_inc(keys_act.sem, 1)
            for c in range(2):
                act.wait_ge(v_done.sem, v_done.at(t, c + 1))
                act.copy(v0[:, 2 * c:2 * c + 2, :].rearrange("p a d -> p (a d)"), ps[:, 6 + c, :]).then_inc(v_ready.sem, 1)

            def out_turned(bb):
                act.wait_ge(o_turned.sem, o_turned.at(t, bb + 1))
                for mt in range(KC):
                    act.activation(oT0[:, mt, bb * SEQ:(bb + 1) * SEQ], ps[:, 6 + bb, mt * SEQ:(mt + 1) * SEQ], ACT.Identity,
                                   bias=BV[:, mt:mt + 1]).then_inc(oT_ready.sem, 1)

            def copy_probs(s):
                act.wait_ge(prob_turned.sem, prob_turned.at(t, 2 * s + 2))
                if s >= 2:
                    act.wait_ge(pv_done.sem, pv_done.at(t, 2 * (s - 2) + 2))
                act.copy(probT[:, s % 2, 1, :], ps[:, 5, 0:BLK]).then_inc(probT_act.sem, 1)

            for s in range(SLOTS + LAG):
                bb = s // PAIRS
                if s >= LAG:
                    copy_probs(s - LAG)
                if s < SLOTS:
                    act.wait_ge(max_ready.sem, max_ready.at(t, 2 * s + 2))
                    for hh in range(2):
                        h = head_of(2 * s + hh)
                        pr = prob[:, s % RING, hh, :]
                        act.activation(pr[:, 0:P], pr[:, 0:P], ACT.Exp, bias=nmax[:, s % RING, 0, hh:hh + 1],
                                       accum_out=total[:, bb, 0, h:h + 1])
                        act.activation(pr[:, P:BLK], pr[:, P:BLK], ACT.Exp, bias=nmax[:, s % RING, 1, hh:hh + 1],
                                       accum_out=total[:, bb, 1, h:h + 1]).then_inc(exp_done.sem, 1)
                if s == PAIRS + LAG + 3:
                    out_turned(0)
            out_turned(1)
            for mt in range(KC):
                act.wait_ge(out_done.sem, out_done.at(t, mt + 1))
                act.activation(sT0[:, mt, :], ps[:, mt, :], ACT.Identity, bias=BO[:, mt:mt + 1]).then_inc(sT_ready.sem, 1)

        def dve_layer0(dve, t, x_now):
            norm0.dve_all(dve, t, x_now)
            dve.wait_ge(k_done.sem, k_done.at(t, 1))
            for j in range(HPQ):
                dve.tensor_scalar(kTm[:, j, 0, :], ps[:, 4, :], BK[:, 0:1], MASK[:, j:j + 1], ALU.add, ALU.mult)\
                   .then_inc(keys_dve.sem, 1)

            def copy_probs(s):
                dve.wait_ge(prob_turned.sem, prob_turned.at(t, 2 * s + 1))
                if s >= 2:
                    dve.wait_ge(pv_done.sem, pv_done.at(t, 2 * (s - 2) + 1))
                dve.tensor_copy(probT[:, s % 2, 0, :], ps[:, 4, 0:BLK]).then_inc(probT_dve.sem, 1)

            def normalise(bb):
                dve.wait_ge(pv_done.sem, pv_done.at(t, NH0 * (bb + 1)))
                dve.reciprocal(inv0, total[:, bb, :, :]).then_inc(inv_ready.sem, 1)
                dve.wait_ge(inv_ready.sem, inv_ready.at(t, bb + 1))
                if bb:
                    dve.wait_ge(o_turned.sem, o_turned.at(t, 1))
                for c in range(ST):
                    dve.tensor_tensor(o0[:, c, :].rearrange("p (h e) -> p h e", e=HD0),
                                      ps[:, 6 + bb, c * D:(c + 1) * D].rearrange("p (h e) -> p h e", e=HD0),
                                      inv0[:, c, :].unsqueeze(2).broadcast_to([P, NH0, HD0]), ALU.mult)\
                       .then_inc(o_ready.sem, 1)

            for s in range(SLOTS + LAG):
                if s < SLOTS:
                    b = 2 * (s % 2)
                    pr = prob[:, s % RING, :, :]
                    dve.wait_ge(scores_done.sem, scores_done.at(t, 2 * s + 2))
                    if s >= RING:
                        dve.wait_ge(prob_turned.sem, prob_turned.at(t, 2 * (s - RING) + 2))
                    dve.tensor_tensor(pr, ps[:, b:b + 2, 0:BLK], causal[:, :].unsqueeze(1).broadcast_to([P, 2, BLK]),
                                      ALU.add).then_inc(masked.sem, 1)
                    dve.wait_ge(masked.sem, masked.at(t, s + 1))
                    dve.tensor_reduce(nmax[:, s % RING, 0, :], pr[:, :, 0:P], AX.X, ALU.max, negate=True)\
                       .then_inc(max_ready.sem, 1)
                    dve.tensor_reduce(nmax[:, s % RING, 1, :], pr[:, :, P:BLK], AX.X, ALU.max, negate=True)\
                       .then_inc(max_ready.sem, 1)
                if s >= LAG:
                    copy_probs(s - LAG)
                if s == PAIRS + LAG + 2:
                    normalise(0)
            normalise(1)

        norm1 = Norm("slots", ST)
        s1T = carve("slots", SEQ)
        s_sum = carve("slots", ST, P)
        s_clip = carve("slots", ST, P)
        es = carve("slots", 2, ST, P)
        enz = carve("slots", 2, ST, P)
        esT = carve("slots", 2, SEQ)
        raw = carve("slots", 2, 2, SEQ)
        rot_c = carve("slots", 2, 2, SEQ)
        rot_s = carve("slots", 2, 2, SEQ)
        qk = carve("slots", 4, 2, SEQ)
        v1 = carve("slots", 4, ST, DK)
        gate_th = carve("slots", 2, ST, DK)
        gate = carve("slots", 2, ST, DK)
        gate_n = carve("slots", 4, ST, DK)
        aT = carve("slots", 2, BLK)
        w2T = carve("slots", 2, BLK)
        okz = carve("slots", ST, 2, M)
        oks = carve("slots", ST, 2, M)
        okp = carve("slots", ST, 2, M)
        qe = carve("slots", ST, P)
        qeT = carve("slots", SEQ)
        okmax, oksum, rs, ssq, ms, rstd1, comb = (carve("slots", ST, 2) for _ in range(7))
        squares = carve("slots", 2, ST, DK)
        og = carve("slots", 2, ST, DK)
        ogT = carve("slots", 2, SEQ)

        s1_done, s_done, cum_done, es_turned = count("s1_done", 1), count("s_done", PAIR1), count("cum_done", PAIR1), count("es_turned", PAIR1)
        qk_done, vg_done, a_done, ok_done = count("qk_done", NH1), count("vg_done", NH1), count("a_done", NH1), count("ok_done", PAIR1)
        qe_turned, w2_done, o_done = count("qe_turned", PAIR1), count("w2_done", NH1), count("o_done", NH1)
        og_turned, out1_done = count("og_turned", PAIR1), count("out1_done", 1)
        s1_ready, es_ready, esT_ready = count("s1_ready", 1), count("es_ready", PAIR1), count("esT_ready", PAIR1)
        raw_ready, v1_ready, gate_tanh = count("raw_ready", NH1), count("v1_ready", NH1), count("gate_tanh", NH1)
        okp_ready, qeT_ready, ssq_ready = count("okp_ready", PAIR1), count("qeT_ready", PAIR1), count("ssq_ready", NH1)
        ogT_ready, sT1_ready = count("ogT_ready", PAIR1), count("sT1_ready", 1)
        s_biased, s_clipped, enz_ready = count("s_biased", PAIR1), count("s_clipped", PAIR1), count("enz_ready", PAIR1)
        aT_ready, w2T_ready, rot_s_ready = count("aT_ready", NH1), count("w2T_ready", NH1), count("rot_s_ready", NH1)
        ok_step, oks_ready, sum_step, rs_ready = count("ok_step", 2 * PAIR1), count("oks_ready", PAIR1), count("sum_step", PAIR1), count("rs_ready", PAIR1)
        gate_ready, og_ready = count("gate_ready", NH1), count("og_ready", PAIR1)
        rot_c_ready, qk_ready, qe_ready = count("rot_c_ready", NH1), count("qk_ready", NH1), count("qe_ready", PAIR1)
        gate_n_ready, rms_step, comb_ready = count("gate_n_ready", NH1), count("rms_step", 2 * PAIR1), count("comb_ready", PAIR1)

        def w1(h, at, n):
            at += w1_head(h)
            return weights[:, at:at + n]

        def pe_slots(pe, t):
            norm1.pe_all(pe, t)
            pe.wait_ge(norm1.xT_ready.sem, norm1.xT_ready.at(t, KC))
            xT = norm1.xT
            for kc in range(KC):
                last = pe.matmul(ps[0:R1, 0, 0:SEQ], s1w[:, kc, :], xT[:, kc, :], start=kc == 0, stop=kc == KC - 1)
            last.then_inc(s1_done.sem, 1)

            def slot_scores(pp):
                if pp == 0:
                    pe.wait_ge(s1_ready.sem, s1_ready.at(t, 1))
                else:
                    pe.wait_ge(esT_ready.sem, esT_ready.at(t, pp))
                for c in range(ST):
                    last = pe.matmul(ps[:, 0, c * P:(c + 1) * P], s1T[0:R1, c * P:(c + 1) * P],
                                     s2w[:, pp * P:(pp + 1) * P], start=True, stop=True)
                last.then_inc(s_done.sem, 1)

            def running_sum(pp):
                pe.wait_ge(es_ready.sem, es_ready.at(t, pp + 1))
                e = es[:, pp % 2, :, :]
                pe.matmul(ps[:, 0, SEQ:SEQ + P], tri[:, :], e[:, 0, :], start=True, stop=True)
                pe.matmul(ps[:, 0, SEQ + P:2 * SEQ], ones[:, :], e[:, 0, :], start=True, stop=False)
                pe.matmul(ps[:, 0, SEQ + P:2 * SEQ], tri[:, :], e[:, 1, :], start=False, stop=True)\
                  .then_inc(cum_done.sem, 1)

            def turn_es(pp):
                pe.wait_ge(enz_ready.sem, enz_ready.at(t, pp + 1))
                for c in range(ST):
                    last = pe.transpose(ps[:, 0, c * P:(c + 1) * P], es[:, pp % 2, c, :], ident[:, :])
                last.then_inc(es_turned.sem, 1)

            def queries_keys(h):
                if h % 2 == 0:
                    pe.wait_ge(w1_loaded[h // 2], 16)
                if h:
                    pe.wait_ge(raw_ready.sem, raw_ready.at(t, h))
                for which in range(2):
                    for kc in range(KC):
                        last = pe.matmul(ps[:, 2, which * SEQ:(which + 1) * SEQ], w1(h, (which * KC + kc) * P, P),
                                         xT[:, kc, :], start=kc == 0, stop=kc == KC - 1)
                last.then_inc(qk_done.sem, 1)

            def values_gates(h):
                if h:
                    pe.wait_ge(gate_ready.sem, gate_ready.at(t, h))
                for c in range(ST):
                    for kc in range(KC):
                        last = pe.matmul(ps[:, 3, c * 2 * DK:(c + 1) * 2 * DK], xT[:, kc, c * P:(c + 1) * P],
                                         w1(h, 2 * KC * P + kc * 2 * DK, 2 * DK), start=kc == 0, stop=kc == KC - 1)
                last.then_inc(vg_done.sem, 1)

            def causal_blocks(bank, key, query, done):
                pe.matmul(ps[:, bank, 0:SEQ], key[:, 0:P], query[:, 0:SEQ], start=True, stop=True)
                pe.matmul(ps[:, bank, SEQ:BLK], key[:, P:SEQ], query[:, P:SEQ], start=True, stop=True)\
                  .then_inc(done.sem, 1)

            def over_keys(outs, left, rhs):
                pe.matmul(outs[0], left[:, 0:P], rhs[0], start=True, stop=True)
                pe.matmul(outs[1], left[:, P:SEQ], rhs[0], start=True, stop=False)
                return pe.matmul(outs[1], left[:, SEQ:BLK], rhs[1], start=False, stop=True)

            def scores1(h):
                pe.wait_ge(qk_ready.sem, qk_ready.at(t, h + 1))
                if h >= 2:
                    pe.wait_ge(w2T_ready.sem, w2T_ready.at(t, h - 1))
                causal_blocks(4 + h % 2, qk[:, h % 4, 1, :], qk[:, h % 4, 0, :], a_done)

            def slots_read(pp):
                for hh in range(2):
                    h = 2 * pp + hh
                    pe.wait_ge(aT_ready.sem, aT_ready.at(t, h + 1))
                    last = over_keys([ps[:, 4 + hh, BLK + c * M:BLK + (c + 1) * M] for c in range(ST)], aT[:, hh, :],
                                     [es[:, pp % 2, c, hh * M:(hh + 1) * M] for c in range(ST)])
                last.then_inc(ok_done.sem, 1)

            def turn_qe(pp):
                pe.wait_ge(qe_ready.sem, qe_ready.at(t, pp + 1))
                for c in range(ST):
                    last = pe.transpose(ps[:, 1, c * P:(c + 1) * P], qe[:, c, :], ident[:, :])
                last.then_inc(qe_turned.sem, 1)

            def slots_write(h):
                a = slice(M * (h % 2), M * (h % 2) + M)
                causal_blocks(4 + h % 2, esT[a, (h // 2) % 2, :], qeT[a, :], w2_done)

            def mix_values(h):
                pe.wait_ge(w2T_ready.sem, w2T_ready.at(t, h + 1))
                at = (h % 2) * SEQ
                if h % 2 == 0 and h:
                    pe.wait_ge(og_ready.sem, og_ready.at(t, h // 2))
                over_keys([ps[:, 6, at + c * P:at + (c + 1) * P] for c in range(ST)], w2T[:, h % 2, :],
                          [v1[:, h % 4, c, :] for c in range(ST)]).then_inc(o_done.sem, 1)

            def turn_og(pp):
                pe.wait_ge(og_ready.sem, og_ready.at(t, pp + 1))
                for hh in range(2):
                    for c in range(ST):
                        last = pe.transpose(ps[:, 1, hh * SEQ + c * P:hh * SEQ + (c + 1) * P], og[:, hh, c, :], ident[:, :])
                last.then_inc(og_turned.sem, 1)

            def project(pp):
                pe.wait_ge(ogT_ready.sem, ogT_ready.at(t, pp + 1))
                for hh in range(2):
                    h = 2 * pp + hh
                    for mt in range(KC):
                        wo = weights[:, W1O + h * D + mt * P:W1O + h * D + (mt + 1) * P]
                        last = pe.matmul(ps[:, 7, mt * SEQ:(mt + 1) * SEQ], wo, ogT[:, hh, :],
                                         start=h == 0 and mt == 0, stop=h == NH1 - 1, skip_group_check=True)
                if pp == PAIR1 - 1:
                    last.then_inc(out1_done.sem, 1)

            for pp in range(-1, PAIR1 + 1):
                now, ahead, behind = 0 <= pp < PAIR1, pp + 1 < PAIR1, pp >= 1
                if now:
                    scores1(2 * pp)
                    scores1(2 * pp + 1)
                if ahead:
                    slot_scores(pp + 1)
                    queries_keys(2 * pp + 2)
                if now:
                    slots_read(pp)
                if ahead:
                    queries_keys(2 * pp + 3)
                    values_gates(2 * pp + 2)
                if behind:
                    turn_og(pp - 1)
                if ahead:
                    running_sum(pp + 1)
                if behind:
                    project(pp - 1)
                if now:
                    turn_qe(pp)
                if ahead:
                    values_gates(2 * pp + 3)
                    turn_es(pp + 1)
                if now:
                    pe.wait_ge(qeT_ready.sem, qeT_ready.at(t, pp + 1))
                    if pp == 0:
                        pe.wait_ge(esT_ready.sem, esT_ready.at(t, 1))
                    slots_write(2 * pp)
                    slots_write(2 * pp + 1)
                    mix_values(2 * pp)
                    mix_values(2 * pp + 1)

        def act_slots(act, t):
            norm1.act_all(act, t)
            act.wait_ge(s1_done.sem, s1_done.at(t, 1))
            act.copy(s1T[0:R1, :], ps[0:R1, 0, 0:SEQ]).then_inc(s1_ready.sem, 1)

            def copy_qk(h):
                act.wait_ge(qk_done.sem, qk_done.at(t, h + 1))
                act.copy(raw[:, h % 2, :, :].rearrange("p a b -> p (a b)"), ps[:, 2, :]).then_inc(raw_ready.sem, 1)

            def gates(h):
                act.wait_ge(vg_done.sem, vg_done.at(t, h + 1))
                vg = ps[:, 3, :].rearrange("p (c w d) -> p c w d", c=ST, w=2)
                act.copy(v1[:, h % 4, :, :], vg[:, :, 0, :]).then_inc(v1_ready.sem, 1)
                act.activation(gate_th[:, h % 2, :, :], vg[:, :, 1, :], ACT.Tanh, scale=0.5).then_inc(gate_tanh.sem, 1)

            for pp in range(-1, PAIR1 + 1):
                now, ahead, behind = 0 <= pp < PAIR1, pp + 1 < PAIR1, pp >= 1
                if behind:
                    act.wait_ge(rs_ready.sem, rs_ready.at(t, pp))
                    act.wait_ge(o_done.sem, o_done.at(t, 2 * pp))
                    for hh in range(2):
                        for c in range(ST):
                            at = hh * SEQ + c * P
                            last = act.activation(squares[:, hh, c, :], ps[:, 6, at:at + P], ACT.Square, scale=rs[:, c, hh:hh + 1],
                                                  accum_out=ssq[:, c, hh:hh + 1])
                        last.then_inc(ssq_ready.sem, 1)
                if ahead:
                    act.wait_ge(s_clipped.sem, s_clipped.at(t, pp + 2))
                    act.activation(es[:, (pp + 1) % 2, :, :], s_clip, ACT.Exp).then_inc(es_ready.sem, 1)
                    copy_qk(2 * pp + 2)
                    copy_qk(2 * pp + 3)
                if now:
                    act.wait_ge(oks_ready.sem, oks_ready.at(t, pp + 1))
                    act.activation(okp, oks, ACT.Exp).then_inc(okp_ready.sem, 1)
                if ahead:
                    gates(2 * pp + 2)
                if behind:
                    act.wait_ge(og_turned.sem, og_turned.at(t, pp))
                    act.copy(ogT.rearrange("p a b -> p (a b)"), ps[:, 1, :]).then_inc(ogT_ready.sem, 1)
                if now:
                    act.wait_ge(qe_turned.sem, qe_turned.at(t, pp + 1))
                    act.copy(qeT, ps[:, 1, 0:SEQ]).then_inc(qeT_ready.sem, 1)
                if ahead:
                    gates(2 * pp + 3)
                    act.wait_ge(es_turned.sem, es_turned.at(t, pp + 2))
                    act.copy(esT[:, (pp + 1) % 2, :], ps[:, 0, 0:SEQ]).then_inc(esT_ready.sem, 1)
            act.wait_ge(out1_done.sem, out1_done.at(t, 1))
            act.copy(sT1[:, :, bass.ds(t * SEQ, SEQ)], ps[:, 7, :].rearrange("p (k n) -> p k n", k=KC))\
               .then_inc(sT1_ready.sem, 1)

        def dve_slots(dve, t, x_now):
            norm1.dve_all(dve, t, x_now)

            def rotate(h):
                dve.wait_ge(raw_ready.sem, raw_ready.at(t, h + 1))
                H = DK // 2
                for dst, src in ((0, H), (H, 0)):
                    last = dve.tensor_tensor(rot_s[dst:dst + H, h % 2, :, :], raw[src:src + H, h % 2, :, :],
                                             rope[src:src + H, 1, :].unsqueeze(1).broadcast_to([H, 2, SEQ]), ALU.mult)
                last.then_inc(rot_s_ready.sem, 1)

            def gates(h):
                dve.wait_ge(gate_tanh.sem, gate_tanh.at(t, h + 1))
                if h >= 2:
                    dve.wait_ge(gate_n_ready.sem, gate_n_ready.at(t, h - 1))
                g = ps[:, 3, :].rearrange("p (c w d) -> p c w d", c=ST, w=2)[:, :, 1, :]
                dve.scalar_tensor_tensor(gate[:, h % 2, :, :], gate_th[:, h % 2, :, :], 1.0, g, ALU.add, ALU.mult)\
                   .then_inc(gate_ready.sem, 1)

            def keep(h, src_done, dst, mask, ready):
                dve.wait_ge(src_done.sem, src_done.at(t, h + 1))
                dve.tensor_tensor(dst[:, h % 2, :], ps[:, 4 + h % 2, 0:BLK], mask[:, :], ALU.mult).then_inc(ready.sem, 1)

            def gated(pp):
                dve.wait_ge(comb_ready.sem, comb_ready.at(t, pp + 1))
                dve.wait_ge(gate_n_ready.sem, gate_n_ready.at(t, 2 * pp + 2))
                for hh in range(2):
                    for c in range(ST):
                        at = hh * SEQ + c * P
                        last = dve.scalar_tensor_tensor(og[:, hh, c, :], ps[:, 6, at:at + P], comb[:, c, hh:hh + 1],
                                                        gate_n[:, (2 * pp + hh) % 4, c, :], ALU.mult, ALU.mult)
                last.then_inc(og_ready.sem, 1)

            for pp in range(-1, PAIR1 + 1):
                now, ahead, behind = 0 <= pp < PAIR1, pp + 1 < PAIR1, pp >= 1
                if now:
                    keep(2 * pp, a_done, aT, keep_a, aT_ready)
                    keep(2 * pp + 1, a_done, aT, keep_a, aT_ready)
                if ahead:
                    n = pp + 1
                    dve.wait_ge(s_done.sem, s_done.at(t, n + 1))
                    dve.tensor_tensor(s_sum, ps[:, 0, 0:SEQ].rearrange("p (c n) -> p c n", c=ST),
                                      s2b[:, n * P:(n + 1) * P].unsqueeze(1).broadcast_to([P, ST, P]), ALU.add)\
                       .then_inc(s_biased.sem, 1)
                    dve.wait_ge(s_biased.sem, s_biased.at(t, n + 1))
                    dve.tensor_scalar(s_clip, s_sum, -CLAMP, CLAMP, ALU.max, ALU.min).then_inc(s_clipped.sem, 1)
                if behind:
                    gated(pp - 1)
                if now:
                    dve.wait_ge(ok_done.sem, ok_done.at(t, pp + 1))
                    for hh in range(2):
                        last = dve.tensor_tensor(okz[:, :, hh, :], ps[:, 4 + hh, BLK:512].rearrange("p (c m) -> p c m", c=ST),
                                                 enz[:, pp % 2, :, hh * M:(hh + 1) * M], ALU.mult)
                    last.then_inc(ok_step.sem, 1)
                    dve.wait_ge(ok_step.sem, ok_step.at(t, 2 * pp + 1))
                    dve.tensor_reduce(okmax, okz, AX.X, ALU.max).then_inc(ok_step.sem, 1)
                    dve.wait_ge(ok_step.sem, ok_step.at(t, 2 * pp + 2))
                    flat = "p c h m -> p (c h) m"
                    dve.tensor_tensor(oks.rearrange(flat), okz.rearrange(flat),
                                      okmax.rearrange("p c h -> p (c h)").unsqueeze(2).broadcast_to([P, ST * 2, M]), ALU.subtract)\
                       .then_inc(oks_ready.sem, 1)
                if ahead:
                    rotate(2 * n)
                    rotate(2 * n + 1)
                    gates(2 * n)
                    dve.wait_ge(cum_done.sem, cum_done.at(t, n + 1))
                    dve.reciprocal(enz[:, n % 2, :, :].rearrange("p c n -> p (c n)"), ps[:, 0, SEQ:2 * SEQ])\
                       .then_inc(enz_ready.sem, 1)
                if now:
                    dve.wait_ge(okp_ready.sem, okp_ready.at(t, pp + 1))
                    dve.tensor_reduce(oksum, okp, AX.X, ALU.add).then_inc(sum_step.sem, 1)
                    dve.wait_ge(sum_step.sem, sum_step.at(t, pp + 1))
                    dve.reciprocal(rs, oksum).then_inc(rs_ready.sem, 1)
                    keep(2 * pp, w2_done, w2T, keep_w, w2T_ready)
                    keep(2 * pp + 1, w2_done, w2T, keep_w, w2T_ready)
                if ahead:
                    gates(2 * n + 1)

        def pool_slots(pool, t):
            norm1.pool_all(pool, t)

            def rotate(h):
                pool.wait_ge(raw_ready.sem, raw_ready.at(t, h + 1))
                pool.tensor_tensor(rot_c[:, h % 2, :, :], raw[:, h % 2, :, :],
                                   rope[:, 0, :].unsqueeze(1).broadcast_to([P, 2, SEQ]), ALU.mult).then_inc(rot_c_ready.sem, 1)
                pool.wait_ge(rot_c_ready.sem, rot_c_ready.at(t, h + 1))
                pool.wait_ge(rot_s_ready.sem, rot_s_ready.at(t, h + 1))
                pool.tensor_tensor(qk[:, h % 4, :, :], rot_c[:, h % 2, :, :], rot_s[:, h % 2, :, :], ALU.add)\
                    .then_inc(qk_ready.sem, 1)

            def gates(h):
                pool.wait_ge(gate_ready.sem, gate_ready.at(t, h + 1))
                pool.tensor_tensor(gate_n[:, h % 4, :, :], gate[:, h % 2, :, :],
                                   g_half[:, :].unsqueeze(1).broadcast_to([P, ST, DK]), ALU.mult).then_inc(gate_n_ready.sem, 1)

            def rms(pp):
                pool.wait_ge(ssq_ready.sem, ssq_ready.at(t, 2 * pp + 2))
                four = "p c h -> p (c h)"
                pool.tensor_tensor(ms.rearrange(four), ssq.rearrange(four), eps_dk, ALU.add).then_inc(rms_step.sem, 1)
                pool.wait_ge(rms_step.sem, rms_step.at(t, 2 * pp + 1))
                pool.tensor_tensor(rstd1.rearrange(four), ms.rearrange(four), minus_half[:, 0:ST * 2], ALU.pow)\
                    .then_inc(rms_step.sem, 1)
                pool.wait_ge(rms_step.sem, rms_step.at(t, 2 * pp + 2))
                pool.tensor_tensor(comb.rearrange(four), rstd1.rearrange(four), rs.rearrange(four), ALU.mult)\
                    .then_inc(comb_ready.sem, 1)

            for pp in range(-1, PAIR1 + 1):
                now, ahead, behind = 0 <= pp < PAIR1, pp + 1 < PAIR1, pp >= 1
                if behind:
                    rms(pp - 1)
                if ahead:
                    rotate(2 * pp + 2)
                if now:
                    pool.wait_ge(okp_ready.sem, okp_ready.at(t, pp + 1))
                    pool.tensor_tensor(qe, okp.rearrange("p c h m -> p c (h m)"), enz[:, pp % 2, :, :], ALU.mult)\
                        .then_inc(qe_ready.sem, 1)
                if ahead:
                    rotate(2 * pp + 3)
                    gates(2 * pp + 2)
                    gates(2 * pp + 3)

        norm2 = Norm("experts", CT)
        moe1 = MoE("experts", E1, K1, NT1, sel1, lower1, 2)

        block = ctx.enter_context(nc.Block())
        const_loads = [(ident, "ident"), (causal, "causal"), (cols, "cols"), (router0, "router0"),
                       (lower0, "lower0"), (lower1, "lower1"), (router1, "router1"), (rope, "rope"), (tri, "tri"),
                       (keep_a, "keep_a"), (keep_w, "keep_w"), (s1w, "s1w"), (s2w, "s2w")]
        row_loads = [(s2b[:, :], "s2b"), (g_norm[:, :], "g_norm"), (expert_rows[:, 0, :], "extra_scale"),
                     (expert_rows[:, 1, :], "extra_bias")]
        NCONST = 16 * (len(const_loads) + len(row_loads))
        MOE_LOT = 5
        MOE_LOTS = -(-NT1 // MOE_LOT)
        w1_loaded = [sem(f"w1_loaded{n}") for n in range(PAIR1)]
        wo1_loaded = sem("wo1_loaded")
        f1_loaded = [sem(f"f1_loaded{n}") for n in range(MOE_LOTS)]
        stored = sem("stored")

        @block.sync
        def _(sp):
            def load_pair(pp):
                at = w1_head(2 * pp + 1)
                sp.dma_start(weights[:, at:at + 2 * HW], A["w1"][:, at:at + 2 * HW]).then_inc(w1_loaded[pp], 16)

            sp.dma_start(x_res[:, :, :], A["x"].rearrange("b (c p) d -> p (b c) d", p=P)).then_inc(x_loaded, 16)
            for dst, name in const_loads:
                sp.dma_start(dst[tuple(slice(None) for _ in dst.shape)], A[name]).then_inc(consts_loaded, 16)
            for dst, name in row_loads:
                sp.dma_start(dst, A[name].partition_broadcast(P)).then_inc(consts_loaded, 16)
            sp.dma_start(weights[:, W0Q:W0F], A["w0"]).then_inc(w0_loaded, 16)
            sp.dma_start(weights[:, W0F:W0F + NT0 * WT].rearrange("p (j w) -> p j w", w=WT),
                         A["f0"].rearrange("j p w -> p j w")).then_inc(f0_loaded, 16)
            sp.dma_start(weights[:, W1O:WCOLS], A["wo1"]).then_inc(wo1_loaded, 16)
            load_pair(0)
            sp.wait_ge(moe0.x_ready.sem, 2 * TURNS)
            for pp in range(1, PAIR1):
                load_pair(pp)
            sp.wait_ge(out1_done.sem, BATCH)
            for n in range(MOE_LOTS):
                j0, j1 = n * MOE_LOT, min((n + 1) * MOE_LOT, NT1)
                sp.dma_start(weights[:, j0 * WT:j1 * WT].rearrange("p (j w) -> p j w", w=WT),
                             A["f1"][j0:j1].rearrange("j p w -> p j w")).then_inc(f1_loaded[n], 16)
            with sp.Fori(0, TURNS) as t:
                sp.wait_ge(moe1.x_ready.sem, moe1.x_ready.at(t, 2))
                sp.dma_start(out.rearrange("b (c p) d -> p (b c) d", p=P)[:, bass.ds(t * CT, CT), :],
                             x_res[:, bass.ds(t * CT, CT), :]).then_inc(stored, 16)
            sp.wait_ge(stored, 16 * TURNS)

        @block.gpsimd
        def _(pool):
            pool.dma_start(sel0[:, :], A["sel0"]).then_inc(casts_done, 16)
            pool.dma_start(sel1[:, :], A["sel1"]).then_inc(casts_done, 16)
            for n, value in enumerate((-0.5, EPS, DK * EPS, 0.0)):
                pool.memset(minus_half[:, 16 * n:16 * n + 16], value).then_inc(pow_rows, 1)
            pool.memset(ones[:, :], 1.0).then_inc(pow_rows, 1)
            pool.wait_ge(pow_rows, 5)
            pool.wait_ge(bias_done, 3)
            with pool.Fori(0, TURNS) as t:
                norm0.pool_all(pool, t)
                moe0.pool_all(pool, t)
            with pool.Fori(0, BATCH) as t:
                pool_slots(pool, t)
            with pool.Fori(0, TURNS) as t:
                norm2.pool_all(pool, t)
                moe1.pool_all(pool, t)

        @block.vector
        def _(dve):
            dve.wait_ge(consts_loaded, NCONST)
            dve.tensor_scalar(bqs[:, :], BQ, HD0 ** -0.5, None, ALU.mult).then_inc(bias_done, 1)
            dve.tensor_scalar(bkm[:, :], MASK, BK[:, 1:2], None, ALU.mult).then_inc(bias_done, 1)
            dve.tensor_scalar(g_half[:, :], g_norm[:, :], 0.5 * DK ** 0.5, None, ALU.mult).then_inc(bias_done, 1)
            dve.wait_ge(x_loaded, 16)
            with dve.Fori(0, TURNS) as t:
                def x_now(c, n):
                    return x_res[:, bass.ds(t * CT + c, n), :]
                dve_layer0(dve, t, x_now)
                dve.wait_ge(sT_ready.sem, sT_ready.at(t, KC))
                moe0.dve_all(dve, t, sT0, x_now)
            dve.wait_ge(moe0.x_ready.sem, 2 * TURNS)
            with dve.Fori(0, BATCH) as t:
                dve_slots(dve, t, lambda c, n: x_res[:, bass.ds(t * ST + c, n), :])
            dve.wait_ge(sT1_ready.sem, BATCH)
            with dve.Fori(0, TURNS) as t:
                def x_now(c, n):
                    return x_res[:, bass.ds(t * CT + c, n), :]
                norm2.dve_all(dve, t, x_now)
                moe1.dve_all(dve, t, sT1[:, :, bass.ds(t * CH, CH)], x_now)

        @block.scalar
        def _(act):
            act.wait_ge(bias_done, 3)
            with act.Fori(0, TURNS) as t:
                act_layer0(act, t)
                moe0.act_all(act, t)
            with act.Fori(0, BATCH) as t:
                act_slots(act, t)
            with act.Fori(0, TURNS) as t:
                norm2.act_all(act, t)
                moe1.act_all(act, t)

        @block.tensor
        def _(pe):
            pe.wait_ge(bias_done, 3)
            pe.wait_ge(pow_rows, 5)
            pe.wait_ge(w0_loaded, 16)
            pe.wait_ge(f0_loaded, 16)
            pe.wait_ge(casts_done, 32)
            with pe.Fori(0, TURNS) as t:
                pe_layer0(pe, t)
                pe.wait_ge(sT_ready.sem, sT_ready.at(t, KC))
                moe0.pe_all(pe, t, norm0.xT, router0, lambda j: None)
            pe.wait_ge(wo1_loaded, 16)
            with pe.Fori(0, BATCH) as t:
                pe_slots(pe, t)
            with pe.Fori(0, TURNS) as t:
                norm2.pe_all(pe, t)
                pe.wait_ge(norm2.xT_ready.sem, norm2.xT_ready.at(t, KC))

                def loaded(j):
                    if j % MOE_LOT == 0:
                        pe.wait_ge(f1_loaded[j // MOE_LOT], 16)

                moe1.pe_all(pe, t, norm2.xT, router1, loaded)


def _constants():
    p = np.arange(P)
    tri_jt = (p[:, None] <= p[None, :]).astype(np.float32)
    one = np.ones((P, P), np.float32)
    bias = np.where(p[None, :] > p[:, None], np.float32(NEG), np.float32(0)).astype(np.float32)
    keep = np.concatenate([tri_jt, one, tri_jt], 1)
    inv_freq = 1.0 / np.float32(10000.0) ** (np.arange(0, DK, 2, dtype=np.float32) / np.float32(DK))
    ang = (np.arange(SEQ, dtype=np.float32)[:, None] * inv_freq[None, :].astype(np.float32)).astype(np.float32)
    cos, sin = np.cos(ang).T.astype(np.float32), np.sin(ang).T.astype(np.float32)

    def sel(experts, f, tiles):
        row = np.minimum(np.arange(tiles * P) // f, experts)
        hot = (row[None, :] == np.arange(experts + 1)[:, None]).astype(np.float32)
        return np.concatenate([hot] * 3, 0)

    def lower(e):
        n = np.arange(e)
        return np.ascontiguousarray(np.broadcast_to((n[None, :] < n[:, None]).astype(np.float32).reshape(1, e * e), (P, e * e)))

    return {
        "ident": np.eye(P, dtype=np.float32),
        "causal": np.concatenate([bias, np.zeros((P, P), np.float32), bias], 1),
        "sel0": sel(E0, F0, NT0), "sel1": sel(E1, F1, NT1),
        "lower0": lower(E0), "lower1": lower(E1),
        "rope": np.stack([np.concatenate([cos, cos], 0), np.concatenate([sin, -sin], 0)], 1),
        "tri": tri_jt, "keep_a": keep * np.float32(SCALE1), "keep_w": keep,
    }


def _chunks(w_t):
    return w_t.reshape(KC, P, -1).transpose(1, 0, 2)


def _moe_tiles(wg, wu, wd, sg, su, sd, tiles):
    e, f, d = wg.shape
    pad = tiles * P - e * f - sg.shape[0]
    z = np.zeros((pad, d), wg.dtype)
    gate = np.concatenate([wg.reshape(e * f, d), sg, z], 0).reshape(tiles, P, KC, P).transpose(0, 3, 2, 1)
    up = np.concatenate([wu.reshape(e * f, d), su, z], 0).reshape(tiles, P, KC, P).transpose(0, 3, 2, 1)
    down = np.concatenate([wd.transpose(0, 2, 1).reshape(e * f, d), sd.T, z], 0).reshape(tiles, P, d)
    return np.concatenate([gate.reshape(tiles, P, KC * P), up.reshape(tiles, P, KC * P), down], 2)


def layout(i):
    c = _constants()
    p = np.arange(P)
    mask = ((p[:, None] // HD0) % HPQ == np.arange(HPQ)[None, :]).astype(np.float32)
    col = [i["L0_attn_" + n].reshape(KC, P).T for n in ("bq", "bk", "bv", "bo")]
    c["cols"] = np.concatenate([mask, *col, np.zeros((P, 4), np.float32)], 1)
    c["x"] = i["L0_attn_hidden_states"]
    c["w0"] = np.stack([_chunks(i["L0_attn_" + n].T) for n in ("wq", "wk", "wv", "wo")], 1).reshape(P, -1)
    c["f0"] = _moe_tiles(i["L0_ffn_Wg"], i["L0_ffn_Wu"], i["L0_ffn_Wd"], i["L0_ffn_Wsg"], i["L0_ffn_Wsu"],
                         i["L0_ffn_Wsd"], NT0)
    c["router0"] = _chunks(i["L0_ffn_Wr"].T)
    c["f1"] = _moe_tiles(i["L1_ffn_Wg"], i["L1_ffn_Wu"], i["L1_ffn_Wd"], i["L1_ffn_Sg"], i["L1_ffn_Su"],
                         i["L1_ffn_Sd"], NT1)
    c["router1"] = _chunks(np.concatenate([i["L1_ffn_rg_w"], i["L1_ffn_ru_w"]], 0).T)
    c["s1w"] = _chunks(i["L1_attn_Ws1"].T)
    c["s2w"] = i["L1_attn_Ws2"].T
    c["s2b"], c["g_norm"] = i["L1_attn_bs2"], i["L1_attn_g_norm_weight"]
    c["extra_scale"], c["extra_bias"] = i["L1_ffn_extra_scale"], i["L1_ffn_extra_bias"]
    wq, wk, wv, wg = (i["L1_attn_" + n].T.reshape(KC, P, NH1, DK).transpose(2, 1, 0, 3) for n in ("Wq", "Wk", "Wv", "Wg"))
    vg = np.concatenate([wv, wg], 3)
    heads = np.concatenate([a.reshape(NH1, P, -1) for a in (wq, wk, vg)], 2)
    c["w1"] = heads[::-1].transpose(1, 0, 2).reshape(P, -1)
    c["wo1"] = i["L1_attn_Wo"].T.reshape(NH1, DK, D).transpose(1, 0, 2).reshape(P, -1)
    return {k: np.ascontiguousarray(v) for k, v in c.items()}


def kernel(**inputs):
    import concourse.bacc as bacc
    from concourse.bass_utils import run_bass_kernel_spmd

    arrays = layout({k: np.asarray(v) for k, v in inputs.items()})
    nc = bacc.Bacc("TRN2", target_bir_lowering=False, num_devices=1)
    A = {k: nc.dram_tensor("in_" + k, v.shape, mybir.dt.from_np(v.dtype), kind="ExternalInput").ap()
         for k, v in arrays.items()}
    out = nc.dram_tensor("out_x", (BATCH, SEQ, D), F32, kind="ExternalOutput").ap()
    build(nc, A, out)
    r = run_bass_kernel_spmd(nc, [{"in_" + k: v for k, v in arrays.items()}], core_ids=[0])
    return r.results[0]["out_x"]
```

```python
from contextlib import ExitStack

import numpy as np

import concourse.bass as bass
from concourse import mybir

F32 = mybir.dt.float32
BF16 = mybir.dt.bfloat16
F32R = mybir.dt.float32r
ALU = mybir.AluOpType
ACT = mybir.ActivationFunctionType
AX = mybir.AxisListType

P = 128
BATCH, SEQ, D = 8, 256, 256
TOK = BATCH * SEQ
KC = D // P
TILES = TOK // P
CH = 512
TURNS = TOK // CH
CT = CH // P
ST = SEQ // P
EPS = 1e-5
NEG = -1.0e30

NH0, HD0 = 32, 8
HPQ = 4
PAIRS = NH0 // 2
SLOTS = 2 * PAIRS
BLK = 3 * P
RING = 3
LAG = 2

E0, F0, K0, FS0 = 8, 176, 2, 352
E1, F1, K1, FS1 = 16, 176, 4, 352
NT0 = -(-(E0 * F0 + FS0) // P)
NT1 = -(-(E1 * F1 + FS1) // P)
WT = 2 * KC * P + D

NH1, DK, M = 16, 128, 64
HW = KC * (DK + DK + 2 * DK)
R1 = 16
SCALE1 = DK ** -0.5
CLAMP = 32.0
PAIR1 = NH1 // 2

NORM_TILE, TURN_TILE, LOGITS_TILE, TOKENS_TILE, EXP_TILE, RANK_TILE, COEF_TILE = 5, 8, 11, 12, 14, 18, 23

W0Q, W0F = 0, 4 * KC * D
W1O = NH1 * HW
WCOLS = W1O + NH1 * D
W0V = W1O
assert W0V + HPQ * CT * D <= WCOLS and W0F + NT0 * WT <= (NH1 - 2) * HW and NT1 * WT <= WCOLS


def w1_head(h):
    return (NH1 - 1 - h) * HW


class Count:

    def __init__(self, sem, per, base=0):
        self.sem, self.per, self.base = sem, per, base

    def at(self, turn, n):
        return turn * self.per + (self.base + n)


def build(nc, A, out, phases=3):
    with ExitStack() as ctx:
        def sb(name, shape, dt=F32):
            return ctx.enter_context(nc.sbuf_tensor(name, shape, dt))

        def sem(name):
            return ctx.enter_context(nc.semaphore(name))

        def count(name, per):
            return Count(sem(name), per)

        ps = ctx.enter_context(nc.psum_tensor("ps", [P, 8, 512], F32))

        x_res = sb("x_res", [P, TILES, D])
        weights = sb("weights", [P, WCOLS])
        ident = sb("ident", [P, P])
        causal = sb("causal", [P, P])
        causal_b, ident_b = sb("causal_b", [P, P], BF16), sb("ident_b", [P, P], BF16)
        sel0 = sb("sel0", [3 * (E0 + 1), NT0 * P], BF16)
        sel1 = sb("sel1", [3 * (E1 + 1), NT1 * P], BF16)
        cols = sb("cols", [P, 16])
        bkm = sb("bkm", [P, HPQ])
        bqs = sb("bqs", [P, KC])
        router0 = sb("router0", [P, KC, E0])
        lower0 = sb("lower0", [P, E0 * E0])
        lower1 = sb("lower1", [P, E1 * E1])
        router1 = sb("router1", [P, KC, 2 * E1])
        expert_rows = sb("expert_rows", [P, 2, E1])
        minus_half = sb("minus_half", [P, 64])
        rope = sb("rope", [P, 2, SEQ])
        tri = sb("tri", [P, P])
        ones = sb("ones", [P, P])
        keep_a = sb("keep_a", [P, BLK])
        keep_w = sb("keep_w", [P, BLK])
        s1w = sb("s1w", [P, KC, R1])
        s2w = sb("s2w", [R1, NH1 * M])
        s2b = sb("s2b", [P, NH1 * M])
        g_half = sb("g_half", [P, 1])
        LEFT = (nc.sbuf_bytes_remaining // 4) - 64
        SPLIT = 2 * (2 * 2 * KC * P + 2 * D + 2 * CH + KC * CH)
        SPLIT1 = 2 * (KC * SEQ + 2 * 2 * KC * DK + 2 * D + 2 * SEQ)
        with nc.sbuf_tensor("split", [P, SPLIT], F32R) as split:
            pass
        work = sb("work", [P, LEFT])
        sT1 = work[:, LEFT - KC * TOK:LEFT].rearrange("p (k t) -> p k t", k=KC)
        room = {"layer0": LEFT, "slots": LEFT - KC * TOK, "experts": LEFT - KC * TOK}
        used = {"layer0": SPLIT, "slots": SPLIT1, "experts": SPLIT}

        def carve(loop, *shape, parts=P, dt=F32):
            n = int(np.prod(shape))
            words = n if dt is F32 else (n + 1) // 2
            at = used[loop]
            used[loop] += words
            assert used[loop] <= room[loop], (loop, used[loop], room[loop])
            ap = work[0:parts, at:at + words]
            if dt is not F32:
                ap = ap.bitcast(dt)
            if len(shape) == 1:
                return ap
            names = "abcd"[:len(shape)]
            return ap.rearrange(f"p ({' '.join(names)}) -> p {' '.join(names)}",
                                **dict(zip(names, shape)))

        MASK = cols[:, 0:4]
        G_NORM = cols[:, 12:13]
        BQ, BK, BV, BO = (cols[:, 4 + 2 * i:6 + 2 * i] for i in range(4))

        x_first, x_loaded, w0_loaded = sem("x_first"), sem("x_loaded"), sem("w0_loaded")
        first_loaded, consts_loaded = sem("first_loaded"), sem("consts_loaded")
        f0_loaded = sem("f0_loaded")
        casts_done, bias_done, pow_rows = sem("casts_done"), sem("bias_done"), sem("pow_rows")

        def part(at, *shape):
            n = int(np.prod(shape))
            names = "abcd"[:len(shape)]
            return split[:, at:at + n].rearrange(f"p ({' '.join(names)}) -> p {' '.join(names)}",
                                                 **dict(zip(names, shape)))

        GU = 2 * KC * P
        w_gu = part(0, 2, 2, GU)
        w_down = part(4 * GU, 2, 2, D)
        h_split = part(4 * GU + 4 * D, 2, 2, CH)
        x1_split = part(0, 2, KC, SEQ)
        w_qk = part(2 * KC * SEQ, 2, 2 * KC * DK)
        w_vg = part(2 * KC * SEQ + 4 * KC * DK, 2, 2 * KC * DK)
        at1 = 2 * KC * SEQ + 8 * KC * DK
        w_out = part(at1, 2, 2, D)
        og_split = part(at1 + 4 * D, 2, 2, SEQ)
        x_split = part(4 * GU + 4 * D + 4 * CH, 2, KC, CH)
        TERMS = ((0, 0), (0, 1), (1, 0))

        class MoE:

            def __init__(self, loop, experts, top, tiles, sel, lower, per_token, hidden_room, before=None):
                self.loop, self.E, self.top, self.NT, self.sel, self.lower = loop, experts, top, tiles, sel, lower
                self.per_token = per_token
                made = iter(before.counts) if before else None
                self.counts = []

                def count(name, per):
                    was = next(made) if made else Count(sem("moe_" + name), 0)
                    self.counts.append(Count(was.sem, per, was.at(TURNS, 0) if made else 0))
                    return self.counts[-1]

                self.logits_done = count("logits_done", 1)
                self.tokens_done = count("tokens_done", 1)
                self.coef_turned = count("coef_turned", 1)
                self.gate_up_done = count("gate_up_done", tiles)
                self.coef_done = count("coef_done", tiles)
                self.down_done = count("down_done", tiles)
                self.delta_turned = count("delta_turned", 1)
                self.logits_copied = count("logits_copied", 1)
                self.tokens_copied = count("tokens_copied", 1)
                self.router_act = count("router_act", 1 if per_token == 1 else 2)
                self.coef_copied = count("coef_copied", 1)
                self.tanh_done = count("tanh_done", tiles)
                self.out_tanh = count("out_tanh", KC)
                self.router_step = count("router_step", 9 if per_token == 1 else 15)
                self.coef_ready = count("coef_ready", 1)
                self.half_step = count("half_step", 4 * tiles)
                self.x_upper, self.x_lower = count("x_upper", 1), count("x_lower", 1)
                self.gu_upper, self.gu_lower = count("gu_upper", tiles), count("gu_lower", tiles)
                self.down_upper, self.down_lower = count("down_upper", tiles), count("down_lower", tiles)
                self.hidden_ready = count("hidden_ready", tiles)
                self.out_step = count("out_step", KC)
                self.delta_ready = count("delta_ready", 1)
                self.x_ready = count("x_ready", 2)
                self.ties_step = count("ties_step", 2)
                self.split_step = count("split_step", 6)
                self.split_ready = count("split_ready", 1)
                E, c = experts, carve
                self.lg_sb = c(loop, CH)
                self.lg_tok = c(loop, CT, E * per_token)
                self.tok = [c(loop, CT, E) for _ in range(3)]
                self.cmp = [c(loop, CT, E, E) for _ in range(2)]
                self.small = c(loop, 4, CT)
                self.coef = c(loop, CT, E + 1)
                self.part = c(loop, CT, 3, E + 1)
                self.rest = c(loop, CT, E + 1)
                self.narrow = c(loop, CT * (E + 1) + 1, dt=BF16)[:, 0:CT * (E + 1)].rearrange(
                    "p (a b) -> p a b", a=CT)
                self.coefT = c(loop, CH, dt=BF16)
                self.th = hidden_room[:, 0:2, :]
                self.half, self.both, self.hidden = (hidden_room[:, n, :] for n in (2, 3, 4))
                self.out_th = hidden_room[:, 5:5 + KC, :]
                self.delta = self.out_th

            def w(self, j):
                w0 = (W0F if self.loop == "layer0" else 0) + j * WT
                return weights[:, w0:w0 + WT]

            def pe_logits(self, pe, t, xT, rw, bank):
                n = self.E * self.per_token
                for kc in range(KC):
                    last = pe.matmul(ps[0:n, bank, :], rw[:, kc, :], xT[:, kc, :], start=kc == 0, stop=kc == KC - 1)
                last.then_inc(self.logits_done.sem, 1)

            def pe_gate_up(self, pe, t, j):
                b = j % 2
                if j == 0:
                    pe.wait_ge(self.x_lower.sem, self.x_lower.at(t, 1))
                pe.wait_ge(self.gu_lower.sem, self.gu_lower.at(t, j + 1))
                for which, bank in enumerate((2 + b, 4 + b)):
                    for n, (wp, xp) in enumerate(TERMS):
                        for kc in range(KC):
                            at = (which * KC + kc) * P
                            last = pe.matmul(ps[:, bank, :], w_gu[:, b, wp, at:at + P], x_split[:, xp, kc, :],
                                             start=n == 0 and kc == 0, stop=n == len(TERMS) - 1 and kc == KC - 1)
                last.then_inc(self.gate_up_done.sem, 1)

            def pe_router(self, pe, t, bank):
                n = self.E * self.per_token
                pe.wait_ge(self.logits_copied.sem, self.logits_copied.at(t, 1))
                for c in range(CT):
                    last = pe.matmul(ps[:, bank, c * n:(c + 1) * n], self.lg_sb[0:n, c * P:(c + 1) * P], ident[0:n, 0:n],
                                     start=True, stop=True)
                last.then_inc(self.tokens_done.sem, 1)

            def pe_coef(self, pe, t, bank):
                n = 3 * (self.E + 1)
                pe.wait_ge(self.split_ready.sem, self.split_ready.at(t, 1))
                for c in range(CT):
                    last = pe.matmul(ps[0:n, bank, c * P:(c + 1) * P],
                                     self.part[:, c, :, :].rearrange("p a b -> p (a b)"), ident[:, :],
                                     start=True, stop=True)
                last.then_inc(self.coef_turned.sem, 1)

            def pe_spread(self, pe, t, j):
                n = 3 * (self.E + 1)
                if j == 0:
                    pe.wait_ge(self.coef_copied.sem, self.coef_copied.at(t, 1))
                pe.matmul(ps[:, j % 2, :], self.sel[:, j * P:(j + 1) * P], self.coefT[0:n, :],
                          start=True, stop=True).then_inc(self.coef_done.sem, 1)

            def pe_down(self, pe, t, j):
                pe.wait_ge(self.down_lower.sem, self.down_lower.at(t, j + 1))
                pe.wait_ge(self.hidden_ready.sem, self.hidden_ready.at(t, j + 1))
                for mt in range(KC):
                    for n, (wp, hp) in enumerate(TERMS):
                        last = pe.matmul(ps[:, 6 + mt, :], w_down[:, j % 2, wp, mt * P:(mt + 1) * P], h_split[:, j % 2, hp, :],
                                         start=j == 0 and n == 0, stop=j == self.NT - 1 and n == len(TERMS) - 1)
                last.then_inc(self.down_done.sem, 1)

            def pe_tiles(self, pe, t, ahead, bank_read):
                self.pe_spread(pe, t, 0)
                self.pe_spread(pe, t, 1)
                for j in range(2, self.NT):
                    pe.wait_ge(self.half_step.sem, self.half_step.at(t, 4 * (j - 2) + 3))
                    ahead(j)
                    self.pe_gate_up(pe, t, j)
                    bank_read(j)
                    self.pe_spread(pe, t, j)
                    self.pe_down(pe, t, j - 2)
                self.pe_down(pe, t, self.NT - 2)

            def pe_delta(self, pe, t):
                pe.wait_ge(self.delta_ready.sem, self.delta_ready.at(t, 1))
                for c in range(CT):
                    for mt in range(KC):
                        last = pe.transpose(ps[:, c // 2, (c % 2) * D + mt * P:(c % 2) * D + (mt + 1) * P],
                                            self.delta[:, mt, c * P:(c + 1) * P], ident[:, :])
                last.then_inc(self.delta_turned.sem, 1)

            def act_split_x(self, act, t, norm):
                act.wait_ge(norm.xT_ready.sem, norm.xT_ready.at(t, KC))
                act.copy(x_split[:, 0, :, :], norm.xT).then_inc(self.x_upper.sem, 1)

            def act_upper_gu(self, act, t, j):
                if j >= 2:
                    act.wait_ge(self.gate_up_done.sem, self.gate_up_done.at(t, j - 1))
                act.copy(w_gu[:, j % 2, 0, :], self.w(j)[:, 0:GU]).then_inc(self.gu_upper.sem, 1)

            def act_upper_down(self, act, t, j):
                if j >= 2:
                    act.wait_ge(self.down_done.sem, self.down_done.at(t, j - 1))
                act.copy(w_down[:, j % 2, 0, :], self.w(j)[:, GU:WT]).then_inc(self.down_upper.sem, 1)

            def act_logits(self, act, t, bank):
                n = self.E * self.per_token
                act.wait_ge(self.logits_done.sem, self.logits_done.at(t, 1))
                act.copy(self.lg_sb[0:n, :], ps[0:n, bank, :]).then_inc(self.logits_copied.sem, 1)

            def act_tokens(self, act, t, bank):
                act.wait_ge(self.tokens_done.sem, self.tokens_done.at(t, 1))
                act.copy(self.lg_tok.rearrange("p c n -> p (c n)"), ps[:, bank, 0:CT * self.E * self.per_token])\
                   .then_inc(self.tokens_copied.sem, 1)
                if self.per_token == 2:
                    act.wait_ge(self.tokens_copied.sem, self.tokens_copied.at(t, 1))
                    act.activation(self.tok[0], self.lg_tok[:, :, 0:self.E], ACT.Tanh, scale=0.5).then_inc(self.router_act.sem, 1)

            def act_exp(self, act, t):
                if self.per_token == 2:
                    act.wait_ge(self.router_step.sem, self.router_step.at(t, 5))
                    act.activation(self.tok[1], self.tok[0], ACT.Exp, scale=0.5).then_inc(self.router_act.sem, 1)
                else:
                    act.wait_ge(self.router_step.sem, self.router_step.at(t, 2))
                    act.activation(self.tok[1], self.tok[0], ACT.Exp).then_inc(self.router_act.sem, 1)

            def act_coef(self, act, t, bank):
                n = 3 * (self.E + 1)
                act.wait_ge(self.coef_turned.sem, self.coef_turned.at(t, 1))
                act.copy(self.coefT[0:n, :], ps[0:n, bank, :]).then_inc(self.coef_copied.sem, 1)

            def act_tanh(self, act, t, j):
                act.wait_ge(self.gate_up_done.sem, self.gate_up_done.at(t, j + 1))
                if j >= 2:
                    act.wait_ge(self.hidden_ready.sem, self.hidden_ready.at(t, j - 1))
                act.activation(self.th[:, j % 2, :], ps[:, 2 + j % 2, :], ACT.Tanh, scale=0.5)\
                   .then_inc(self.tanh_done.sem, 1)

            def act_tiles(self, act, t, ahead, loaded):
                for j in range(2, self.NT):
                    ahead(j)
                    self.act_tanh(act, t, j)
                    if j + 2 < self.NT:
                        loaded(j + 2)
                        self.act_upper_gu(act, t, j + 2)
                    if j + 1 < self.NT:
                        self.act_upper_down(act, t, j)

            def act_out(self, act, t):
                act.wait_ge(self.down_done.sem, self.down_done.at(t, self.NT))
                for mt in range(KC):
                    act.activation(self.out_th[:, mt, :], ps[:, 6 + mt, :], ACT.Tanh, scale=0.5)\
                       .then_inc(self.out_tanh.sem, 1)

            def pool_ties(self, pool, t, n):
                E = self.E
                gt, eq = self.cmp
                low = self.lower[:, :].rearrange("p (e f) -> p e f", e=E).unsqueeze(1).broadcast_to([P, CT, E, E])
                if n == 0:
                    pool.wait_ge(self.router_step.sem, self.router_step.at(t, 7 if self.per_token == 1 else 13))
                    pool.tensor_tensor(eq, eq, low, ALU.mult).then_inc(self.ties_step.sem, 1)
                else:
                    pool.wait_ge(self.ties_step.sem, self.ties_step.at(t, 1))
                    pool.tensor_tensor(gt, gt, eq, ALU.add).then_inc(self.ties_step.sem, 1)

            def pool_coef(self, pool, t):
                n = [0]
                zero = zeros.unsqueeze(2).broadcast_to([P, CT, self.E + 1])

                def step(ins):
                    n[0] += 1
                    ins.then_inc(self.split_step.sem, 1)
                    pool.wait_ge(self.split_step.sem, self.split_step.at(t, n[0]))

                pool.wait_ge(self.coef_ready.sem, self.coef_ready.at(t, 1))
                step(pool.tensor_tensor(self.narrow, self.coef, zero, ALU.add))
                step(pool.tensor_tensor(self.part[:, :, 0, :], self.narrow, zero, ALU.add))
                step(pool.tensor_tensor(self.rest, self.coef, self.part[:, :, 0, :], ALU.subtract))
                step(pool.tensor_tensor(self.narrow, self.rest, zero, ALU.add))
                step(pool.tensor_tensor(self.part[:, :, 1, :], self.narrow, zero, ALU.add))
                step(pool.tensor_tensor(self.coef, self.rest, self.part[:, :, 1, :], ALU.subtract))
                pool.tensor_tensor(self.part[:, :, 2, :], self.coef, zero, ALU.add).then_inc(self.split_ready.sem, 1)
                assert n[0] == self.split_step.per

            def pool_lower_gu(self, pool, t, j):
                pool.wait_ge(self.gu_upper.sem, self.gu_upper.at(t, j + 1))
                pool.tensor_tensor(w_gu[:, j % 2, 1, :], self.w(j)[:, 0:GU], w_gu[:, j % 2, 0, :], ALU.subtract)\
                    .then_inc(self.gu_lower.sem, 1)

            def pool_lower_down(self, pool, t, j):
                pool.wait_ge(self.down_upper.sem, self.down_upper.at(t, j + 1))
                pool.tensor_tensor(w_down[:, j % 2, 1, :], self.w(j)[:, GU:WT], w_down[:, j % 2, 0, :], ALU.subtract)\
                    .then_inc(self.down_lower.sem, 1)

            def split_x(self, eng, t, norm):
                eng.wait_ge(self.x_upper.sem, self.x_upper.at(t, 1))
                eng.tensor_tensor(x_split[:, 1, :, :], norm.xT, x_split[:, 0, :, :], ALU.subtract).then_inc(self.x_lower.sem, 1)

            def pool_tiles(self, pool, t, ahead):
                for j in range(1, self.NT):
                    if j + 1 < self.NT:
                        self.pool_lower_gu(pool, t, j + 1)
                        self.pool_lower_down(pool, t, j)
                    ahead(j)

            def router_stepper(self, dve, t, done):
                n = [done]

                def step(ins):
                    n[0] += 1
                    ins.then_inc(self.router_step.sem, 1)
                    dve.wait_ge(self.router_step.sem, self.router_step.at(t, n[0]))

                return step

            def dve_router_scores(self, dve, t):
                step = self.router_stepper(dve, t, 0)
                a, b, c = self.tok
                lg = self.lg_tok
                E, mx = self.E, self.small[:, 0, :]
                dve.wait_ge(self.tokens_copied.sem, self.tokens_copied.at(t, 1))
                if self.per_token == 2:
                    dve.wait_ge(self.router_act.sem, self.router_act.at(t, 1))
                    step(dve.scalar_tensor_tensor(b, a, 1.0, lg[:, :, 0:E], ALU.add, ALU.mult))
                    step(dve.tensor_tensor(c, b, lg[:, :, E:2 * E], ALU.mult))
                    step(dve.scalar_tensor_tensor(b, c, -1.0, c, ALU.mult, ALU.max))
                    lg = b
                step(dve.tensor_reduce(mx, lg, AX.X, ALU.max))
                step(dve.tensor_tensor(a, lg, mx.unsqueeze(2).broadcast_to([P, CT, E]), ALU.subtract))

            def dve_router_probs(self, dve, t):
                step = self.router_stepper(dve, t, 2 if self.per_token == 1 else 5)
                a, b, c = self.tok
                row = [P, CT, self.E]
                sm, inv = self.small[:, 1, :], self.small[:, 2, :]
                dve.wait_ge(self.router_act.sem, self.router_act.at(t, self.per_token))
                step(dve.tensor_reduce(sm, b, AX.X, ALU.add))
                step(dve.reciprocal(inv, sm))
                step(dve.tensor_tensor(a, b, inv.unsqueeze(2).broadcast_to(row), ALU.mult))
                if self.per_token == 2:
                    step(dve.tensor_tensor(c, a, expert_rows[:, 1, :].unsqueeze(1).broadcast_to(row), ALU.add))
                    step(dve.tensor_tensor(b, a, expert_rows[:, 0, :].unsqueeze(1).broadcast_to(row), ALU.mult))
                    step(dve.tensor_scalar(a, b, 1.0, None, ALU.add))

            def dve_router_compare(self, dve, t, n):
                E = self.E
                step = self.router_stepper(dve, t, n + (5 if self.per_token == 1 else 11))
                cube = [P, CT, E, E]
                rank_of = self.tok[0 if self.per_token == 1 else 2]
                mine = rank_of.unsqueeze(3).broadcast_to(cube)
                other = rank_of.unsqueeze(2).broadcast_to(cube)
                step(dve.tensor_tensor(self.cmp[n], other, mine, (ALU.is_gt, ALU.is_equal)[n]))

            def dve_router_choose(self, dve, t):
                step = self.router_stepper(dve, t, 7 if self.per_token == 1 else 13)
                a, b, c = self.tok
                dve.wait_ge(self.ties_step.sem, self.ties_step.at(t, 2))
                dve.memset(self.coef[:, :, self.E:self.E + 1], 0.5)
                step(dve.tensor_reduce(b, self.cmp[0], AX.X, ALU.add))
                step(dve.tensor_scalar(c, b, self.top - 0.5, 0.5, ALU.is_lt, ALU.mult))
                dve.tensor_tensor(self.coef[:, :, 0:self.E], c, a, ALU.mult).then_inc(self.coef_ready.sem, 1)

            def dve_tiles(self, dve, t, ahead):
                for j in range(self.NT):
                    ahead(j)
                    b = j % 2
                    dve.wait_ge(self.tanh_done.sem, self.tanh_done.at(t, j + 1))
                    dve.scalar_tensor_tensor(self.half, self.th[:, b, :], 1.0, ps[:, 2 + b, :], ALU.add, ALU.mult)\
                       .then_inc(self.half_step.sem, 1)
                    dve.wait_ge(self.half_step.sem, self.half_step.at(t, 4 * j + 1))
                    dve.tensor_tensor(self.both, self.half, ps[:, 4 + b, :], ALU.mult).then_inc(self.half_step.sem, 1)
                    dve.wait_ge(self.half_step.sem, self.half_step.at(t, 4 * j + 2))
                    dve.wait_ge(self.coef_done.sem, self.coef_done.at(t, j + 1))
                    dve.tensor_tensor(self.hidden, self.both, ps[:, b, :], ALU.mult).then_inc(self.half_step.sem, 1)
                    dve.wait_ge(self.half_step.sem, self.half_step.at(t, 4 * j + 3))
                    if j >= 2:
                        dve.wait_ge(self.down_done.sem, self.down_done.at(t, j - 1))
                    dve.tensor_copy(h_split[:, b, 0, :], self.hidden).then_inc(self.half_step.sem, 1)
                    dve.wait_ge(self.half_step.sem, self.half_step.at(t, 4 * j + 4))
                    dve.tensor_tensor(h_split[:, b, 1, :], self.hidden, h_split[:, b, 0, :], ALU.subtract)\
                       .then_inc(self.hidden_ready.sem, 1)

            def dve_out(self, dve, t, sT, x_now):
                for mt in range(KC):
                    dve.wait_ge(self.out_tanh.sem, self.out_tanh.at(t, mt + 1))
                    dve.scalar_tensor_tensor(self.out_th[:, mt, :], self.out_th[:, mt, :], 1.0, ps[:, 6 + mt, :],
                                             ALU.add, ALU.mult).then_inc(self.out_step.sem, 1)
                dve.wait_ge(self.out_step.sem, self.out_step.at(t, KC))
                dve.tensor_tensor(self.delta, self.out_th, sT, ALU.mult).then_inc(self.delta_ready.sem, 1)
                dve.wait_ge(self.delta_turned.sem, self.delta_turned.at(t, 1))
                for c in range(CT // 2):
                    xs = x_now(2 * c, 2)
                    dve.scalar_tensor_tensor(xs, ps[:, c, :].rearrange("p (a d) -> p a d", a=2), 0.5, xs,
                                             ALU.mult, ALU.add).then_inc(self.x_ready.sem, 1)

        class Norm:
            def __init__(self, loop, tiles, banks, shared=False):
                self.T = tiles
                self.shared = shared
                self.banks = banks
                self.stats_done = count(loop + "_stats_done", tiles)
                self.mean_done = count(loop + "_mean_done", tiles)
                self.var_done = count(loop + "_var_done", 1)
                self.rstd_done = count(loop + "_rstd_done", 1)
                self.xn_ready = count(loop + "_xn_ready", tiles)
                self.xn_turned = count(loop + "_xn_turned", KC)
                self.xT_ready = count(loop + "_xT_ready", KC)
                self.stats = carve(loop, tiles, 6)
                self.mean = carve(loop, tiles, 2)
                self.var = carve(loop, tiles)
                self.rstd = carve(loop, tiles)
                self.xn = carve(loop, tiles, D)
                self.xT = carve(loop, KC, tiles * P)

            def dve_all(self, dve, t, x_now):
                self.dve_stats(dve, t, x_now)
                self.dve_scale(dve, t, x_now)

            def dve_stats(self, dve, t, x_now):
                T = self.T
                for c in range(T):
                    dve.bn_stats(self.stats[:, c, :], x_now(c, 1).rearrange("p a d -> p (a d)"))\
                       .then_inc(self.stats_done.sem, 1)
                dve.wait_ge(self.stats_done.sem, self.stats_done.at(t, T))
                dve.memset(self.rstd, 0.0)
                for c in range(T):
                    dve.bn_aggr(self.mean[:, c, :], self.stats[:, c, :]).then_inc(self.mean_done.sem, 1)

            def dve_scale(self, dve, t, x_now):
                dve.wait_ge(self.rstd_done.sem, self.rstd_done.at(t, 1))
                for c in range(self.T):
                    dve.tensor_scalar(self.xn[:, c, :], x_now(c, 1).rearrange("p a d -> p (a d)"),
                                      self.mean[:, c, 0:1], self.rstd[:, c:c + 1], ALU.subtract, ALU.mult)\
                       .then_inc(self.xn_ready.sem, 1)

            def pool_all(self, pool, t):
                T = self.T
                pool.wait_ge(self.mean_done.sem, self.mean_done.at(t, T))
                pool.tensor_tensor(self.var, self.mean[:, :, 1], eps_row[:, 0:T], ALU.add).then_inc(self.var_done.sem, 1)
                pool.wait_ge(self.var_done.sem, self.var_done.at(t, 1))
                pool.tensor_tensor(self.rstd, self.var, minus_half[:, 0:T], ALU.pow).then_inc(self.rstd_done.sem, 1)

            def pe_all(self, pe, t):
                for kc in range(KC):
                    self.pe_turn(pe, t, kc)

            def pe_turn(self, pe, t, kc):
                if kc == 0:
                    pe.wait_ge(self.xn_ready.sem, self.xn_ready.at(t, self.T))
                for c in range(self.T):
                    last = pe.transpose(self.banks[kc][:, c * P:(c + 1) * P], self.xn[:, c, kc * P:(kc + 1) * P], ident[:, :])
                last.then_inc(self.xn_turned.sem, 1)

            def act_all(self, act, t):
                for kc in range(KC):
                    self.act_copy(act, t, kc)

            def act_copy(self, act, t, kc):
                act.wait_ge(self.xn_turned.sem, self.xn_turned.at(t, KC if self.shared else kc + 1))
                act.copy(self.xT[:, kc, :], self.banks[kc]).then_inc(self.xT_ready.sem, 1)

        eps_row, eps_dk, zeros = minus_half[:, 16:32], minus_half[:, 32:32 + ST * 2], minus_half[:, 48:49]

        norm0 = Norm("layer0", CT, [ps[:, kc, :] for kc in range(KC)])
        qT = carve("layer0", KC, CH)
        kTm = carve("layer0", HPQ, KC, CH)
        v0 = weights[:, W0V:W0V + HPQ * CT * D].rearrange("p (j c d) -> p j c d", j=HPQ, c=CT)
        prob = carve("layer0", RING, 2, BLK)
        probT = carve("layer0", 2, 2, BLK)
        nmax = carve("layer0", RING, ST, 2)
        total = carve("layer0", 2, ST, NH0)
        inv0 = carve("layer0", 2, ST * NH0)
        inv_wide = carve("layer0", 2, ST * NH0, HD0)
        oT0 = norm0.xn.rearrange("p c d -> p (c d)").rearrange("p (k t) -> p k t", k=KC)
        sT0 = qT
        moe0 = MoE("layer0", E0, K0, NT0, sel0, lower0, 1, kTm.rearrange("p j k t -> p (j k) t"))

        HEADS2 = 2 * SLOTS
        q_done, k_done, v_done = count("q_done", KC), count("k_done", KC), count("v_done", 2)
        qT_ready, v_ready = count("qT_ready", KC), count("v_ready", 2 * HPQ)
        keys_dve, keys_act = count("keys_dve", HPQ), count("keys_act", HPQ)
        scores_done = count("scores_done", HEADS2)
        max_ready = count("max_ready", 2 * SLOTS)
        exp_done = count("exp_done", HEADS2)
        prob_turned = count("prob_turned", HEADS2)
        probT_ready = count("probT_ready", HEADS2)
        pv_done = count("pv_done", HEADS2)
        inv_ready, wide_ready, inv_turned = count("inv_ready", 2), count("wide_ready", 2), count("inv_turned", 2)
        o_copied, o_ready, oT_ready = count("o_copied", 2), count("o_ready", 2), count("oT_ready", 2 * KC)
        out_done, sT_ready = count("out_done", KC), count("sT_ready", KC)

        def w0(which, kc, a, b):
            at = W0Q + (which * KC + kc) * D
            return weights[:, at + a:at + b]

        def pair_of(s):
            w = s % PAIRS
            return s // PAIRS, w // (PAIRS // 2), (w % (PAIRS // 2)) // 2, (2 * (w % 2), 2 * (w % 2) + 1)

        def head_of(n):
            bb, mt, j, rows = pair_of(n // 2)
            return mt * (NH0 // KC) + rows[n % 2] * HPQ + j

        def pe_queries_keys(pe, t, mt):
            xT = norm0.xT
            if mt == 0:
                pe.wait_ge(norm0.xT_ready.sem, norm0.xT_ready.at(t, KC))
            for which, bank, done in ((0, 2 + mt, q_done), (1, 4 + mt, k_done)):
                for kc in range(KC):
                    last = pe.matmul(ps[:, bank, :], w0(which, kc, mt * P, (mt + 1) * P), xT[:, kc, :],
                                     start=kc == 0, stop=kc == KC - 1)
                last.then_inc(done.sem, 1)

        def pe_values(pe, t, half):
            xT = norm0.xT
            for c in range(2 * half, 2 * half + 2):
                for kc in range(KC):
                    last = pe.matmul(ps[:, 6 + half, (c % 2) * D:(c % 2 + 1) * D], xT[:, kc, c * P:(c + 1) * P],
                                     w0(2, kc, 0, D), start=kc == 0, stop=kc == KC - 1)
            last.then_inc(v_done.sem, 1)

        def pe_layer0(pe, t):
            moe0.pe_logits(pe, t, norm0.xT, router0, 0)
            pe_values(pe, t, 1)
            moe0.pe_router(pe, t, 1)

            def scores(s, hh):
                bb, mt, j, rows = pair_of(s)
                bank, r, q0 = 2 * (s % 2) + hh, rows[hh], bb * SEQ
                if s == 0 and hh == 0:
                    pe.wait_ge(qT_ready.sem, qT_ready.at(t, KC))
                    pe.wait_ge(keys_dve.sem, keys_dve.at(t, HPQ))
                    pe.wait_ge(moe0.tokens_copied.sem, moe0.tokens_copied.at(t, 1))
                if s == PAIRS // 2 and hh == 0:
                    pe.wait_ge(keys_act.sem, keys_act.at(t, HPQ))
                if s >= 2 and hh == 0:
                    pe.wait_ge(exp_done.sem, exp_done.at(t, 2 * s - 2))
                q = qT[32 * r:32 * r + 32, mt, :]
                k = kTm[32 * r:32 * r + 32, j, mt, :]
                pe.matmul(ps[:, bank, 0:P], q[:, q0:q0 + P], k[:, q0:q0 + P], start=True, stop=False)
                pe.matmul(ps[:, bank, 0:P], ident_b[:, :], causal_b[:, :], start=False, stop=True)
                pe.matmul(ps[:, bank, P:BLK], q[:, q0 + P:q0 + SEQ], k[:, q0:q0 + SEQ], start=True, stop=False,
                          skip_group_check=True)
                pe.matmul(ps[:, bank, 2 * P:BLK], ident_b[:, :], causal_b[:, :], start=False, stop=True,
                          skip_group_check=True).then_inc(scores_done.sem, 1)

            def turn(s, hh):
                pe.wait_ge(exp_done.sem, exp_done.at(t, 2 * s + hh + 1))
                if s == 0 and hh == 0:
                    pe.wait_ge(keys_act.sem, keys_act.at(t, HPQ))
                if s:
                    pe.wait_ge(probT_ready.sem, probT_ready.at(t, 2 * s - 1 + hh))
                for k in range(3):
                    last = pe.transpose(ps[:, 4 + hh, k * P:(k + 1) * P], prob[:, s % RING, hh, k * P:(k + 1) * P],
                                        ident[:, :])
                last.then_inc(prob_turned.sem, 1)

            def pv(s, hh):
                bb, mt, j, rows = pair_of(s)
                if s == 0 and hh == 0:
                    pe.wait_ge(v_ready.sem, v_ready.at(t, 2 * HPQ))
                pe.wait_ge(probT_ready.sem, probT_ready.at(t, 2 * s + hh + 1))
                r = 32 * rows[hh]
                pt = probT[:, s % 2, hh, :]
                at = mt * SEQ
                pe.matmul(ps[r:r + 32, 6 + bb, at:at + SEQ], v0[:, j, ST * bb, mt * P + r:mt * P + r + 32], pt[:, 0:SEQ],
                          start=j == 0, stop=False, skip_group_check=True)
                pe.matmul(ps[r:r + 32, 6 + bb, at + P:at + SEQ], v0[:, j, ST * bb + 1, mt * P + r:mt * P + r + 32],
                          pt[:, SEQ:BLK], start=False, stop=j == HPQ - 1, skip_group_check=True).then_inc(pv_done.sem, 1)

            def turn_inverse(bb):
                pe.wait_ge(wide_ready.sem, wide_ready.at(t, bb + 1))
                if bb == 0:
                    pe.wait_ge(exp_done.sem, exp_done.at(t, HEADS2))
                wide = inv_wide[:, bb, :, :].rearrange("p n e -> p (n e)")
                for mt in range(KC):
                    for c in range(ST):
                        last = pe.transpose(ps[:, bb, mt * SEQ + c * P:mt * SEQ + (c + 1) * P],
                                            wide[:, c * D + mt * P:c * D + (mt + 1) * P], ident[:, :])
                last.then_inc(inv_turned.sem, 1)

            for s in range(SLOTS + LAG + 1):
                for hh in range(2):
                    if s < SLOTS:
                        scores(s, hh)
                for hh in range(2):
                    if LAG <= s < SLOTS + LAG:
                        turn(s - LAG, hh)
                for hh in range(2):
                    if s > LAG:
                        pv(s - LAG - 1, hh)
            turn_inverse(0)
            turn_inverse(1)
            pe.wait_ge(o_copied.sem, o_copied.at(t, 1))
            moe0.pe_coef(pe, t, 6)
            moe0.pe_gate_up(pe, t, 0)
            moe0.pe_gate_up(pe, t, 1)
            pe.wait_ge(oT_ready.sem, oT_ready.at(t, 2 * KC))
            for mt in range(KC):
                for kc in range(KC):
                    last = pe.matmul(ps[:, mt, :], w0(3, kc, mt * P, (mt + 1) * P), oT0[:, kc, :],
                                     start=kc == 0, stop=kc == KC - 1)
                last.then_inc(out_done.sem, 1)

        def act_layer0(act, t):
            def queries(mt):
                act.wait_ge(q_done.sem, q_done.at(t, mt + 1))
                act.activation(qT[:, mt, :], ps[:, 2 + mt, :], ACT.Identity, bias=bqs[:, mt:mt + 1],
                               scale=HD0 ** -0.5).then_inc(qT_ready.sem, 1)

            queries(0)
            queries(1)
            moe0.act_logits(act, t, 0)
            moe0.act_tokens(act, t, 1)
            act.wait_ge(k_done.sem, k_done.at(t, 2))
            for j in range(HPQ):
                act.activation(kTm[:, j, 1, :], ps[:, 5, :], ACT.Identity, bias=bkm[:, j:j + 1],
                               scale=MASK[:, j:j + 1]).then_inc(keys_act.sem, 1)
            for c in range(2):
                act.wait_ge(v_done.sem, v_done.at(t, c + 1))
                for j in range(HPQ):
                    four = slice(j * HD0, (j + 1) * HD0)
                    act.copy(v0[:, j, 2 * c:2 * c + 2, :].rearrange("p a (g w) -> p (a g) w", w=HPQ * HD0)[:, :, four],
                             ps[:, 6 + c, :].rearrange("p (a w) -> p a w", w=HPQ * HD0)[:, :, four]).then_inc(v_ready.sem, 1)

            moe0.act_exp(act, t)

            def copy_out(bb):
                act.wait_ge(pv_done.sem, pv_done.at(t, NH0 * (bb + 1)))
                act.copy(oT0[:, :, bb * SEQ:(bb + 1) * SEQ], ps[:, 6 + bb, :].rearrange("p (k q) -> p k q", k=KC))\
                   .then_inc(o_copied.sem, 1)

            def add_bias(bb):
                act.wait_ge(o_ready.sem, o_ready.at(t, bb + 1))
                for mt in range(KC):
                    seq = oT0[:, mt, bb * SEQ:(bb + 1) * SEQ]
                    act.activation(seq, seq, ACT.Identity, bias=BV[:, mt:mt + 1]).then_inc(oT_ready.sem, 1)

            for s in range(SLOTS + LAG):
                bb = s // PAIRS
                if s < SLOTS:
                    if s >= RING:
                        act.wait_ge(prob_turned.sem, prob_turned.at(t, 2 * (s - RING) + 2))
                    act.wait_ge(max_ready.sem, max_ready.at(t, 2 * s + 2))
                    for hh in range(2):
                        h = head_of(2 * s + hh)
                        pr, sc = prob[:, s % RING, hh, :], ps[:, 2 * (s % 2) + hh, :]
                        act.activation(pr[:, 0:P], sc[:, 0:P], ACT.Exp, bias=nmax[:, s % RING, 0, hh:hh + 1],
                                       accum_out=total[:, bb, 0, h:h + 1])
                        act.activation(pr[:, P:BLK], sc[:, P:BLK], ACT.Exp, bias=nmax[:, s % RING, 1, hh:hh + 1],
                                       accum_out=total[:, bb, 1, h:h + 1]).then_inc(exp_done.sem, 1)
                if s == 6:
                    moe0.act_split_x(act, t, norm0)
                if s == 8:
                    act.wait_ge(f0_loaded, 16)
                    moe0.act_upper_gu(act, t, 0)
                if s == 10:
                    moe0.act_upper_gu(act, t, 1)
                if s == 12:
                    moe0.act_upper_down(act, t, 0)
                if s == PAIRS + LAG + 2:
                    copy_out(0)
            copy_out(1)
            add_bias(0)
            add_bias(1)
            moe0.act_coef(act, t, 6)
            moe0.act_tanh(act, t, 0)
            moe0.act_upper_gu(act, t, 2)
            moe0.act_tanh(act, t, 1)
            for mt in range(KC):
                act.wait_ge(out_done.sem, out_done.at(t, mt + 1))
                act.activation(sT0[:, mt, :], ps[:, mt, :], ACT.Identity, bias=BO[:, mt:mt + 1]).then_inc(sT_ready.sem, 1)

        def dve_layer0(dve, t):
            dve.wait_ge(k_done.sem, k_done.at(t, 1))
            for j in range(HPQ):
                dve.tensor_scalar(kTm[:, j, 0, :], ps[:, 4, :], BK[:, 0:1], MASK[:, j:j + 1], ALU.add, ALU.mult)\
                   .then_inc(keys_dve.sem, 1)
            moe0.dve_router_scores(dve, t)

            def copy_probs(s):
                for hh in range(2):
                    dve.wait_ge(prob_turned.sem, prob_turned.at(t, 2 * s + hh + 1))
                    if s >= 2:
                        dve.wait_ge(pv_done.sem, pv_done.at(t, 2 * (s - 2) + hh + 1))
                    dve.tensor_copy(probT[:, s % 2, hh, :], ps[:, 4 + hh, 0:BLK]).then_inc(probT_ready.sem, 1)

            def inverse(bb):
                dve.wait_ge(exp_done.sem, exp_done.at(t, NH0 * (bb + 1)))
                dve.reciprocal(inv0[:, bb, :], total[:, bb, :, :].rearrange("p c h -> p (c h)")).then_inc(inv_ready.sem, 1)
                dve.wait_ge(inv_ready.sem, inv_ready.at(t, bb + 1))
                dve.tensor_copy(inv_wide[:, bb, :, :], inv0[:, bb, :].unsqueeze(2).broadcast_to([P, ST * NH0, HD0]))\
                   .then_inc(wide_ready.sem, 1)

            def normalise(bb):
                dve.wait_ge(inv_turned.sem, inv_turned.at(t, bb + 1))
                dve.wait_ge(o_copied.sem, o_copied.at(t, bb + 1))
                seq = oT0[:, :, bb * SEQ:(bb + 1) * SEQ]
                dve.tensor_tensor(seq, seq,
                                  ps[:, bb, :].rearrange("p (k q) -> p k q", k=KC), ALU.mult).then_inc(o_ready.sem, 1)

            for s in range(SLOTS + LAG):
                if s < SLOTS:
                    b = 2 * (s % 2)
                    sc = ps[:, b:b + 2, :]
                    dve.wait_ge(scores_done.sem, scores_done.at(t, 2 * s + 2))
                    dve.tensor_reduce(nmax[:, s % RING, 0, :], sc[:, :, 0:P], AX.X, ALU.max, negate=True)\
                       .then_inc(max_ready.sem, 1)
                    dve.tensor_reduce(nmax[:, s % RING, 1, :], sc[:, :, P:BLK], AX.X, ALU.max, negate=True)\
                       .then_inc(max_ready.sem, 1)
                if s >= LAG:
                    copy_probs(s - LAG)
                if s == 1:
                    moe0.dve_router_probs(dve, t)
                if s == 2:
                    moe0.dve_router_compare(dve, t, 0)
                    moe0.dve_router_compare(dve, t, 1)
                if s == 5:
                    moe0.dve_router_choose(dve, t)
                if s == PAIRS + LAG:
                    inverse(0)
                if s == SLOTS:
                    inverse(1)
            normalise(0)
            normalise(1)

        norm1 = Norm("slots", ST, [ps[:, 2, kc * SEQ:(kc + 1) * SEQ] for kc in range(KC)], shared=True)
        s1T = carve("slots", SEQ)
        s_sum = carve("slots", ST, P)
        s_clip = s_sum
        es = carve("slots", 2, ST, P)
        enz = carve("slots", 2, ST, P)
        esT = carve("slots", 2, SEQ)
        raw = carve("slots", 2, 2, SEQ)
        rot_s = carve("slots", 2, 2, SEQ)
        qk = carve("slots", 4, 2, SEQ)
        v1 = carve("slots", 4, ST, DK)
        gate = carve("slots", 4, ST, DK)
        aT = carve("slots", 2, BLK)
        w2T = carve("slots", 2, BLK)
        okz = carve("slots", ST, 2, M)
        oks = okp = okz
        qe = carve("slots", ST, P)
        qeT = carve("slots", SEQ)
        okmax, oksum, rs, ssq, ms, rstd1, comb = (carve("slots", ST, 2) for _ in range(7))
        og = carve("slots", 2, ST, DK)
        squares = og

        s1_done, s_done, cum_done, es_turned = count("s1_done", 1), count("s_done", PAIR1), count("cum_done", PAIR1), count("es_turned", PAIR1)
        qk_done, vg_done, a_done, ok_done = count("qk_done", NH1), count("vg_done", NH1), count("a_done", NH1), count("ok_done", PAIR1)
        qe_turned, w2_done, o_done = count("qe_turned", PAIR1), count("w2_done", NH1), count("o_done", NH1)
        og_turned, out1_done = count("og_turned", PAIR1), count("out1_done", 1)
        s1_ready, es_ready, esT_ready = count("s1_ready", 1), count("es_ready", PAIR1), count("esT_ready", PAIR1)
        raw_ready, v1_ready, gate_tanh = count("raw_ready", NH1), count("v1_ready", NH1), count("gate_tanh", NH1)
        okp_ready, qeT_ready, ssq_ready = count("okp_ready", PAIR1), count("qeT_ready", PAIR1), count("ssq_ready", NH1)
        ogT_ready, sT1_ready = count("ogT_ready", PAIR1), count("sT1_ready", 1)
        s_biased, s_clipped, enz_ready = count("s_biased", PAIR1), count("s_clipped", PAIR1), count("enz_ready", PAIR1)
        aT_ready, w2T_ready, rot_s_ready = count("aT_ready", NH1), count("w2T_ready", NH1), count("rot_s_ready", NH1)
        ok_step, oks_ready, sum_step, rs_ready = count("ok_step", 2 * PAIR1), count("oks_ready", PAIR1), count("sum_step", PAIR1), count("rs_ready", PAIR1)
        gate_ready, og_ready = count("gate_ready", NH1), count("og_ready", PAIR1)
        rot_c_ready, qk_ready, qe_ready = count("rot_c_ready", NH1), count("qk_ready", NH1), count("qe_ready", PAIR1)
        x1_upper, x1_lower = count("x1_upper", 1), count("x1_lower", 1)
        qk_upper, qk_lower, vg_upper, vg_lower = (count(n, NH1) for n in ("qk_upper", "qk_lower", "vg_upper", "vg_lower"))
        og_upper, wo_upper, wo_lower = count("og_upper", PAIR1), count("wo_upper", PAIR1), count("wo_lower", PAIR1)
        rms_step, comb_ready = count("rms_step", 2 * PAIR1), count("comb_ready", PAIR1)

        LAST = PAIR1 - 1

        def w1(h, at, n):
            at += w1_head(h % NH1)
            return weights[:, at:at + n]

        SEQ_END = BATCH - 1

        def slots_over(eng):
            eng.wait_ge(o_done.sem, o_done.at(SEQ_END, NH1 + 2))
            eng.wait_ge(esT_ready.sem, esT_ready.at(SEQ_END, PAIR1 + 2))
            eng.wait_ge(vg_lower.sem, vg_lower.at(SEQ_END, NH1 + 5))
            eng.wait_ge(qk_lower.sem, qk_lower.at(SEQ_END, NH1 + 5))
            eng.wait_ge(qk_ready.sem, qk_ready.at(SEQ_END, NH1 + 4))
            eng.wait_ge(wo_lower.sem, wo_lower.at(SEQ_END, PAIR1 + 1))

        def pe_slots(pe, t, first):
            xT = norm1.xT

            def slot_rank(turn):
                pe.wait_ge(norm1.xT_ready.sem, norm1.xT_ready.at(turn, KC))
                for kc in range(KC):
                    last = pe.matmul(ps[0:R1, 0, 0:SEQ], s1w[:, kc, :], xT[:, kc, :], start=kc == 0, stop=kc == KC - 1)
                last.then_inc(s1_done.sem, 1)

            def slot_scores(pp):
                if pp % PAIR1 == 0:
                    pe.wait_ge(s1_ready.sem, s1_ready.at(t, pp // PAIR1 + 1))
                else:
                    pe.wait_ge(esT_ready.sem, esT_ready.at(t, pp))
                for c in range(ST):
                    last = pe.matmul(ps[:, 0, c * P:(c + 1) * P], s1T[0:R1, c * P:(c + 1) * P],
                                     s2w[:, pp % PAIR1 * P:(pp % PAIR1 + 1) * P], start=True, stop=True)
                last.then_inc(s_done.sem, 1)

            def running_sum(pp):
                pe.wait_ge(es_ready.sem, es_ready.at(t, pp + 1))
                e = es[:, pp % 2, :, :]
                pe.matmul(ps[:, 0, SEQ:SEQ + P], tri[:, :], e[:, 0, :], start=True, stop=True)
                pe.matmul(ps[:, 0, SEQ + P:2 * SEQ], ones[:, :], e[:, 0, :], start=True, stop=False)
                pe.matmul(ps[:, 0, SEQ + P:2 * SEQ], tri[:, :], e[:, 1, :], start=False, stop=True)\
                  .then_inc(cum_done.sem, 1)

            def turn_es(pp):
                pe.wait_ge(enz_ready.sem, enz_ready.at(t, pp + 1))
                for c in range(ST):
                    last = pe.transpose(ps[:, 0, c * P:(c + 1) * P], es[:, pp % 2, c, :], ident[:, :])
                last.then_inc(es_turned.sem, 1)

            def queries_keys(h):
                if h % NH1 == 0:
                    pe.wait_ge(x1_lower.sem, x1_lower.at(t, h // NH1 + 1))
                pe.wait_ge(qk_lower.sem, qk_lower.at(t, h + 1))
                if h:
                    pe.wait_ge(raw_ready.sem, raw_ready.at(t, h))
                for which in range(2):
                    for n, (wp, xp) in enumerate(TERMS):
                        for kc in range(KC):
                            at = (which * KC + kc) * P
                            last = pe.matmul(ps[:, 2, which * SEQ:(which + 1) * SEQ], w_qk[:, wp, at:at + P],
                                             x1_split[:, xp, kc, :], start=n == 0 and kc == 0,
                                             stop=n == len(TERMS) - 1 and kc == KC - 1)
                last.then_inc(qk_done.sem, 1)

            def values_gates(h):
                pe.wait_ge(vg_lower.sem, vg_lower.at(t, h + 1))
                if h:
                    pe.wait_ge(gate_ready.sem, gate_ready.at(t, h))
                for c in range(ST):
                    for n, (wp, xp) in enumerate(TERMS):
                        for kc in range(KC):
                            last = pe.matmul(ps[:, 3, c * 2 * DK:(c + 1) * 2 * DK], x1_split[:, xp, kc, c * P:(c + 1) * P],
                                             w_vg[:, wp, kc * 2 * DK:(kc + 1) * 2 * DK], start=n == 0 and kc == 0,
                                             stop=n == len(TERMS) - 1 and kc == KC - 1)
                last.then_inc(vg_done.sem, 1)

            def causal_blocks(bank, key, query, done):
                pe.matmul(ps[:, bank, 0:SEQ], key[:, 0:P], query[:, 0:SEQ], start=True, stop=True)
                pe.matmul(ps[:, bank, SEQ:BLK], key[:, P:SEQ], query[:, P:SEQ], start=True, stop=True)\
                  .then_inc(done.sem, 1)

            def over_keys(outs, left, rhs):
                pe.matmul(outs[0], left[:, 0:P], rhs[0], start=True, stop=True)
                pe.matmul(outs[1], left[:, P:SEQ], rhs[0], start=True, stop=False)
                return pe.matmul(outs[1], left[:, SEQ:BLK], rhs[1], start=False, stop=True)

            def scores1(h):
                pe.wait_ge(qk_ready.sem, qk_ready.at(t, h + 1))
                if h >= 2:
                    pe.wait_ge(w2T_ready.sem, w2T_ready.at(t, h - 1))
                causal_blocks(4 + h % 2, qk[:, h % 4, 1, :], qk[:, h % 4, 0, :], a_done)

            def slots_read(pp):
                for hh in range(2):
                    h = 2 * pp + hh
                    pe.wait_ge(aT_ready.sem, aT_ready.at(t, h + 1))
                    last = over_keys([ps[:, 4 + hh, BLK + c * M:BLK + (c + 1) * M] for c in range(ST)], aT[:, hh, :],
                                     [es[:, pp % 2, c, hh * M:(hh + 1) * M] for c in range(ST)])
                last.then_inc(ok_done.sem, 1)

            def turn_qe(pp):
                pe.wait_ge(qe_ready.sem, qe_ready.at(t, pp + 1))
                for c in range(ST):
                    last = pe.transpose(ps[:, 1, c * P:(c + 1) * P], qe[:, c, :], ident[:, :])
                last.then_inc(qe_turned.sem, 1)

            def slots_write(h):
                a = slice(M * (h % 2), M * (h % 2) + M)
                causal_blocks(4 + h % 2, esT[a, (h // 2) % 2, :], qeT[a, :], w2_done)

            def mix_values(h):
                pe.wait_ge(w2T_ready.sem, w2T_ready.at(t, h + 1))
                at = (h % 2) * SEQ
                if h % 2 == 0 and h:
                    pe.wait_ge(og_ready.sem, og_ready.at(t, h // 2))
                over_keys([ps[:, 6, at + c * P:at + (c + 1) * P] for c in range(ST)], w2T[:, h % 2, :],
                          [v1[:, h % 4, c, :] for c in range(ST)]).then_inc(o_done.sem, 1)

            def turn_og(pp):
                pe.wait_ge(og_ready.sem, og_ready.at(t, pp + 1))
                for hh in range(2):
                    for c in range(ST):
                        last = pe.transpose(ps[:, 1, hh * SEQ + c * P:hh * SEQ + (c + 1) * P], og[:, hh, c, :], ident[:, :])
                last.then_inc(og_turned.sem, 1)

            def project(pp):
                pe.wait_ge(wo_lower.sem, wo_lower.at(t, pp + 1))
                pe.wait_ge(ogT_ready.sem, ogT_ready.at(t, pp + 1))
                for hh in range(2):
                    h = 2 * pp + hh
                    for mt in range(KC):
                        for n, (wp, gp) in enumerate(TERMS):
                            last = pe.matmul(ps[:, 7, mt * SEQ:(mt + 1) * SEQ], w_out[:, wp, hh, mt * P:(mt + 1) * P],
                                             og_split[:, gp, hh, :], start=h == 0 and mt == 0 and n == 0,
                                             stop=h == NH1 - 1 and n == len(TERMS) - 1, skip_group_check=True)
                if pp == PAIR1 - 1:
                    last.then_inc(out1_done.sem, 1)

            def early(pp):
                if pp == LAST:
                    pe.wait_ge(esT_ready.sem, esT_ready.at(t, PAIR1))
                    slot_rank(t + 1)
                scores1(2 * pp)
                scores1(2 * pp + 1)
                slot_scores(pp + 1)
                queries_keys(2 * pp + 2)

            def late(pp):
                behind = pp >= 1
                slots_read(pp)
                values_gates(2 * pp + 2)
                if behind:
                    turn_og(pp - 1)
                queries_keys(2 * pp + 3)
                running_sum(pp + 1)
                if behind:
                    project(pp - 1)
                turn_qe(pp)
                values_gates(2 * pp + 3)
                pe.wait_ge(qeT_ready.sem, qeT_ready.at(t, pp + 1))
                slots_write(2 * pp)
                slots_write(2 * pp + 1)
                turn_es(pp + 1)
                if pp == LAST - 1:
                    pe.wait_ge(raw_ready.sem, raw_ready.at(t, NH1))
                    norm1.pe_all(pe, t + 1)
                mix_values(2 * pp)
                mix_values(2 * pp + 1)

            if first:
                norm1.pe_all(pe, 0)
                slot_rank(0)
                slot_scores(0)
                queries_keys(0)
                values_gates(0)
                queries_keys(1)
                running_sum(0)
                values_gates(1)
                turn_es(0)
                early(0)
                late(0)
                return
            for pp in range(1, PAIR1 + 1):
                early(pp)
                late(pp)

        def act_slots(act, t, first):
            def next_tokens(turn):
                norm1.act_all(act, turn)
                act.wait_ge(norm1.xT_ready.sem, norm1.xT_ready.at(turn, KC))
                act.copy(x1_split[:, 0, :, :], norm1.xT).then_inc(x1_upper.sem, 1)

            def slot_rank(turn):
                act.wait_ge(s1_done.sem, s1_done.at(turn, 1))
                act.copy(s1T[0:R1, :], ps[0:R1, 0, 0:SEQ]).then_inc(s1_ready.sem, 1)

            def exp_scores(pp):
                act.wait_ge(s_clipped.sem, s_clipped.at(t, pp + 1))
                act.activation(es[:, pp % 2, :, :], s_clip, ACT.Exp).then_inc(es_ready.sem, 1)

            def upper_qk(h):
                if h % 2 == 0:
                    act.wait_ge(w1_loaded[h // 2 % PAIR1], 16)
                act.copy(w_qk[:, 0, :], w1(h, 0, 2 * KC * DK)).then_inc(qk_upper.sem, 1)

            def upper_wo(pp):
                if pp % PAIR1 == 0:
                    act.wait_ge(wo1_loaded, 16)
                n = pp % PAIR1
                act.activation(w_out[:, 0, :, :].rearrange("p a b -> p (a b)"), weights[:, W1O + 2 * n * D:W1O + 2 * (n + 1) * D],
                               ACT.Copy, scale=g_half[:, 0:1]).then_inc(wo_upper.sem, 1)

            def upper_vg(h):
                if h % 2 == 0:
                    act.wait_ge(w1_loaded[h // 2 % PAIR1], 16)
                act.copy(w_vg[:, 0, :], w1(h, 2 * KC * DK, 2 * KC * DK)).then_inc(vg_upper.sem, 1)

            def copy_qk(h):
                act.wait_ge(qk_done.sem, qk_done.at(t, h + 1))
                act.copy(raw[:, h % 2, :, :].rearrange("p a b -> p (a b)"), ps[:, 2, :]).then_inc(raw_ready.sem, 1)

            def gates(h):
                act.wait_ge(vg_done.sem, vg_done.at(t, h + 1))
                vg = ps[:, 3, :].rearrange("p (c w d) -> p c w d", c=ST, w=2)
                act.copy(v1[:, h % 4, :, :], vg[:, :, 0, :]).then_inc(v1_ready.sem, 1)
                if h >= 4 and h % 2 == 0:
                    act.wait_ge(og_ready.sem, og_ready.at(t, h // 2 - 1))
                act.activation(gate[:, h % 4, :, :], vg[:, :, 1, :], ACT.Tanh, scale=0.5).then_inc(gate_tanh.sem, 1)

            for pp in (-1, 0) if first else range(1, PAIR1 + 1):
                now, behind = pp >= 0, pp >= 1
                if pp == LAST:
                    slot_rank(t + 1)
                elif pp < 0:
                    upper_qk(0)
                    upper_vg(0)
                    next_tokens(0)
                    slot_rank(0)
                if behind:
                    act.wait_ge(rs_ready.sem, rs_ready.at(t, pp))
                    act.wait_ge(o_done.sem, o_done.at(t, 2 * pp))
                    for hh in range(2):
                        for c in range(ST):
                            at = hh * SEQ + c * P
                            last = act.activation(squares[:, hh, c, :], ps[:, 6, at:at + P], ACT.Square, scale=rs[:, c, hh:hh + 1],
                                                  accum_out=ssq[:, c, hh:hh + 1])
                        last.then_inc(ssq_ready.sem, 1)
                exp_scores(pp + 1)
                copy_qk(2 * pp + 2)
                upper_qk(2 * pp + 3)
                if now:
                    act.wait_ge(oks_ready.sem, oks_ready.at(t, pp + 1))
                    act.activation(okp, oks, ACT.Exp).then_inc(okp_ready.sem, 1)
                if behind:
                    act.wait_ge(og_turned.sem, og_turned.at(t, pp))
                    act.copy(og_split[:, 0, :, :].rearrange("p a b -> p (a b)"), ps[:, 1, :]).then_inc(og_upper.sem, 1)
                gates(2 * pp + 2)
                upper_vg(2 * pp + 3)
                copy_qk(2 * pp + 3)
                upper_qk(2 * pp + 4)
                if now:
                    act.wait_ge(qe_turned.sem, qe_turned.at(t, pp + 1))
                    act.copy(qeT, ps[:, 1, 0:SEQ]).then_inc(qeT_ready.sem, 1)
                    upper_wo(pp)
                gates(2 * pp + 3)
                upper_vg(2 * pp + 4)
                act.wait_ge(es_turned.sem, es_turned.at(t, pp + 2))
                act.copy(esT[:, (pp + 1) % 2, :], ps[:, 0, 0:SEQ]).then_inc(esT_ready.sem, 1)
                if pp == LAST - 1:
                    next_tokens(t + 1)
            if first:
                return
            act.wait_ge(out1_done.sem, out1_done.at(t, 1))
            act.copy(sT1[:, :, bass.ds(t * SEQ, SEQ)], ps[:, 7, :].rearrange("p (k n) -> p k n", k=KC))\
               .then_inc(sT1_ready.sem, 1)

        def dve_slots(dve, t, x_next, first):
            if first:
                norm1.dve_all(dve, 0, x_next)

            def rotate(h):
                dve.wait_ge(raw_ready.sem, raw_ready.at(t, h + 1))
                H = DK // 2
                for dst, src in ((0, H), (H, 0)):
                    last = dve.tensor_tensor(rot_s[dst:dst + H, h % 2, :, :], raw[src:src + H, h % 2, :, :],
                                             rope[src:src + H, 1, :].unsqueeze(1).broadcast_to([H, 2, SEQ]), ALU.mult)
                last.then_inc(rot_s_ready.sem, 1)

            def gates(h):
                dve.wait_ge(gate_tanh.sem, gate_tanh.at(t, h + 1))
                g = ps[:, 3, :].rearrange("p (c w d) -> p c w d", c=ST, w=2)[:, :, 1, :]
                dve.scalar_tensor_tensor(gate[:, h % 4, :, :], gate[:, h % 4, :, :], 1.0, g, ALU.add, ALU.mult)\
                   .then_inc(gate_ready.sem, 1)

            def keep(h, src_done, dst, mask, ready):
                dve.wait_ge(src_done.sem, src_done.at(t, h + 1))
                dve.tensor_tensor(dst[:, h % 2, :], ps[:, 4 + h % 2, 0:BLK], mask[:, :], ALU.mult).then_inc(ready.sem, 1)

            def lower_vg(h):
                dve.wait_ge(vg_upper.sem, vg_upper.at(t, h + 1))
                dve.tensor_tensor(w_vg[:, 1, :], w1(h, 2 * KC * DK, 2 * KC * DK), w_vg[:, 0, :], ALU.subtract)\
                   .then_inc(vg_lower.sem, 1)

            def lower_og(pp):
                dve.wait_ge(og_upper.sem, og_upper.at(t, pp + 1))
                dve.tensor_tensor(og_split[:, 1, :, :].rearrange("p a b -> p (a b)"), ps[:, 1, :],
                                  og_split[:, 0, :, :].rearrange("p a b -> p (a b)"), ALU.subtract).then_inc(ogT_ready.sem, 1)

            def lower_wo(pp):
                n = pp % PAIR1
                dve.wait_ge(wo_upper.sem, wo_upper.at(t, pp + 1))
                dve.scalar_tensor_tensor(w_out[:, 1, :, :].rearrange("p a b -> p (a b)"),
                                         weights[:, W1O + 2 * n * D:W1O + 2 * (n + 1) * D], g_half[:, 0:1],
                                         w_out[:, 0, :, :].rearrange("p a b -> p (a b)"), ALU.mult, ALU.subtract)\
                   .then_inc(wo_lower.sem, 1)

            def lower_x(turn):
                dve.wait_ge(x1_upper.sem, x1_upper.at(turn, 1))
                dve.tensor_tensor(x1_split[:, 1, :, :], norm1.xT, x1_split[:, 0, :, :], ALU.subtract).then_inc(x1_lower.sem, 1)

            if first:
                lower_vg(0)
                lower_x(0)

            def gated(pp):
                dve.wait_ge(comb_ready.sem, comb_ready.at(t, pp + 1))
                for hh in range(2):
                    for c in range(ST):
                        at = hh * SEQ + c * P
                        last = dve.scalar_tensor_tensor(og[:, hh, c, :], ps[:, 6, at:at + P], comb[:, c, hh:hh + 1],
                                                        gate[:, (2 * pp + hh) % 4, c, :], ALU.mult, ALU.mult)
                last.then_inc(og_ready.sem, 1)

            for pp in (-1, 0) if first else range(1, PAIR1 + 1):
                now, behind = pp >= 0, pp >= 1
                if now:
                    keep(2 * pp, a_done, aT, keep_a, aT_ready)
                    keep(2 * pp + 1, a_done, aT, keep_a, aT_ready)
                n = pp + 1
                dve.wait_ge(s_done.sem, s_done.at(t, n + 1))
                dve.tensor_tensor(s_sum, ps[:, 0, 0:SEQ].rearrange("p (c n) -> p c n", c=ST),
                                  s2b[:, n % PAIR1 * P:(n % PAIR1 + 1) * P].unsqueeze(1).broadcast_to([P, ST, P]), ALU.add)\
                   .then_inc(s_biased.sem, 1)
                dve.wait_ge(s_biased.sem, s_biased.at(t, n + 1))
                dve.tensor_scalar(s_clip, s_sum, -CLAMP, CLAMP, ALU.max, ALU.min).then_inc(s_clipped.sem, 1)
                if behind:
                    gated(pp - 1)
                if now:
                    dve.wait_ge(ok_done.sem, ok_done.at(t, pp + 1))
                    for hh in range(2):
                        last = dve.tensor_tensor(okz[:, :, hh, :], ps[:, 4 + hh, BLK:512].rearrange("p (c m) -> p c m", c=ST),
                                                 enz[:, pp % 2, :, hh * M:(hh + 1) * M], ALU.mult)
                    last.then_inc(ok_step.sem, 1)
                    dve.wait_ge(ok_step.sem, ok_step.at(t, 2 * pp + 1))
                    dve.tensor_reduce(okmax, okz, AX.X, ALU.max).then_inc(ok_step.sem, 1)
                    dve.wait_ge(ok_step.sem, ok_step.at(t, 2 * pp + 2))
                    flat = "p c h m -> p (c h) m"
                    dve.tensor_tensor(oks.rearrange(flat), okz.rearrange(flat),
                                      okmax.rearrange("p c h -> p (c h)").unsqueeze(2).broadcast_to([P, ST * 2, M]), ALU.subtract)\
                       .then_inc(oks_ready.sem, 1)
                rotate(2 * n)
                if behind:
                    lower_og(pp - 1)
                gates(2 * n)
                lower_vg(2 * n + 1)
                rotate(2 * n + 1)
                dve.wait_ge(cum_done.sem, cum_done.at(t, n + 1))
                dve.reciprocal(enz[:, n % 2, :, :].rearrange("p c n -> p (c n)"), ps[:, 0, SEQ:2 * SEQ])\
                   .then_inc(enz_ready.sem, 1)
                if now:
                    dve.wait_ge(okp_ready.sem, okp_ready.at(t, pp + 1))
                    dve.tensor_reduce(oksum, okp, AX.X, ALU.add).then_inc(sum_step.sem, 1)
                    dve.wait_ge(sum_step.sem, sum_step.at(t, pp + 1))
                    dve.reciprocal(rs, oksum).then_inc(rs_ready.sem, 1)
                    keep(2 * pp, w2_done, w2T, keep_w, w2T_ready)
                    keep(2 * pp + 1, w2_done, w2T, keep_w, w2T_ready)
                gates(2 * n + 1)
                lower_vg(2 * n + 2)
                if now:
                    lower_wo(pp)
                if pp == LAST - 3:
                    norm1.dve_stats(dve, t + 1, x_next)
                if pp == LAST - 2:
                    norm1.dve_scale(dve, t + 1, x_next)
                if pp == LAST - 1:
                    lower_x(t + 1)

        def pool_slots(pool, t, first):
            if first:
                norm1.pool_all(pool, 0)

            def rotate(h):
                pool.wait_ge(raw_ready.sem, raw_ready.at(t, h + 1))
                pool.tensor_tensor(qk[:, h % 4, :, :], raw[:, h % 2, :, :],
                                   rope[:, 0, :].unsqueeze(1).broadcast_to([P, 2, SEQ]), ALU.mult).then_inc(rot_c_ready.sem, 1)

            def rotate_end(h):
                pool.wait_ge(rot_c_ready.sem, rot_c_ready.at(t, h + 1))
                pool.wait_ge(rot_s_ready.sem, rot_s_ready.at(t, h + 1))
                pool.tensor_tensor(qk[:, h % 4, :, :], qk[:, h % 4, :, :], rot_s[:, h % 2, :, :], ALU.add)\
                    .then_inc(qk_ready.sem, 1)

            def lower_qk(h):
                pool.wait_ge(qk_upper.sem, qk_upper.at(t, h + 1))
                pool.tensor_tensor(w_qk[:, 1, :], w1(h, 0, 2 * KC * DK), w_qk[:, 0, :], ALU.subtract).then_inc(qk_lower.sem, 1)

            if first:
                lower_qk(0)

            def rms(pp):
                pool.wait_ge(ssq_ready.sem, ssq_ready.at(t, 2 * pp + 2))
                four = "p c h -> p (c h)"
                pool.tensor_tensor(ms.rearrange(four), ssq.rearrange(four), eps_dk, ALU.add).then_inc(rms_step.sem, 1)
                pool.wait_ge(rms_step.sem, rms_step.at(t, 2 * pp + 1))
                pool.tensor_tensor(rstd1.rearrange(four), ms.rearrange(four), minus_half[:, 0:ST * 2], ALU.pow)\
                    .then_inc(rms_step.sem, 1)
                pool.wait_ge(rms_step.sem, rms_step.at(t, 2 * pp + 2))
                pool.tensor_tensor(comb.rearrange(four), rstd1.rearrange(four), rs.rearrange(four), ALU.mult)\
                    .then_inc(comb_ready.sem, 1)

            for pp in (-1, 0) if first else range(1, PAIR1 + 1):
                now, behind = pp >= 0, pp >= 1
                if pp == LAST - 2:
                    norm1.pool_all(pool, t + 1)
                if behind:
                    rms(pp - 1)
                lower_qk(2 * pp + 3)
                rotate(2 * pp + 2)
                if now:
                    pool.wait_ge(okp_ready.sem, okp_ready.at(t, pp + 1))
                    pool.tensor_tensor(qe, okp.rearrange("p c h m -> p c (h m)"), enz[:, pp % 2, :, :], ALU.mult)\
                        .then_inc(qe_ready.sem, 1)
                rotate_end(2 * pp + 2)
                lower_qk(2 * pp + 4)
                rotate(2 * pp + 3)
                rotate_end(2 * pp + 3)

        norm2 = Norm("experts", CT, [ps[:, kc, :] for kc in range(KC)])
        moe1 = MoE("experts", E1, K1, NT1, sel1, lower1, 2, carve("experts", 5 + KC, CH), before=moe0)

        block = ctx.enter_context(nc.Block())
        first_loads = [(ident, "ident"), (cols, "cols")]
        const_loads = [(causal, "causal"), (router0, "router0"),
                       (lower0, "lower0"), (lower1, "lower1"), (router1, "router1"), (rope, "rope"), (tri, "tri"),
                       (keep_a, "keep_a"), (keep_w, "keep_w"), (s1w, "s1w"), (s2w, "s2w")]
        row_loads = [(s2b[:, :], "s2b"), (expert_rows[:, 0, :], "extra_scale"),
                     (expert_rows[:, 1, :], "extra_bias")]
        NCONST = 16 * (len(const_loads) + len(row_loads))
        MOE_LOT = [0, 1, 3, 8, 16, NT1]
        MOE_LOTS = len(MOE_LOT) - 1
        w1_loaded = [sem(f"w1_loaded{n}") for n in range(PAIR1)]
        wo1_loaded = sem("wo1_loaded")
        f1_loaded = [sem(f"f1_loaded{n}") for n in range(MOE_LOTS)]
        stored = sem("stored")

        @block.sync
        def _(sp):
            def load_pair(pp):
                at = w1_head(2 * pp + 1)
                sp.dma_start(weights[:, at:at + 2 * HW], A["w1"][:, at:at + 2 * HW]).then_inc(w1_loaded[pp], 16)

            x_tiles = A["x"].rearrange("b (c p) d -> p (b c) d", p=P)
            sp.dma_start(x_res[:, 0:CT, :], x_tiles[:, 0:CT, :]).then_inc(x_first, 16)
            for dst, name in first_loads:
                sp.dma_start(dst[tuple(slice(None) for _ in dst.shape)], A[name]).then_inc(first_loaded, 16)
            for dst, name in const_loads:
                sp.dma_start(dst[tuple(slice(None) for _ in dst.shape)], A[name]).then_inc(consts_loaded, 16)
            for dst, name in row_loads:
                sp.dma_start(dst, A[name].partition_broadcast(P)).then_inc(consts_loaded, 16)
            sp.dma_start(x_res[:, CT:TILES, :], x_tiles[:, CT:TILES, :]).then_inc(x_loaded, 16)
            sp.dma_start(weights[:, W0F:W0F + NT0 * WT].rearrange("p (j w) -> p j w", w=WT),
                         A["f0"].rearrange("j p w -> p j w")).then_inc(f0_loaded, 16)
            load_pair(0)
            sp.wait_ge(moe0.x_ready.sem, 2 * TURNS)
            for pp in range(1, PAIR1):
                if w1_head(2 * pp + 1) < W0F:
                    sp.wait_ge(v_done.sem, v_done.at(TURNS, 1))
                load_pair(pp)
                if pp == 1:
                    sp.dma_start(weights[:, W1O:WCOLS], A["wo1"]).then_inc(wo1_loaded, 16)
            slots_over(sp)
            for n in range(MOE_LOTS):
                j0, j1 = MOE_LOT[n], MOE_LOT[n + 1]
                sp.dma_start(weights[:, j0 * WT:j1 * WT].rearrange("p (j w) -> p j w", w=WT),
                             A["f1"][j0:j1].rearrange("j p w -> p j w")).then_inc(f1_loaded[n], 16)
            with sp.Fori(0, TURNS) as t:
                sp.wait_ge(moe1.x_ready.sem, moe1.x_ready.at(t, 2))
                sp.dma_start(out.rearrange("b (c p) d -> p (b c) d", p=P)[:, bass.ds(t * CT, CT), :],
                             x_res[:, bass.ds(t * CT, CT), :]).then_inc(stored, 16)
            sp.wait_ge(stored, 16 * TURNS)

        @block.gpsimd
        def _(pool):
            pool.dma_start(sel0[:, :], A["sel0"]).then_inc(casts_done, 16)
            pool.dma_start(sel1[:, :], A["sel1"]).then_inc(casts_done, 16)
            for n, value in enumerate((-0.5, EPS, DK * EPS, 0.0)):
                pool.memset(minus_half[:, 16 * n:16 * n + 16], value).then_inc(pow_rows, 1)
            pool.memset(ones[:, :], 1.0).then_inc(pow_rows, 1)
            pool.wait_ge(pow_rows, 5)
            norm0.pool_all(pool, 0)
            pool.memset(v0, 0.0).then_inc(pow_rows, 1)
            pool.wait_ge(consts_loaded, NCONST)
            with pool.Fori(0, TURNS) as t:
                def ahead(j):
                    if j == NORM_TILE:
                        norm0.pool_all(pool, t + 1)

                moe0.pool_ties(pool, t, 0)
                moe0.pool_ties(pool, t, 1)
                moe0.pool_coef(pool, t)
                moe0.split_x(pool, t, norm0)
                moe0.pool_lower_gu(pool, t, 0)
                moe0.pool_lower_gu(pool, t, 1)
                moe0.pool_lower_down(pool, t, 0)
                moe0.pool_tiles(pool, t, ahead)
                moe0.pool_lower_down(pool, t, NT0 - 1)
            pool_slots(pool, 0, True)
            with pool.Fori(0, BATCH) as t:
                pool_slots(pool, t, False)
            slots_over(pool)
            norm2.pool_all(pool, 0)
            moe1.pool_lower_gu(pool, 0, 0)
            moe1.pool_lower_gu(pool, 0, 1)
            moe1.pool_lower_down(pool, 0, 0)
            moe1.pool_ties(pool, 0, 0)
            moe1.pool_ties(pool, 0, 1)
            moe1.pool_coef(pool, 0)
            with pool.Fori(0, TURNS) as t:
                def ahead(j):
                    if j == NORM_TILE:
                        norm2.pool_all(pool, t + 1)
                    if RANK_TILE <= j < RANK_TILE + 2:
                        moe1.pool_ties(pool, t + 1, j - RANK_TILE)
                    if j == COEF_TILE:
                        moe1.pool_coef(pool, t + 1)

                moe1.pool_tiles(pool, t, ahead)
                moe1.pool_lower_gu(pool, t + 1, 0)
                moe1.pool_lower_down(pool, t, NT1 - 1)
                moe1.pool_lower_gu(pool, t + 1, 1)
                moe1.pool_lower_down(pool, t + 1, 0)

        @block.vector
        def _(dve):
            dve.wait_ge(x_first, 16)
            norm0.dve_stats(dve, 0, lambda c, n: x_res[:, c:c + n, :])
            dve.wait_ge(first_loaded, 16 * len(first_loads))
            dve.tensor_scalar(bqs[:, :], BQ, HD0 ** -0.5, None, ALU.mult).then_inc(bias_done, 1)
            dve.tensor_scalar(bkm[:, :], MASK, BK[:, 1:2], None, ALU.mult).then_inc(bias_done, 1)
            norm0.dve_scale(dve, 0, lambda c, n: x_res[:, c:c + n, :])
            dve.tensor_copy(ident_b[:, :], ident[:, :]).then_inc(bias_done, 1)
            dve.wait_ge(consts_loaded, NCONST)
            dve.tensor_scalar(g_half[:, :], G_NORM, 0.5 * DK ** 0.5, None, ALU.mult).then_inc(bias_done, 1)
            dve.tensor_copy(causal_b[:, :], causal[:, :]).then_inc(bias_done, 1)
            dve.wait_ge(x_loaded, 16)
            with dve.Fori(0, TURNS) as t:
                def x_now(c, n):
                    return x_res[:, bass.ds(t * CT + c, n), :]

                def x_next(c, n):
                    return x_res[:, bass.ds((t + 1) % TURNS * CT + c, n), :]

                def ahead(j):
                    if j == NORM_TILE:
                        norm0.dve_stats(dve, t + 1, x_next)
                    if j == NORM_TILE + 1:
                        norm0.dve_scale(dve, t + 1, x_next)

                dve_layer0(dve, t)
                moe0.dve_tiles(dve, t, ahead)
                dve.wait_ge(sT_ready.sem, sT_ready.at(t, KC))
                moe0.dve_out(dve, t, sT0, x_now)
            dve.wait_ge(moe0.x_ready.sem, 2 * TURNS)
            dve_slots(dve, 0, lambda c, n: x_res[:, c:c + n, :], True)
            with dve.Fori(0, BATCH) as t:
                dve_slots(dve, t, lambda c, n: x_res[:, bass.ds((t + 1) % BATCH * ST + c, n), :], False)
            dve.wait_ge(sT1_ready.sem, BATCH)
            slots_over(dve)
            norm2.dve_all(dve, 0, lambda c, n: x_res[:, c:c + n, :])
            moe1.split_x(dve, 0, norm2)
            moe1.dve_router_scores(dve, 0)
            moe1.dve_router_probs(dve, 0)
            moe1.dve_router_compare(dve, 0, 0)
            moe1.dve_router_compare(dve, 0, 1)
            moe1.dve_router_choose(dve, 0)
            with dve.Fori(0, TURNS) as t:
                def x_now(c, n):
                    return x_res[:, bass.ds(t * CT + c, n), :]

                def x_next(c, n):
                    return x_res[:, bass.ds((t + 1) % TURNS * CT + c, n), :]

                def ahead(j):
                    if j == NORM_TILE:
                        norm2.dve_stats(dve, t + 1, x_next)
                    if j == NORM_TILE + 1:
                        norm2.dve_scale(dve, t + 1, x_next)
                    if j == TOKENS_TILE + 1:
                        moe1.dve_router_scores(dve, t + 1)
                    if j == EXP_TILE + 1:
                        moe1.dve_router_probs(dve, t + 1)
                    if RANK_TILE - 2 <= j < RANK_TILE:
                        moe1.dve_router_compare(dve, t + 1, j - RANK_TILE + 2)
                    if j == COEF_TILE - 2:
                        moe1.dve_router_choose(dve, t + 1)

                moe1.dve_tiles(dve, t, ahead)
                moe1.split_x(dve, t + 1, norm2)
                moe1.dve_out(dve, t, sT1[:, :, bass.ds(t * CH, CH)], x_now)

        @block.scalar
        def _(act):
            act.dma_start(weights[:, W0Q:W0F], A["w0"]).then_inc(w0_loaded, 16)
            norm0.act_all(act, 0)
            act.wait_ge(bias_done, 5)
            act.wait_ge(pow_rows, 6)
            with act.Fori(0, TURNS) as t:
                def ahead(j):
                    if TURN_TILE <= j < TURN_TILE + KC:
                        norm0.act_copy(act, t + 1, j - TURN_TILE)

                act_layer0(act, t)
                moe0.act_upper_down(act, t, 1)
                moe0.act_upper_gu(act, t, 3)
                moe0.act_tiles(act, t, ahead, lambda j: None)
                moe0.act_upper_down(act, t, NT0 - 1)
                moe0.act_out(act, t)
                act.wait_ge(moe0.delta_turned.sem, moe0.delta_turned.at(t, 1))
            act_slots(act, 0, True)
            with act.Fori(0, BATCH) as t:
                act_slots(act, t, False)
            def loaded(j):
                if j in MOE_LOT:
                    act.wait_ge(f1_loaded[MOE_LOT.index(j)], 16)

            slots_over(act)
            norm2.act_all(act, 0)
            moe1.act_split_x(act, 0, norm2)
            moe1.act_logits(act, 0, LOGITS_TILE % 2)
            moe1.act_tokens(act, 0, TOKENS_TILE % 2)
            loaded(0)
            moe1.act_upper_gu(act, 0, 0)
            loaded(1)
            moe1.act_upper_gu(act, 0, 1)
            moe1.act_upper_down(act, 0, 0)
            moe1.act_exp(act, 0)
            moe1.act_coef(act, 0, 1)
            with act.Fori(0, TURNS) as t:
                def ahead(j):
                    if TURN_TILE <= j < TURN_TILE + KC:
                        norm2.act_copy(act, t + 1, j - TURN_TILE)
                    if j == LOGITS_TILE:
                        moe1.act_logits(act, t + 1, j % 2)
                    if j == TOKENS_TILE:
                        moe1.act_tokens(act, t + 1, j % 2)
                    if j == EXP_TILE:
                        moe1.act_exp(act, t + 1)

                moe1.act_upper_down(act, t, 1)
                moe1.act_tanh(act, t, 0)
                moe1.act_upper_gu(act, t, 2)
                moe1.act_tanh(act, t, 1)
                loaded(3)
                moe1.act_upper_gu(act, t, 3)
                moe1.act_tiles(act, t, ahead, loaded)
                act.wait_ge(moe1.gate_up_done.sem, moe1.gate_up_done.at(t, NT1))
                moe1.act_split_x(act, t + 1, norm2)
                moe1.act_upper_gu(act, t + 1, 0)
                moe1.act_upper_down(act, t, NT1 - 1)
                moe1.act_upper_gu(act, t + 1, 1)
                moe1.act_coef(act, t + 1, 1)
                moe1.act_out(act, t)
                moe1.act_upper_down(act, t + 1, 0)

        @block.tensor
        def _(pe):
            pe.wait_ge(first_loaded, 16 * len(first_loads))
            norm0.pe_all(pe, 0)
            pe.wait_ge(w0_loaded, 16)
            pe_queries_keys(pe, 0, 0)
            pe_queries_keys(pe, 0, 1)
            pe_values(pe, 0, 0)
            pe.wait_ge(consts_loaded, NCONST)
            pe.wait_ge(bias_done, 5)
            pe.wait_ge(pow_rows, 6)
            pe.wait_ge(casts_done, 32)
            with pe.Fori(0, TURNS) as t:
                def ahead(j):
                    if TURN_TILE <= j < TURN_TILE + KC:
                        norm0.pe_turn(pe, t + 1, j - TURN_TILE)

                def bank_read(j):
                    if TURN_TILE <= j < TURN_TILE + KC:
                        pe.wait_ge(norm0.xT_ready.sem, norm0.xT_ready.at(t + 1, j - TURN_TILE + 1))

                pe_layer0(pe, t)
                pe.wait_ge(sT_ready.sem, sT_ready.at(t, KC))
                moe0.pe_tiles(pe, t, ahead, bank_read)
                pe_queries_keys(pe, t + 1, 0)
                moe0.pe_down(pe, t, NT0 - 1)
                pe_queries_keys(pe, t + 1, 1)
                moe0.pe_delta(pe, t)
                pe_values(pe, t + 1, 0)
                pe.wait_ge(moe0.x_ready.sem, moe0.x_ready.at(t, 2))
            pe_slots(pe, 0, True)
            with pe.Fori(0, BATCH) as t:
                pe_slots(pe, t, False)
            norm2.pe_all(pe, 0)
            pe.wait_ge(norm2.xT_ready.sem, norm2.xT_ready.at(0, KC))
            moe1.pe_logits(pe, 0, norm2.xT, router1, LOGITS_TILE % 2)
            moe1.pe_router(pe, 0, TOKENS_TILE % 2)
            moe1.pe_gate_up(pe, 0, 0)
            moe1.pe_gate_up(pe, 0, 1)
            moe1.pe_coef(pe, 0, 1)
            with pe.Fori(0, TURNS) as t:
                def ahead(j):
                    if TURN_TILE <= j < TURN_TILE + KC:
                        norm2.pe_turn(pe, t + 1, j - TURN_TILE)
                    if j == LOGITS_TILE:
                        moe1.pe_logits(pe, t + 1, norm2.xT, router1, j % 2)
                    if j == TOKENS_TILE:
                        moe1.pe_router(pe, t + 1, j % 2)

                def bank_read(j):
                    if TURN_TILE <= j < TURN_TILE + KC:
                        pe.wait_ge(norm2.xT_ready.sem, norm2.xT_ready.at(t + 1, j - TURN_TILE + 1))
                    if j == LOGITS_TILE:
                        pe.wait_ge(moe1.logits_copied.sem, moe1.logits_copied.at(t + 1, 1))
                    if j == TOKENS_TILE:
                        pe.wait_ge(moe1.tokens_copied.sem, moe1.tokens_copied.at(t + 1, 1))

                moe1.pe_tiles(pe, t, ahead, bank_read)
                moe1.pe_coef(pe, t + 1, 1)
                moe1.pe_down(pe, t, NT1 - 1)
                moe1.pe_gate_up(pe, t + 1, 0)
                moe1.pe_delta(pe, t)
                moe1.pe_gate_up(pe, t + 1, 1)
                pe.wait_ge(moe1.x_ready.sem, moe1.x_ready.at(t, 2))


def _constants():
    p = np.arange(P)
    tri_jt = (p[:, None] <= p[None, :]).astype(np.float32)
    one = np.ones((P, P), np.float32)
    bias = np.where(p[None, :] > p[:, None], np.float32(NEG), np.float32(0)).astype(np.float32)
    keep = np.concatenate([tri_jt, one, tri_jt], 1)
    inv_freq = 1.0 / np.float32(10000.0) ** (np.arange(0, DK, 2, dtype=np.float32) / np.float32(DK))
    ang = (np.arange(SEQ, dtype=np.float32)[:, None] * inv_freq[None, :].astype(np.float32)).astype(np.float32)
    cos, sin = np.cos(ang).T.astype(np.float32), np.sin(ang).T.astype(np.float32)

    def sel(experts, f, tiles):
        row = np.minimum(np.arange(tiles * P) // f, experts)
        hot = (row[None, :] == np.arange(experts + 1)[:, None]).astype(np.float32)
        return np.concatenate([hot] * 3, 0)

    def lower(e):
        n = np.arange(e)
        return np.ascontiguousarray(np.broadcast_to((n[None, :] < n[:, None]).astype(np.float32).reshape(1, e * e), (P, e * e)))

    return {
        "ident": np.eye(P, dtype=np.float32),
        "causal": bias,
        "sel0": sel(E0, F0, NT0), "sel1": sel(E1, F1, NT1),
        "lower0": lower(E0), "lower1": lower(E1),
        "rope": np.stack([np.concatenate([cos, cos], 0), np.concatenate([sin, -sin], 0)], 1),
        "tri": tri_jt, "keep_a": keep * np.float32(SCALE1), "keep_w": keep,
    }


def _chunks(w_t):
    return w_t.reshape(KC, P, -1).transpose(1, 0, 2)


def _moe_tiles(wg, wu, wd, sg, su, sd, tiles):
    e, f, d = wg.shape
    pad = tiles * P - e * f - sg.shape[0]
    z = np.zeros((pad, d), wg.dtype)
    gate = np.concatenate([wg.reshape(e * f, d), sg, z], 0).reshape(tiles, P, KC, P).transpose(0, 3, 2, 1)
    up = np.concatenate([wu.reshape(e * f, d), su, z], 0).reshape(tiles, P, KC, P).transpose(0, 3, 2, 1)
    down = np.concatenate([wd.transpose(0, 2, 1).reshape(e * f, d), sd.T, z], 0).reshape(tiles, P, d)
    return np.concatenate([gate.reshape(tiles, P, KC * P), up.reshape(tiles, P, KC * P), down], 2)


def layout(i):
    c = _constants()
    p = np.arange(P)
    mask = ((p[:, None] // HD0) % HPQ == np.arange(HPQ)[None, :]).astype(np.float32)
    col = [i["L0_attn_" + n].reshape(KC, P).T for n in ("bq", "bk", "bv", "bo")]
    c["cols"] = np.concatenate([mask, *col, i["L1_attn_g_norm_weight"].reshape(DK, 1), np.zeros((P, 3), np.float32)], 1)
    c["x"] = i["L0_attn_hidden_states"]
    c["w0"] = np.stack([_chunks(i["L0_attn_" + n].T) for n in ("wq", "wk", "wv", "wo")], 1).reshape(P, -1)
    c["f0"] = _moe_tiles(i["L0_ffn_Wg"], i["L0_ffn_Wu"], i["L0_ffn_Wd"], i["L0_ffn_Wsg"], i["L0_ffn_Wsu"],
                         i["L0_ffn_Wsd"], NT0)
    c["router0"] = _chunks(i["L0_ffn_Wr"].T)
    c["f1"] = _moe_tiles(i["L1_ffn_Wg"], i["L1_ffn_Wu"], i["L1_ffn_Wd"], i["L1_ffn_Sg"], i["L1_ffn_Su"],
                         i["L1_ffn_Sd"], NT1)
    c["router1"] = _chunks(np.concatenate([i["L1_ffn_rg_w"], i["L1_ffn_ru_w"]], 0).T)
    c["s1w"] = _chunks(i["L1_attn_Ws1"].T)
    c["s2w"] = i["L1_attn_Ws2"].T
    c["s2b"] = i["L1_attn_bs2"]
    c["extra_scale"], c["extra_bias"] = i["L1_ffn_extra_scale"], i["L1_ffn_extra_bias"]
    wq, wk, wv, wg = (i["L1_attn_" + n].T.reshape(KC, P, NH1, DK).transpose(2, 1, 0, 3) for n in ("Wq", "Wk", "Wv", "Wg"))
    vg = np.concatenate([wv, wg], 3)
    heads = np.concatenate([a.reshape(NH1, P, -1) for a in (wq, wk, vg)], 2)
    c["w1"] = heads[::-1].transpose(1, 0, 2).reshape(P, -1)
    c["wo1"] = i["L1_attn_Wo"].T.reshape(NH1, DK, D).transpose(1, 0, 2).reshape(P, -1)
    return {k: np.ascontiguousarray(v) for k, v in c.items()}


def kernel(**inputs):
    import concourse.bacc as bacc
    from concourse.bass_utils import run_bass_kernel_spmd

    arrays = layout({k: np.asarray(v) for k, v in inputs.items()})
    nc = bacc.Bacc("TRN2", target_bir_lowering=False, num_devices=1)
    A = {k: nc.dram_tensor("in_" + k, v.shape, mybir.dt.from_np(v.dtype), kind="ExternalInput").ap()
         for k, v in arrays.items()}
    out = nc.dram_tensor("out_x", (BATCH, SEQ, D), F32, kind="ExternalOutput").ap()
    build(nc, A, out)
    r = run_bass_kernel_spmd(nc, [{"in_" + k: v for k, v in arrays.items()}], core_ids=[0])
    return r.results[0]["out_x"]
```

```python
from contextlib import ExitStack

import numpy as np

import concourse.bass as bass
from concourse import mybir

F32 = mybir.dt.float32
BF16 = mybir.dt.bfloat16
F32R = mybir.dt.float32r
ALU = mybir.AluOpType
ACT = mybir.ActivationFunctionType
AX = mybir.AxisListType

P = 128
BATCH, SEQ, D = 8, 256, 256
TOK = BATCH * SEQ
KC = D // P
TILES = TOK // P
CH = 512
TURNS = TOK // CH
CT = CH // P
ST = SEQ // P
EPS = 1e-5
NEG = -1.0e30

NH0, HD0 = 32, 8
HPQ = 4
PAIRS = NH0 // 2
SLOTS = 2 * PAIRS
BLK = 3 * P
RING = 3
LAG = 2

E0, F0, K0, FS0 = 8, 176, 2, 352
E1, F1, K1, FS1 = 16, 176, 4, 352
NT0 = -(-(E0 * F0 + FS0) // P)
NT1 = -(-(E1 * F1 + FS1) // P)
WT = 2 * KC * P + D

NH1, DK, M = 16, 128, 64
HW = KC * (DK + DK + 2 * DK)
R1 = 16
SCALE1 = DK ** -0.5
CLAMP = 32.0
PAIR1 = NH1 // 2
RG = 32
RS = 3 * RG

NORM_TILE, TURN_TILE, LOGITS_TILE, TOKENS_TILE, EXP_TILE, RANK_TILE, COEF_TILE = 5, 8, 11, 12, 14, 18, 23

W0Q, W0F = 0, 4 * KC * D
W1O = NH1 * HW
WCOLS = W1O + NH1 * D
W0V = W1O
W0S = W0F + NT0 * WT
assert W0V + HPQ * CT * D <= WCOLS and W0S + NH1 * M + P <= (NH1 - 2) * HW and NT1 * WT <= WCOLS


def w1_head(h):
    return (NH1 - 1 - h) * HW


class Count:

    def __init__(self, sem, per, base=0):
        self.sem, self.per, self.base = sem, per, base

    def at(self, turn, n):
        return turn * self.per + (self.base + n)


def build(nc, A, out, phases=3):
    with ExitStack() as ctx:
        def sb(name, shape, dt=F32):
            return ctx.enter_context(nc.sbuf_tensor(name, shape, dt))

        def sem(name):
            return ctx.enter_context(nc.semaphore(name))

        def count(name, per):
            return Count(sem(name), per)

        ps = ctx.enter_context(nc.psum_tensor("ps", [P, 8, 512], F32))

        x_res = sb("x_res", [P, TILES, D])
        weights = sb("weights", [P, WCOLS])
        ident = sb("ident", [P, P])
        causal_b, ident_b = sb("causal_b", [P, 2 * P], BF16), sb("ident_b", [P, P], BF16)
        sel0 = sb("sel0", [3 * (E0 + 1), NT0 * P], BF16)
        sel1 = sb("sel1", [3 * (E1 + 1), NT1 * P], BF16)
        cols = sb("cols", [P, 16])
        bqs = sb("bqs", [P, KC])
        router0 = sb("router0", [P, KC, E0])
        lower0 = sb("lower0", [P, E0 * E0])
        lower1 = sb("lower1", [P, E1 * E1])
        router1 = sb("router1", [P, KC, 2 * E1])
        expert_rows = sb("expert_rows", [P, 2, E1])
        minus_half = sb("minus_half", [P, 64])
        rope = sb("rope", [P, 2, SEQ])
        tri = sb("tri", [P, P])
        tri_r, ones_r = sb("tri_r", [P, P], F32R), sb("ones_r", [P, P], F32R)
        keep_a = sb("keep_a", [P, BLK])
        keep_w = sb("keep_w", [P, BLK])
        causal = weights[:, W0S + NH1 * M:W0S + NH1 * M + P]
        s1w = sb("s1w", [P, KC, RS])
        s1_split, s2_split = sb("s1_split", [RS, SEQ], F32R), sb("s2_split", [RS, NH1 * M], F32R)
        g_half = sb("g_half", [P, 1])
        LEFT = (nc.sbuf_bytes_remaining // 4) - 64
        SPLIT = 2 * (2 * 2 * KC * P + 2 * D + 2 * CH + KC * CH)
        SPLIT1 = 2 * (KC * SEQ + 2 * 2 * KC * DK + 2 * D + 2 * SEQ + SEQ)
        with nc.sbuf_tensor("split", [P, SPLIT], F32R) as split:
            pass
        work = sb("work", [P, LEFT])
        sT1 = work[:, LEFT - KC * TOK:LEFT].rearrange("p (k t) -> p k t", k=KC)
        room = {"layer0": LEFT, "slots": LEFT - KC * TOK, "experts": LEFT - KC * TOK}
        used = {"layer0": SPLIT, "slots": SPLIT1, "experts": SPLIT}

        def carve(loop, *shape, parts=P, dt=F32):
            n = int(np.prod(shape))
            words = n if dt is F32 else (n + 1) // 2
            at = used[loop]
            used[loop] += words
            assert used[loop] <= room[loop], (loop, used[loop], room[loop])
            ap = work[0:parts, at:at + words]
            if dt is not F32:
                ap = ap.bitcast(dt)
            if len(shape) == 1:
                return ap
            names = "abcd"[:len(shape)]
            return ap.rearrange(f"p ({' '.join(names)}) -> p {' '.join(names)}",
                                **dict(zip(names, shape)))

        MASK = cols[:, 0:4]
        G_NORM = cols[:, 12:13]
        BQ, BK, BV, BO = (cols[:, 4 + 2 * i:6 + 2 * i] for i in range(4))

        x_first, x_loaded, w0_loaded = sem("x_first"), sem("x_loaded"), sem("w0_loaded")
        first_loaded, consts_loaded = sem("first_loaded"), sem("consts_loaded")
        f0_loaded = sem("f0_loaded")
        casts_done, bias_done, pow_rows = sem("casts_done"), sem("bias_done"), sem("pow_rows")
        s2_upper, s2_lower = sem("s2_upper"), sem("s2_lower")

        def part(at, *shape):
            n = int(np.prod(shape))
            names = "abcd"[:len(shape)]
            return split[:, at:at + n].rearrange(f"p ({' '.join(names)}) -> p {' '.join(names)}",
                                                 **dict(zip(names, shape)))

        GU = 2 * KC * P
        w_gu = part(0, 2, 2, GU)
        w_down = part(4 * GU, 2, 2, D)
        h_split = part(4 * GU + 4 * D, 2, 2, CH)
        x1_split = part(0, 2, KC, SEQ)
        w_qk = part(2 * KC * SEQ, 2, 2 * KC * DK)
        w_vg = part(2 * KC * SEQ + 4 * KC * DK, 2, 2 * KC * DK)
        at1 = 2 * KC * SEQ + 8 * KC * DK
        w_out = part(at1, 2, 2, D)
        og_split = part(at1 + 4 * D, 2, 2, SEQ)
        es_split = part(at1 + 4 * D + 4 * SEQ, 2, SEQ)
        x_split = part(4 * GU + 4 * D + 4 * CH, 2, KC, CH)
        TERMS = ((0, 0), (0, 1), (1, 0))

        class MoE:

            def __init__(self, loop, experts, top, tiles, sel, lower, per_token, hidden_room, before=None):
                self.loop, self.E, self.top, self.NT, self.sel, self.lower = loop, experts, top, tiles, sel, lower
                self.per_token = per_token
                made = iter(before.counts) if before else None
                self.counts = []

                def count(name, per):
                    was = next(made) if made else Count(sem("moe_" + name), 0)
                    self.counts.append(Count(was.sem, per, was.at(TURNS, 0) if made else 0))
                    return self.counts[-1]

                self.logits_done = count("logits_done", 1)
                self.tokens_done = count("tokens_done", 1)
                self.coef_turned = count("coef_turned", 1)
                self.gate_up_done = count("gate_up_done", tiles)
                self.coef_done = count("coef_done", tiles)
                self.down_done = count("down_done", tiles)
                self.delta_turned = count("delta_turned", 1)
                self.logits_copied = count("logits_copied", 1)
                self.tokens_copied = count("tokens_copied", 1)
                self.router_act = count("router_act", 1 if per_token == 1 else 2)
                self.coef_copied = count("coef_copied", 1)
                self.tanh_done = count("tanh_done", tiles)
                self.out_tanh = count("out_tanh", KC)
                self.router_step = count("router_step", 9 if per_token == 1 else 15)
                self.coef_ready = count("coef_ready", 1)
                self.half_step = count("half_step", 4 * tiles)
                self.x_upper, self.x_lower = count("x_upper", 1), count("x_lower", 1)
                self.gu_upper, self.gu_lower = count("gu_upper", tiles), count("gu_lower", tiles)
                self.down_upper, self.down_lower = count("down_upper", tiles), count("down_lower", tiles)
                self.hidden_ready = count("hidden_ready", tiles)
                self.out_step = count("out_step", KC)
                self.delta_ready = count("delta_ready", 1)
                self.x_ready = count("x_ready", 2)
                self.ties_step = count("ties_step", 2)
                self.split_step = count("split_step", 6)
                self.split_ready = count("split_ready", 1)
                E, c = experts, carve
                self.lg_sb = c(loop, CH)
                self.lg_tok = c(loop, CT, E * per_token)
                self.tok = [c(loop, CT, E) for _ in range(3)]
                self.cmp = [c(loop, CT, E, E) for _ in range(2)]
                self.small = c(loop, 4, CT)
                self.coef = c(loop, CT, E + 1)
                self.part = c(loop, CT, 3, E + 1)
                self.rest = c(loop, CT, E + 1)
                self.narrow = c(loop, CT * (E + 1) + 1, dt=BF16)[:, 0:CT * (E + 1)].rearrange(
                    "p (a b) -> p a b", a=CT)
                self.coefT = c(loop, CH, dt=BF16)
                if hidden_room is None:
                    hidden_room = c(loop, 5 + KC, CH)
                self.th = hidden_room[:, 0:2, :]
                self.half, self.both, self.hidden = (hidden_room[:, n, :] for n in (2, 3, 4))
                self.out_th = hidden_room[:, 5:5 + KC, :]
                self.delta = self.out_th

            def w(self, j):
                w0 = (W0F if self.loop == "layer0" else 0) + j * WT
                return weights[:, w0:w0 + WT]

            def pe_logits(self, pe, t, xT, rw, bank):
                n = self.E * self.per_token
                for kc in range(KC):
                    last = pe.matmul(ps[0:n, bank, :], rw[:, kc, :], xT[:, kc, :], start=kc == 0, stop=kc == KC - 1)
                last.then_inc(self.logits_done.sem, 1)

            def pe_gate_up(self, pe, t, j):
                b = j % 2
                if j == 0:
                    pe.wait_ge(self.x_lower.sem, self.x_lower.at(t, 1))
                pe.wait_ge(self.gu_lower.sem, self.gu_lower.at(t, j + 1))
                for which, bank in enumerate((2 + b, 4 + b)):
                    for n, (wp, xp) in enumerate(TERMS):
                        for kc in range(KC):
                            at = (which * KC + kc) * P
                            last = pe.matmul(ps[:, bank, :], w_gu[:, b, wp, at:at + P], x_split[:, xp, kc, :],
                                             start=n == 0 and kc == 0, stop=n == len(TERMS) - 1 and kc == KC - 1)
                last.then_inc(self.gate_up_done.sem, 1)

            def pe_router(self, pe, t, bank):
                n = self.E * self.per_token
                pe.wait_ge(self.logits_copied.sem, self.logits_copied.at(t, 1))
                for c in range(CT):
                    last = pe.matmul(ps[:, bank, c * n:(c + 1) * n], self.lg_sb[0:n, c * P:(c + 1) * P], ident[0:n, 0:n],
                                     start=True, stop=True)
                last.then_inc(self.tokens_done.sem, 1)

            def pe_coef(self, pe, t, bank):
                n = 3 * (self.E + 1)
                pe.wait_ge(self.split_ready.sem, self.split_ready.at(t, 1))
                for c in range(CT):
                    last = pe.matmul(ps[0:n, bank, c * P:(c + 1) * P],
                                     self.part[:, c, :, :].rearrange("p a b -> p (a b)"), ident[:, :],
                                     start=True, stop=True)
                last.then_inc(self.coef_turned.sem, 1)

            def pe_spread(self, pe, t, j):
                n = 3 * (self.E + 1)
                if j == 0:
                    pe.wait_ge(self.coef_copied.sem, self.coef_copied.at(t, 1))
                pe.matmul(ps[:, j % 2, :], self.sel[:, j * P:(j + 1) * P], self.coefT[0:n, :],
                          start=True, stop=True).then_inc(self.coef_done.sem, 1)

            def pe_down(self, pe, t, j):
                pe.wait_ge(self.down_lower.sem, self.down_lower.at(t, j + 1))
                pe.wait_ge(self.hidden_ready.sem, self.hidden_ready.at(t, j + 1))
                for mt in range(KC):
                    for n, (wp, hp) in enumerate(TERMS):
                        last = pe.matmul(ps[:, 6 + mt, :], w_down[:, j % 2, wp, mt * P:(mt + 1) * P], h_split[:, j % 2, hp, :],
                                         start=j == 0 and n == 0, stop=j == self.NT - 1 and n == len(TERMS) - 1)
                last.then_inc(self.down_done.sem, 1)

            def pe_tiles(self, pe, t, ahead, bank_read):
                for j in range(2, self.NT):
                    pe.wait_ge(self.half_step.sem, self.half_step.at(t, 4 * (j - 2) + 3))
                    ahead(j)
                    self.pe_gate_up(pe, t, j)
                    bank_read(j)
                    self.pe_spread(pe, t, j)
                    self.pe_down(pe, t, j - 2)
                self.pe_down(pe, t, self.NT - 2)

            def pe_delta(self, pe, t):
                pe.wait_ge(self.delta_ready.sem, self.delta_ready.at(t, 1))
                for c in range(CT):
                    for mt in range(KC):
                        last = pe.transpose(ps[:, c // 2, (c % 2) * D + mt * P:(c % 2) * D + (mt + 1) * P],
                                            self.delta[:, mt, c * P:(c + 1) * P], ident[:, :])
                last.then_inc(self.delta_turned.sem, 1)

            def act_split_x(self, act, t, norm):
                act.wait_ge(norm.xT_ready.sem, norm.xT_ready.at(t, KC))
                act.copy(x_split[:, 0, :, :], norm.xT).then_inc(self.x_upper.sem, 1)

            def act_upper_gu(self, act, t, j):
                if j >= 2:
                    act.wait_ge(self.gate_up_done.sem, self.gate_up_done.at(t, j - 1))
                act.copy(w_gu[:, j % 2, 0, :], self.w(j)[:, 0:GU]).then_inc(self.gu_upper.sem, 1)

            def act_upper_down(self, act, t, j):
                if j >= 2:
                    act.wait_ge(self.down_done.sem, self.down_done.at(t, j - 1))
                act.copy(w_down[:, j % 2, 0, :], self.w(j)[:, GU:WT]).then_inc(self.down_upper.sem, 1)

            def act_logits(self, act, t, bank):
                n = self.E * self.per_token
                act.wait_ge(self.logits_done.sem, self.logits_done.at(t, 1))
                act.copy(self.lg_sb[0:n, :], ps[0:n, bank, :]).then_inc(self.logits_copied.sem, 1)

            def act_tokens(self, act, t, bank):
                act.wait_ge(self.tokens_done.sem, self.tokens_done.at(t, 1))
                act.copy(self.lg_tok.rearrange("p c n -> p (c n)"), ps[:, bank, 0:CT * self.E * self.per_token])\
                   .then_inc(self.tokens_copied.sem, 1)
                if self.per_token == 2:
                    act.wait_ge(self.tokens_copied.sem, self.tokens_copied.at(t, 1))
                    act.activation(self.tok[0], self.lg_tok[:, :, 0:self.E], ACT.Tanh, scale=0.5).then_inc(self.router_act.sem, 1)

            def act_exp(self, act, t):
                if self.per_token == 2:
                    act.wait_ge(self.router_step.sem, self.router_step.at(t, 5))
                    act.activation(self.tok[1], self.tok[0], ACT.Exp, scale=0.5).then_inc(self.router_act.sem, 1)
                else:
                    act.wait_ge(self.router_step.sem, self.router_step.at(t, 2))
                    act.activation(self.tok[1], self.tok[0], ACT.Exp).then_inc(self.router_act.sem, 1)

            def act_coef(self, act, t, bank):
                n = 3 * (self.E + 1)
                act.wait_ge(self.coef_turned.sem, self.coef_turned.at(t, 1))
                act.copy(self.coefT[0:n, :], ps[0:n, bank, :]).then_inc(self.coef_copied.sem, 1)

            def act_tanh(self, act, t, j):
                act.wait_ge(self.gate_up_done.sem, self.gate_up_done.at(t, j + 1))
                if j >= 2:
                    act.wait_ge(self.hidden_ready.sem, self.hidden_ready.at(t, j - 1))
                act.activation(self.th[:, j % 2, :], ps[:, 2 + j % 2, :], ACT.Tanh, scale=0.5)\
                   .then_inc(self.tanh_done.sem, 1)

            def act_tiles(self, act, t, ahead, loaded):
                for j in range(2, self.NT):
                    ahead(j)
                    self.act_tanh(act, t, j)
                    if j + 2 < self.NT:
                        loaded(j + 2)
                        self.act_upper_gu(act, t, j + 2)
                    if j + 1 < self.NT:
                        self.act_upper_down(act, t, j)

            def act_out(self, act, t):
                act.wait_ge(self.down_done.sem, self.down_done.at(t, self.NT))
                for mt in range(KC):
                    act.activation(self.out_th[:, mt, :], ps[:, 6 + mt, :], ACT.Tanh, scale=0.5)\
                       .then_inc(self.out_tanh.sem, 1)

            def ties(self, eng, t, n):
                E = self.E
                gt, eq = self.cmp
                low = self.lower[:, :].rearrange("p (e f) -> p e f", e=E).unsqueeze(1).broadcast_to([P, CT, E, E])
                if n == 0:
                    eng.wait_ge(self.router_step.sem, self.router_step.at(t, 7 if self.per_token == 1 else 13))
                    eng.tensor_tensor(eq, eq, low, ALU.mult).then_inc(self.ties_step.sem, 1)
                else:
                    eng.wait_ge(self.ties_step.sem, self.ties_step.at(t, 1))
                    eng.tensor_tensor(gt, gt, eq, ALU.add).then_inc(self.ties_step.sem, 1)

            def split_coef(self, eng, t):
                n = [0]
                zero = zeros.unsqueeze(2).broadcast_to([P, CT, self.E + 1])

                def step(ins):
                    n[0] += 1
                    ins.then_inc(self.split_step.sem, 1)
                    eng.wait_ge(self.split_step.sem, self.split_step.at(t, n[0]))

                eng.wait_ge(self.coef_ready.sem, self.coef_ready.at(t, 1))
                step(eng.tensor_tensor(self.narrow, self.coef, zero, ALU.add))
                step(eng.tensor_tensor(self.part[:, :, 0, :], self.narrow, zero, ALU.add))
                step(eng.tensor_tensor(self.rest, self.coef, self.part[:, :, 0, :], ALU.subtract))
                step(eng.tensor_tensor(self.narrow, self.rest, zero, ALU.add))
                step(eng.tensor_tensor(self.part[:, :, 1, :], self.narrow, zero, ALU.add))
                step(eng.tensor_tensor(self.coef, self.rest, self.part[:, :, 1, :], ALU.subtract))
                eng.tensor_tensor(self.part[:, :, 2, :], self.coef, zero, ALU.add).then_inc(self.split_ready.sem, 1)
                assert n[0] == self.split_step.per

            def pool_lower_gu(self, pool, t, j):
                pool.wait_ge(self.gu_upper.sem, self.gu_upper.at(t, j + 1))
                pool.tensor_tensor(w_gu[:, j % 2, 1, :], self.w(j)[:, 0:GU], w_gu[:, j % 2, 0, :], ALU.subtract)\
                    .then_inc(self.gu_lower.sem, 1)

            def pool_lower_down(self, pool, t, j):
                pool.wait_ge(self.down_upper.sem, self.down_upper.at(t, j + 1))
                pool.tensor_tensor(w_down[:, j % 2, 1, :], self.w(j)[:, GU:WT], w_down[:, j % 2, 0, :], ALU.subtract)\
                    .then_inc(self.down_lower.sem, 1)

            def split_x(self, eng, t, norm):
                eng.wait_ge(self.x_upper.sem, self.x_upper.at(t, 1))
                eng.tensor_tensor(x_split[:, 1, :, :], norm.xT, x_split[:, 0, :, :], ALU.subtract).then_inc(self.x_lower.sem, 1)

            def pool_tiles(self, pool, t, ahead):
                for j in range(1, self.NT):
                    if j + 1 < self.NT:
                        self.pool_lower_gu(pool, t, j + 1)
                        self.pool_lower_down(pool, t, j)
                    ahead(j)

            def router_stepper(self, dve, t, done):
                n = [done]

                def step(ins):
                    n[0] += 1
                    ins.then_inc(self.router_step.sem, 1)
                    dve.wait_ge(self.router_step.sem, self.router_step.at(t, n[0]))

                return step

            def dve_router_scores(self, dve, t):
                step = self.router_stepper(dve, t, 0)
                a, b, c = self.tok
                lg = self.lg_tok
                E, mx = self.E, self.small[:, 0, :]
                dve.wait_ge(self.tokens_copied.sem, self.tokens_copied.at(t, 1))
                if self.per_token == 2:
                    dve.wait_ge(self.router_act.sem, self.router_act.at(t, 1))
                    step(dve.scalar_tensor_tensor(b, a, 1.0, lg[:, :, 0:E], ALU.add, ALU.mult))
                    step(dve.tensor_tensor(c, b, lg[:, :, E:2 * E], ALU.mult))
                    step(dve.scalar_tensor_tensor(b, c, -1.0, c, ALU.mult, ALU.max))
                    lg = b
                step(dve.tensor_reduce(mx, lg, AX.X, ALU.max))
                step(dve.tensor_tensor(a, lg, mx.unsqueeze(2).broadcast_to([P, CT, E]), ALU.subtract))

            def dve_router_probs(self, dve, t):
                step = self.router_stepper(dve, t, 2 if self.per_token == 1 else 5)
                a, b, c = self.tok
                row = [P, CT, self.E]
                sm, inv = self.small[:, 1, :], self.small[:, 2, :]
                dve.wait_ge(self.router_act.sem, self.router_act.at(t, self.per_token))
                step(dve.tensor_reduce(sm, b, AX.X, ALU.add))
                step(dve.reciprocal(inv, sm))
                step(dve.tensor_tensor(a, b, inv.unsqueeze(2).broadcast_to(row), ALU.mult))
                if self.per_token == 2:
                    step(dve.tensor_tensor(c, a, expert_rows[:, 1, :].unsqueeze(1).broadcast_to(row), ALU.add))
                    step(dve.tensor_tensor(b, a, expert_rows[:, 0, :].unsqueeze(1).broadcast_to(row), ALU.mult))
                    step(dve.tensor_scalar(a, b, 1.0, None, ALU.add))

            def dve_router_compare(self, dve, t, n):
                E = self.E
                step = self.router_stepper(dve, t, n + (5 if self.per_token == 1 else 11))
                cube = [P, CT, E, E]
                rank_of = self.tok[0 if self.per_token == 1 else 2]
                mine = rank_of.unsqueeze(3).broadcast_to(cube)
                other = rank_of.unsqueeze(2).broadcast_to(cube)
                step(dve.tensor_tensor(self.cmp[n], other, mine, (ALU.is_gt, ALU.is_equal)[n]))

            def dve_router_choose(self, dve, t):
                step = self.router_stepper(dve, t, 7 if self.per_token == 1 else 13)
                a, b, c = self.tok
                dve.wait_ge(self.ties_step.sem, self.ties_step.at(t, 2))
                dve.memset(self.coef[:, :, self.E:self.E + 1], 0.5)
                step(dve.tensor_reduce(b, self.cmp[0], AX.X, ALU.add))
                step(dve.tensor_scalar(c, b, self.top - 0.5, 0.5, ALU.is_lt, ALU.mult))
                dve.tensor_tensor(self.coef[:, :, 0:self.E], c, a, ALU.mult).then_inc(self.coef_ready.sem, 1)

            def dve_tiles(self, dve, t, ahead):
                for j in range(self.NT):
                    ahead(j)
                    b = j % 2
                    dve.wait_ge(self.tanh_done.sem, self.tanh_done.at(t, j + 1))
                    dve.scalar_tensor_tensor(self.half, self.th[:, b, :], 1.0, ps[:, 2 + b, :], ALU.add, ALU.mult)\
                       .then_inc(self.half_step.sem, 1)
                    dve.wait_ge(self.half_step.sem, self.half_step.at(t, 4 * j + 1))
                    dve.tensor_tensor(self.both, self.half, ps[:, 4 + b, :], ALU.mult).then_inc(self.half_step.sem, 1)
                    dve.wait_ge(self.half_step.sem, self.half_step.at(t, 4 * j + 2))
                    dve.wait_ge(self.coef_done.sem, self.coef_done.at(t, j + 1))
                    dve.tensor_tensor(self.hidden, self.both, ps[:, b, :], ALU.mult).then_inc(self.half_step.sem, 1)
                    dve.wait_ge(self.half_step.sem, self.half_step.at(t, 4 * j + 3))
                    if j >= 2:
                        dve.wait_ge(self.down_done.sem, self.down_done.at(t, j - 1))
                    dve.tensor_copy(h_split[:, b, 0, :], self.hidden).then_inc(self.half_step.sem, 1)
                    dve.wait_ge(self.half_step.sem, self.half_step.at(t, 4 * j + 4))
                    dve.tensor_tensor(h_split[:, b, 1, :], self.hidden, h_split[:, b, 0, :], ALU.subtract)\
                       .then_inc(self.hidden_ready.sem, 1)

            def dve_out(self, dve, t, sT, x_now):
                for mt in range(KC):
                    dve.wait_ge(self.out_tanh.sem, self.out_tanh.at(t, mt + 1))
                    dve.scalar_tensor_tensor(self.out_th[:, mt, :], self.out_th[:, mt, :], 1.0, ps[:, 6 + mt, :],
                                             ALU.add, ALU.mult).then_inc(self.out_step.sem, 1)
                dve.wait_ge(self.out_step.sem, self.out_step.at(t, KC))
                dve.tensor_tensor(self.delta, self.out_th, sT, ALU.mult).then_inc(self.delta_ready.sem, 1)
                dve.wait_ge(self.delta_turned.sem, self.delta_turned.at(t, 1))
                for c in range(CT // 2):
                    xs = x_now(2 * c, 2)
                    dve.scalar_tensor_tensor(xs, ps[:, c, :].rearrange("p (a d) -> p a d", a=2), 0.5, xs,
                                             ALU.mult, ALU.add).then_inc(self.x_ready.sem, 1)

        class Norm:
            def __init__(self, loop, tiles, banks, shared=False):
                self.T = tiles
                self.shared = shared
                self.banks = banks
                self.stats_done = count(loop + "_stats_done", tiles)
                self.mean_done = count(loop + "_mean_done", tiles)
                self.var_done = count(loop + "_var_done", 1)
                self.rstd_done = count(loop + "_rstd_done", 1)
                self.xn_ready = count(loop + "_xn_ready", tiles)
                self.xn_turned = count(loop + "_xn_turned", KC)
                self.xT_ready = count(loop + "_xT_ready", KC)
                self.stats = carve(loop, tiles, 6)
                self.mean = carve(loop, tiles, 2)
                self.var = carve(loop, tiles)
                self.rstd = carve(loop, tiles)
                self.xn = carve(loop, tiles, D)
                self.xT = carve(loop, KC, tiles * P)

            def dve_all(self, dve, t, x_now):
                self.dve_stats(dve, t, x_now)
                self.dve_scale(dve, t, x_now)

            def dve_stats(self, dve, t, x_now):
                T = self.T
                for c in range(T):
                    dve.bn_stats(self.stats[:, c, :], x_now(c, 1).rearrange("p a d -> p (a d)"))\
                       .then_inc(self.stats_done.sem, 1)
                dve.wait_ge(self.stats_done.sem, self.stats_done.at(t, T))
                dve.memset(self.rstd, 0.0)
                for c in range(T):
                    dve.bn_aggr(self.mean[:, c, :], self.stats[:, c, :]).then_inc(self.mean_done.sem, 1)

            def dve_scale(self, dve, t, x_now):
                dve.wait_ge(self.rstd_done.sem, self.rstd_done.at(t, 1))
                for c in range(self.T):
                    dve.tensor_scalar(self.xn[:, c, :], x_now(c, 1).rearrange("p a d -> p (a d)"),
                                      self.mean[:, c, 0:1], self.rstd[:, c:c + 1], ALU.subtract, ALU.mult)\
                       .then_inc(self.xn_ready.sem, 1)

            def pool_all(self, pool, t):
                T = self.T
                pool.wait_ge(self.mean_done.sem, self.mean_done.at(t, T))
                pool.tensor_tensor(self.var, self.mean[:, :, 1], eps_row[:, 0:T], ALU.add).then_inc(self.var_done.sem, 1)
                pool.wait_ge(self.var_done.sem, self.var_done.at(t, 1))
                pool.tensor_tensor(self.rstd, self.var, minus_half[:, 0:T], ALU.pow).then_inc(self.rstd_done.sem, 1)

            def pe_all(self, pe, t):
                for kc in range(KC):
                    self.pe_turn(pe, t, kc)

            def pe_turn(self, pe, t, kc, banks=None):
                if kc == 0:
                    pe.wait_ge(self.xn_ready.sem, self.xn_ready.at(t, self.T))
                for c in range(self.T):
                    last = pe.transpose((banks or self.banks)[kc][:, c * P:(c + 1) * P], self.xn[:, c, kc * P:(kc + 1) * P], ident[:, :])
                last.then_inc(self.xn_turned.sem, 1)

            def act_all(self, act, t):
                for kc in range(KC):
                    self.act_copy(act, t, kc)

            def act_copy(self, act, t, kc, banks=None):
                act.wait_ge(self.xn_turned.sem, self.xn_turned.at(t, KC if self.shared and not banks else kc + 1))
                act.copy(self.xT[:, kc, :], (banks or self.banks)[kc]).then_inc(self.xT_ready.sem, 1)

        eps_row, eps_dk, zeros = minus_half[:, 16:32], minus_half[:, 32:32 + ST * 2], minus_half[:, 48:49]

        norm0 = Norm("layer0", CT, [ps[:, kc, :] for kc in range(KC)])
        qT = carve("layer0", KC, CH)
        kTm = carve("layer0", HPQ, KC, CH)
        v0 = weights[:, W0V:W0V + HPQ * CT * D].rearrange("p (j c d) -> p j c d", j=HPQ, c=CT)
        prob = carve("layer0", RING, 2, BLK)
        probT = carve("layer0", 2, 2, BLK)
        nmax = carve("layer0", RING, ST, 2)
        total = carve("layer0", 2, ST, NH0)
        inv0 = carve("layer0", 2, ST * NH0)
        inv_wide = carve("layer0", 2, ST * NH0, HD0)
        oT0 = norm0.xn.rearrange("p c d -> p (c d)").rearrange("p (k t) -> p k t", k=KC)
        sT0 = qT
        moe0 = MoE("layer0", E0, K0, NT0, sel0, lower0, 1, kTm.rearrange("p j k t -> p (j k) t"))

        HEADS2 = 2 * SLOTS
        q_done, k_done, v_done = count("q_done", KC), count("k_done", KC), count("v_done", 2)
        qT_ready, v_ready = count("qT_ready", KC), count("v_ready", 2 * HPQ)
        keys_ready = count("keys_ready", KC * HPQ)
        scores_done = count("scores_done", HEADS2)
        max_ready = count("max_ready", 2 * SLOTS)
        exp_done = count("exp_done", HEADS2)
        prob_turned = count("prob_turned", HEADS2)
        probT_ready = count("probT_ready", HEADS2)
        pv_done = count("pv_done", HEADS2)
        inv_ready, wide_ready, inv_turned = count("inv_ready", 2), count("wide_ready", 2), count("inv_turned", 2)
        o_copied, o_ready, oT_ready = count("o_copied", 2), count("o_ready", 2), count("oT_ready", 2 * KC)
        out_done, sT_ready = count("out_done", KC), count("sT_ready", KC)

        def w0(which, kc, a, b):
            at = W0Q + (which * KC + kc) * D
            return weights[:, at + a:at + b]

        def pair_of(s):
            w = s % PAIRS
            return s // PAIRS, w // (PAIRS // 2), (w % (PAIRS // 2)) // 2, (2 * (w % 2), 2 * (w % 2) + 1)

        def head_of(n):
            bb, mt, j, rows = pair_of(n // 2)
            return mt * (NH0 // KC) + rows[n % 2] * HPQ + j

        def pe_queries_keys(pe, t, mt):
            xT = norm0.xT
            if mt == 0:
                pe.wait_ge(norm0.xT_ready.sem, norm0.xT_ready.at(t, KC))
            for which, bank, done in ((0, 2 + mt, q_done), (1, 4 + mt, k_done)):
                for kc in range(KC):
                    last = pe.matmul(ps[:, bank, :], w0(which, kc, mt * P, (mt + 1) * P), xT[:, kc, :],
                                     start=kc == 0, stop=kc == KC - 1)
                last.then_inc(done.sem, 1)

        def pe_values(pe, t, half):
            xT = norm0.xT
            for c in range(2 * half, 2 * half + 2):
                for kc in range(KC):
                    last = pe.matmul(ps[:, 6 + half, (c % 2) * D:(c % 2 + 1) * D], xT[:, kc, c * P:(c + 1) * P],
                                     w0(2, kc, 0, D), start=kc == 0, stop=kc == KC - 1)
            last.then_inc(v_done.sem, 1)

        def pe_layer0(pe, t):
            moe0.pe_logits(pe, t, norm0.xT, router0, 0)
            moe0.pe_router(pe, t, 1)

            def scores(s):
                bb, mt, j, rows = pair_of(s)
                q0 = bb * SEQ
                if s == 0:
                    pe.wait_ge(qT_ready.sem, qT_ready.at(t, KC))
                    pe.wait_ge(keys_ready.sem, keys_ready.at(t, HPQ))
                    pe.wait_ge(moe0.tokens_copied.sem, moe0.tokens_copied.at(t, 1))
                if s == PAIRS // 2:
                    pe.wait_ge(keys_ready.sem, keys_ready.at(t, KC * HPQ))
                if s >= 2:
                    pe.wait_ge(exp_done.sem, exp_done.at(t, 2 * s - 2))
                heads = [(2 * (s % 2) + hh, qT[32 * r:32 * r + 32, mt, :], kTm[32 * r:32 * r + 32, j, mt, :])
                         for hh, r in enumerate(rows)]
                for bank, q, k in heads:
                    pe.matmul(ps[:, bank, 0:SEQ], q[:, q0 + P:q0 + SEQ], k[:, q0:q0 + SEQ], start=True, stop=True)
                for bank, q, k in heads:
                    pe.matmul(ps[:, bank, SEQ:BLK], q[:, q0:q0 + P], k[:, q0:q0 + P], start=False, stop=True,
                              skip_group_check=True)
                for bank, q, k in heads:
                    pe.matmul(ps[:, bank, P:BLK], ident_b[:, :], causal_b[:, :], start=False, stop=True,
                              skip_group_check=True).then_inc(scores_done.sem, 1)

            def turn(s, hh):
                pe.wait_ge(exp_done.sem, exp_done.at(t, 2 * s + hh + 1))
                if s == 0 and hh == 0:
                    pe.wait_ge(keys_ready.sem, keys_ready.at(t, KC * HPQ))
                if s:
                    pe.wait_ge(probT_ready.sem, probT_ready.at(t, 2 * s - 1 + hh))
                for k in range(3):
                    last = pe.transpose(ps[:, 4 + hh, k * P:(k + 1) * P], prob[:, s % RING, hh, k * P:(k + 1) * P],
                                        ident[:, :])
                last.then_inc(prob_turned.sem, 1)

            def pv(s):
                bb, mt, j, rows = pair_of(s)
                if s == 0:
                    pe.wait_ge(v_ready.sem, v_ready.at(t, 2 * HPQ))
                at = mt * SEQ
                for hh in range(2):
                    pe.wait_ge(probT_ready.sem, probT_ready.at(t, 2 * s + hh + 1))
                    r = 32 * rows[hh]
                    pe.matmul(ps[r:r + 32, 6 + bb, at:at + SEQ], v0[:, j, ST * bb, mt * P + r:mt * P + r + 32],
                              probT[:, s % 2, hh, 0:SEQ], start=j == 0, stop=False, skip_group_check=True)
                for hh in range(2):
                    r = 32 * rows[hh]
                    pe.matmul(ps[r:r + 32, 6 + bb, at + P:at + SEQ], v0[:, j, ST * bb + 1, mt * P + r:mt * P + r + 32],
                              probT[:, s % 2, hh, SEQ:BLK], start=False, stop=j == HPQ - 1,
                              skip_group_check=True).then_inc(pv_done.sem, 1)

            def turn_inverse(bb):
                pe.wait_ge(wide_ready.sem, wide_ready.at(t, bb + 1))
                if bb == 0:
                    pe.wait_ge(exp_done.sem, exp_done.at(t, HEADS2))
                wide = inv_wide[:, bb, :, :].rearrange("p n e -> p (n e)")
                for mt in range(KC):
                    for c in range(ST):
                        last = pe.transpose(ps[:, bb, mt * SEQ + c * P:mt * SEQ + (c + 1) * P],
                                            wide[:, c * D + mt * P:c * D + (mt + 1) * P], ident[:, :])
                last.then_inc(inv_turned.sem, 1)

            for s in range(SLOTS + LAG + 1):
                if s < SLOTS:
                    scores(s)
                if s == 1:
                    pe_values(pe, t, 1)
                for hh in range(2):
                    if LAG <= s < SLOTS + LAG:
                        turn(s - LAG, hh)
                if s > LAG:
                    pv(s - LAG - 1)
            turn_inverse(0)
            turn_inverse(1)
            pe.wait_ge(o_copied.sem, o_copied.at(t, 1))
            moe0.pe_coef(pe, t, 6)
            moe0.pe_gate_up(pe, t, 0)
            moe0.pe_gate_up(pe, t, 1)
            pe.wait_ge(oT_ready.sem, oT_ready.at(t, 2 * KC))
            moe0.pe_spread(pe, t, 0)
            for mt in range(KC):
                for kc in range(KC):
                    last = pe.matmul(ps[:, 6 + mt, :], w0(3, kc, mt * P, (mt + 1) * P), oT0[:, kc, :],
                                     start=kc == 0, stop=kc == KC - 1)
                last.then_inc(out_done.sem, 1)
            moe0.pe_spread(pe, t, 1)

        def act_layer0(act, t):
            def queries(mt):
                act.wait_ge(q_done.sem, q_done.at(t, mt + 1))
                act.activation(qT[:, mt, :], ps[:, 2 + mt, :], ACT.Identity, bias=bqs[:, mt:mt + 1],
                               scale=HD0 ** -0.5).then_inc(qT_ready.sem, 1)

            queries(0)
            queries(1)
            moe0.act_logits(act, t, 0)
            moe0.act_tokens(act, t, 1)
            def values(c):
                act.wait_ge(v_done.sem, v_done.at(t, c + 1))
                for j in range(HPQ):
                    four = slice(j * HD0, (j + 1) * HD0)
                    act.copy(v0[:, j, 2 * c:2 * c + 2, :].rearrange("p a (g w) -> p (a g) w", w=HPQ * HD0)[:, :, four],
                             ps[:, 6 + c, :].rearrange("p (a w) -> p a w", w=HPQ * HD0)[:, :, four]).then_inc(v_ready.sem, 1)

            values(0)
            moe0.act_exp(act, t)

            def copy_out(bb):
                act.wait_ge(pv_done.sem, pv_done.at(t, NH0 * (bb + 1)))
                act.copy(oT0[:, :, bb * SEQ:(bb + 1) * SEQ], ps[:, 6 + bb, :].rearrange("p (k q) -> p k q", k=KC))\
                   .then_inc(o_copied.sem, 1)

            def add_bias(bb):
                act.wait_ge(o_ready.sem, o_ready.at(t, bb + 1))
                for mt in range(KC):
                    seq = oT0[:, mt, bb * SEQ:(bb + 1) * SEQ]
                    act.activation(seq, seq, ACT.Identity, bias=BV[:, mt:mt + 1]).then_inc(oT_ready.sem, 1)

            for s in range(SLOTS + LAG):
                bb = s // PAIRS
                if s < SLOTS:
                    if s >= RING:
                        act.wait_ge(prob_turned.sem, prob_turned.at(t, 2 * (s - RING) + 2))
                    act.wait_ge(max_ready.sem, max_ready.at(t, 2 * s + 2))
                    for hh in range(2):
                        h = head_of(2 * s + hh)
                        pr, sc = prob[:, s % RING, hh, :], ps[:, 2 * (s % 2) + hh, :]
                        act.activation(pr[:, 0:P], sc[:, SEQ:BLK], ACT.Exp, bias=nmax[:, s % RING, 0, hh:hh + 1],
                                       accum_out=total[:, bb, 0, h:h + 1])
                        act.activation(pr[:, P:BLK], sc[:, 0:SEQ], ACT.Exp, bias=nmax[:, s % RING, 1, hh:hh + 1],
                                       accum_out=total[:, bb, 1, h:h + 1]).then_inc(exp_done.sem, 1)
                if s == 1:
                    values(1)
                if s == 6:
                    moe0.act_split_x(act, t, norm0)
                if s == 8:
                    act.wait_ge(f0_loaded, 16)
                    moe0.act_upper_gu(act, t, 0)
                if s == 10:
                    moe0.act_upper_gu(act, t, 1)
                if s == 12:
                    moe0.act_upper_down(act, t, 0)
                if s == PAIRS + LAG + 2:
                    copy_out(0)
            copy_out(1)
            add_bias(0)
            add_bias(1)
            moe0.act_coef(act, t, 6)
            moe0.act_tanh(act, t, 0)
            moe0.act_upper_gu(act, t, 2)
            moe0.act_tanh(act, t, 1)
            for mt in range(KC):
                act.wait_ge(out_done.sem, out_done.at(t, mt + 1))
                act.activation(sT0[:, mt, :], ps[:, 6 + mt, :], ACT.Identity, bias=BO[:, mt:mt + 1]).then_inc(sT_ready.sem, 1)

        def dve_layer0(dve, t):
            for mt in range(KC):
                dve.wait_ge(k_done.sem, k_done.at(t, mt + 1))
                for j in range(HPQ):
                    dve.tensor_scalar(kTm[:, j, mt, :], ps[:, 4 + mt, :], BK[:, mt:mt + 1], MASK[:, j:j + 1], ALU.add, ALU.mult)\
                       .then_inc(keys_ready.sem, 1)
            moe0.dve_router_scores(dve, t)

            def copy_probs(s):
                for hh in range(2):
                    dve.wait_ge(prob_turned.sem, prob_turned.at(t, 2 * s + hh + 1))
                    if s >= 2:
                        dve.wait_ge(pv_done.sem, pv_done.at(t, 2 * (s - 2) + hh + 1))
                    dve.tensor_copy(probT[:, s % 2, hh, :], ps[:, 4 + hh, 0:BLK]).then_inc(probT_ready.sem, 1)

            def inverse(bb):
                dve.wait_ge(exp_done.sem, exp_done.at(t, NH0 * (bb + 1)))
                dve.reciprocal(inv0[:, bb, :], total[:, bb, :, :].rearrange("p c h -> p (c h)")).then_inc(inv_ready.sem, 1)
                dve.wait_ge(inv_ready.sem, inv_ready.at(t, bb + 1))
                dve.tensor_copy(inv_wide[:, bb, :, :], inv0[:, bb, :].unsqueeze(2).broadcast_to([P, ST * NH0, HD0]))\
                   .then_inc(wide_ready.sem, 1)

            def normalise(bb):
                dve.wait_ge(inv_turned.sem, inv_turned.at(t, bb + 1))
                dve.wait_ge(o_copied.sem, o_copied.at(t, bb + 1))
                seq = oT0[:, :, bb * SEQ:(bb + 1) * SEQ]
                dve.tensor_tensor(seq, seq,
                                  ps[:, bb, :].rearrange("p (k q) -> p k q", k=KC), ALU.mult).then_inc(o_ready.sem, 1)

            for s in range(SLOTS + LAG):
                if s < SLOTS:
                    b = 2 * (s % 2)
                    sc = ps[:, b:b + 2, :]
                    dve.wait_ge(scores_done.sem, scores_done.at(t, 2 * s + 2))
                    dve.tensor_reduce(nmax[:, s % RING, 0, :], sc[:, :, SEQ:BLK], AX.X, ALU.max, negate=True)\
                       .then_inc(max_ready.sem, 1)
                    dve.tensor_reduce(nmax[:, s % RING, 1, :], sc[:, :, 0:SEQ], AX.X, ALU.max, negate=True)\
                       .then_inc(max_ready.sem, 1)
                if s >= LAG:
                    copy_probs(s - LAG)
                if s == 1:
                    moe0.dve_router_probs(dve, t)
                if s == 2:
                    moe0.dve_router_compare(dve, t, 0)
                    moe0.dve_router_compare(dve, t, 1)
                if s == 5:
                    moe0.dve_router_choose(dve, t)
                if s == PAIRS + LAG:
                    inverse(0)
                if s == SLOTS:
                    inverse(1)
            normalise(0)
            normalise(1)

        s_clip = carve("slots", 2 * SEQ)
        es_both = carve("slots", 2, 2 * SEQ)
        es = es_both[:, :, 0:SEQ].rearrange("p b (c n) -> p b c n", c=ST)
        esT = es_both[:, :, SEQ:2 * SEQ]
        enz = carve("slots", 2, ST, P)
        assert used["slots"] >= SPLIT
        norm1 = Norm("slots", ST, [ps[:, 2, kc * SEQ:(kc + 1) * SEQ] for kc in range(KC)], shared=True)
        RAW_AT = used["slots"]
        raw = carve("slots", 2, 2, SEQ)
        rot_s = carve("slots", 2, 2, SEQ)
        qk = carve("slots", 4, 2, SEQ)
        v1 = carve("slots", 4, ST, DK)
        gate = carve("slots", 4, ST, DK)
        aT = carve("slots", 2, BLK)
        w2T = carve("slots", 2, BLK)
        okz = carve("slots", ST, 2, M)
        oks = okp = okz
        qe = carve("slots", ST, P)
        qeT = carve("slots", SEQ)
        okmax, oksum, rs, ssq, ms, rstd1, comb = (carve("slots", ST, 2) for _ in range(7))
        og = carve("slots", 2, ST, DK)
        squares = og

        s1_done, s_done, cum_done = count("s1_done", 1), count("s_done", PAIR1), count("cum_done", PAIR1)
        qk_done, vg_done, a_done, ok_done = count("qk_done", NH1), count("vg_done", NH1), count("a_done", NH1), count("ok_done", PAIR1)
        qe_turned, w2_done, o_done = count("qe_turned", PAIR1), count("w2_done", NH1), count("o_done", NH1)
        og_turned, out1_done = count("og_turned", PAIR1), count("out1_done", 1)
        s1_upper, es_ready = count("s1_upper", 1), count("es_ready", PAIR1)
        raw_ready, v1_ready, gate_tanh = count("raw_ready", NH1), count("v1_ready", NH1), count("gate_tanh", NH1)
        okp_ready, qeT_ready, ssq_ready = count("okp_ready", PAIR1), count("qeT_ready", PAIR1), count("ssq_ready", NH1)
        ogT_ready, sT1_ready = count("ogT_ready", PAIR1), count("sT1_ready", 1)
        s1_ready, s_clipped, enz_ready = count("s1_ready", 1), count("s_clipped", PAIR1), count("enz_ready", PAIR1)
        aT_ready, w2T_ready, rot_s_ready = count("aT_ready", NH1), count("w2T_ready", NH1), count("rot_s_ready", NH1)
        ok_step, oks_ready, sum_step, rs_ready = count("ok_step", 2 * PAIR1), count("oks_ready", PAIR1), count("sum_step", PAIR1), count("rs_ready", PAIR1)
        gate_ready, og_ready = count("gate_ready", NH1), count("og_ready", PAIR1)
        es_lower = count("es_lower", PAIR1)
        rot_c_ready, qk_ready, qe_ready = count("rot_c_ready", NH1), count("qk_ready", NH1), count("qe_ready", PAIR1)
        x1_upper, x1_lower = count("x1_upper", 1), count("x1_lower", 1)
        qk_upper, qk_lower, vg_upper, vg_lower = (count(n, NH1) for n in ("qk_upper", "qk_lower", "vg_upper", "vg_lower"))
        og_upper, wo_upper, wo_lower = count("og_upper", PAIR1), count("wo_upper", PAIR1), count("wo_lower", PAIR1)
        rms_step, comb_ready = count("rms_step", 2 * PAIR1), count("comb_ready", PAIR1)

        LAST = PAIR1 - 1

        def w1(h, at, n):
            at += w1_head(h % NH1)
            return weights[:, at:at + n]

        SEQ_END = BATCH - 1
        RANK_BANK = 4
        spread_banks = [ps[:, kc, 0:SEQ] for kc in range(KC)]
        idle_banks = [ps[:, 2, :], ps[:, 3, :]]

        def steps(pp, part):
            stays = part != "last"
            return stays or pp < LAST - 1, stays or pp < LAST, pp >= 0 and (stays or pp <= LAST), pp >= 1

        def slots_over(eng):
            eng.wait_ge(sT1_ready.sem, sT1_ready.at(SEQ_END, 1))

        def pe_slots(pe, t, part):
            xT = norm1.xT

            def slot_rank(turn, bank=0):
                pe.wait_ge(norm1.xT_ready.sem, norm1.xT_ready.at(turn, KC))
                for kc in range(KC):
                    last = pe.matmul(ps[0:RS, bank, 0:SEQ], s1w[:, kc, :], xT[:, kc, :], start=kc == 0, stop=kc == KC - 1)
                last.then_inc(s1_done.sem, 1)

            def slot_scores(pp):
                if pp % PAIR1 == 0:
                    pe.wait_ge(s1_ready.sem, s1_ready.at(t, pp // PAIR1 + 1))
                if pp:
                    pe.wait_ge(enz_ready.sem, enz_ready.at(t, pp))
                heads = s2_split[:, pp % PAIR1 * P:(pp % PAIR1 + 1) * P]
                for c in range(ST):
                    pe.matmul(ps[:, 0, c * P:(c + 1) * P], s1_split[:, c * P:(c + 1) * P], heads, start=True, stop=True)
                pe.matmul(ps[:, 0, SEQ:2 * SEQ], heads, s1_split[:, :], start=True, stop=True).then_inc(s_done.sem, 1)

            def running_sum(pp):
                pe.wait_ge(es_lower.sem, es_lower.at(t, pp + 1))
                for n in range(2):
                    pe.matmul(ps[:, 0, SEQ:2 * SEQ], tri_r[:, :], es_split[:, n, :], start=n == 0, stop=False,
                              skip_group_check=True)
                for n in range(2):
                    last = pe.matmul(ps[:, 0, SEQ + P:2 * SEQ], ones_r[:, :], es_split[:, n, 0:P], start=False, stop=n == 1,
                                     skip_group_check=True)
                last.then_inc(cum_done.sem, 1)

            def queries_keys(h):
                if h % NH1 == 0:
                    pe.wait_ge(x1_lower.sem, x1_lower.at(t, h // NH1 + 1))
                pe.wait_ge(qk_lower.sem, qk_lower.at(t, h + 1))
                if h:
                    pe.wait_ge(raw_ready.sem, raw_ready.at(t, h))
                for which in range(2):
                    for n, (wp, xp) in enumerate(TERMS):
                        for kc in range(KC):
                            at = (which * KC + kc) * P
                            last = pe.matmul(ps[:, 2, which * SEQ:(which + 1) * SEQ], w_qk[:, wp, at:at + P],
                                             x1_split[:, xp, kc, :], start=n == 0 and kc == 0,
                                             stop=n == len(TERMS) - 1 and kc == KC - 1)
                last.then_inc(qk_done.sem, 1)

            def values_gates(h, tiles=range(ST)):
                if 0 in tiles:
                    pe.wait_ge(vg_lower.sem, vg_lower.at(t, h + 1))
                    if h:
                        pe.wait_ge(gate_ready.sem, gate_ready.at(t, h))
                for c in tiles:
                    for n, (wp, xp) in enumerate(TERMS):
                        for kc in range(KC):
                            last = pe.matmul(ps[:, 3, c * 2 * DK:(c + 1) * 2 * DK], x1_split[:, xp, kc, c * P:(c + 1) * P],
                                             w_vg[:, wp, kc * 2 * DK:(kc + 1) * 2 * DK], start=n == 0 and kc == 0,
                                             stop=n == len(TERMS) - 1 and kc == KC - 1)
                if ST - 1 in tiles:
                    last.then_inc(vg_done.sem, 1)

            def causal_blocks(bank, key, query, done):
                pe.matmul(ps[:, bank, 0:SEQ], key[:, 0:P], query[:, 0:SEQ], start=True, stop=True)
                pe.matmul(ps[:, bank, SEQ:BLK], key[:, P:SEQ], query[:, P:SEQ], start=True, stop=True)\
                  .then_inc(done.sem, 1)

            def over_keys(outs, left, rhs):
                pe.matmul(outs[0], left[:, 0:P], rhs[0], start=True, stop=True)
                pe.matmul(outs[1], left[:, P:SEQ], rhs[0], start=True, stop=False)
                return pe.matmul(outs[1], left[:, SEQ:BLK], rhs[1], start=False, stop=True)

            def scores1(h):
                pe.wait_ge(qk_ready.sem, qk_ready.at(t, h + 1))
                if h >= 2:
                    pe.wait_ge(w2T_ready.sem, w2T_ready.at(t, h - 1))
                causal_blocks(4 + h % 2, qk[:, h % 4, 1, :], qk[:, h % 4, 0, :], a_done)

            def slots_read(pp):
                for hh in range(2):
                    h = 2 * pp + hh
                    pe.wait_ge(aT_ready.sem, aT_ready.at(t, h + 1))
                    last = over_keys([ps[:, 4 + hh, BLK + c * M:BLK + (c + 1) * M] for c in range(ST)], aT[:, hh, :],
                                     [es[:, pp % 2, c, hh * M:(hh + 1) * M] for c in range(ST)])
                last.then_inc(ok_done.sem, 1)

            def turn_qe(pp):
                pe.wait_ge(qe_ready.sem, qe_ready.at(t, pp + 1))
                for c in range(ST):
                    last = pe.transpose(ps[:, 1, c * P:(c + 1) * P], qe[:, c, :], ident[:, :])
                last.then_inc(qe_turned.sem, 1)

            def slots_write(h):
                a = slice(M * (h % 2), M * (h % 2) + M)
                causal_blocks(4 + h % 2, esT[a, (h // 2) % 2, :], qeT[a, :], w2_done)

            def mix_values(h):
                pe.wait_ge(w2T_ready.sem, w2T_ready.at(t, h + 1))
                at = (h % 2) * SEQ
                if h % 2 == 0 and h:
                    pe.wait_ge(og_ready.sem, og_ready.at(t, h // 2))
                over_keys([ps[:, 6, at + c * P:at + (c + 1) * P] for c in range(ST)], w2T[:, h % 2, :],
                          [v1[:, h % 4, c, :] for c in range(ST)]).then_inc(o_done.sem, 1)

            def turn_og(pp):
                pe.wait_ge(og_ready.sem, og_ready.at(t, pp + 1))
                for hh in range(2):
                    for c in range(ST):
                        last = pe.transpose(ps[:, 1, hh * SEQ + c * P:hh * SEQ + (c + 1) * P], og[:, hh, c, :], ident[:, :])
                last.then_inc(og_turned.sem, 1)

            def project(pp):
                pe.wait_ge(wo_lower.sem, wo_lower.at(t, pp + 1))
                pe.wait_ge(ogT_ready.sem, ogT_ready.at(t, pp + 1))
                for hh in range(2):
                    h = 2 * pp + hh
                    for mt in range(KC):
                        for n, (wp, gp) in enumerate(TERMS):
                            last = pe.matmul(ps[:, 7, mt * SEQ:(mt + 1) * SEQ], w_out[:, wp, hh, mt * P:(mt + 1) * P],
                                             og_split[:, gp, hh, :], start=h == 0 and mt == 0 and n == 0,
                                             stop=h == NH1 - 1 and n == len(TERMS) - 1, skip_group_check=True)
                if pp == PAIR1 - 1:
                    last.then_inc(out1_done.sem, 1)

            def pair(pp):
                _, ahead, now, behind = steps(pp, part)
                if pp == LAST and ahead:
                    pe.wait_ge(enz_ready.sem, enz_ready.at(t, PAIR1))
                    slot_rank(t + 1)
                if now:
                    scores1(2 * pp)
                    scores1(2 * pp + 1)
                if ahead:
                    slot_scores(pp + 1)
                    queries_keys(2 * pp + 2)
                if now:
                    slots_read(pp)
                if ahead:
                    values_gates(2 * pp + 2)
                if not now:
                    pe.wait_ge(norm2.xT_ready.sem, norm2.xT_ready.at(0, KC))
                    moe1.pe_logits(pe, 0, norm2.xT, router1, 0)
                    moe1.pe_router(pe, 0, 0)
                if behind:
                    turn_og(pp - 1)
                if ahead:
                    queries_keys(2 * pp + 3)
                    running_sum(pp + 1)
                if behind:
                    project(pp - 1)
                if now:
                    turn_qe(pp)
                if ahead:
                    values_gates(2 * pp + 3, (0,))
                if now:
                    pe.wait_ge(qeT_ready.sem, qeT_ready.at(t, pp + 1))
                    slots_write(2 * pp)
                    slots_write(2 * pp + 1)
                if ahead:
                    values_gates(2 * pp + 3, (1,))
                if pp == LAST - 1 and part != "last":
                    pe.wait_ge(raw_ready.sem, raw_ready.at(t, NH1))
                    norm1.pe_all(pe, t + 1)
                if pp == LAST and not ahead:
                    for kc in range(KC):
                        norm2.pe_turn(pe, 0, kc, idle_banks)
                if now:
                    mix_values(2 * pp)
                    mix_values(2 * pp + 1)

            if part == "before":
                slot_rank(0, RANK_BANK)
                queries_keys(0)
                return
            if part == "first":
                pe.wait_ge(s2_lower, 1)
                slot_scores(0)
                values_gates(0)
                queries_keys(1)
                running_sum(0)
                values_gates(1)
                pair(0)
                return
            for pp in range(1, PAIR1 + 1):
                pair(pp)

        def act_slots(act, t, part):
            def next_tokens(turn):
                if part != "before":
                    norm1.act_all(act, turn)
                act.wait_ge(norm1.xT_ready.sem, norm1.xT_ready.at(turn, KC))
                act.copy(x1_split[:, 0, :, :], norm1.xT).then_inc(x1_upper.sem, 1)

            def slot_rank(turn, bank=0):
                act.wait_ge(s1_done.sem, s1_done.at(turn, 1))
                for g in range(2):
                    act.copy(s1_split[g * RG:g * RG + R1, :], ps[g * RG:g * RG + R1, bank, 0:SEQ])
                act.copy(s1_split[2 * RG:RS, :], ps[2 * RG:RS, bank, 0:SEQ]).then_inc(s1_upper.sem, 1)

            def exp_scores(pp):
                act.wait_ge(s_clipped.sem, s_clipped.at(t, pp + 1))
                act.activation(es_both[:, pp % 2, :], s_clip, ACT.Exp)
                act.activation(es_split[:, 0, :], s_clip[:, 0:SEQ], ACT.Exp).then_inc(es_ready.sem, 1)

            def upper_qk(h):
                if h % 2 == 0:
                    act.wait_ge(w1_loaded[h // 2 % PAIR1], 16)
                act.copy(w_qk[:, 0, :], w1(h, 0, 2 * KC * DK)).then_inc(qk_upper.sem, 1)

            def upper_wo(pp):
                if pp % PAIR1 == 0:
                    act.wait_ge(wo1_loaded, 16)
                n = pp % PAIR1
                act.activation(w_out[:, 0, :, :].rearrange("p a b -> p (a b)"), weights[:, W1O + 2 * n * D:W1O + 2 * (n + 1) * D],
                               ACT.Copy, scale=g_half[:, 0:1]).then_inc(wo_upper.sem, 1)

            def upper_vg(h):
                if h % 2 == 0:
                    act.wait_ge(w1_loaded[h // 2 % PAIR1], 16)
                act.copy(w_vg[:, 0, :], w1(h, 2 * KC * DK, 2 * KC * DK)).then_inc(vg_upper.sem, 1)

            def copy_qk(h):
                act.wait_ge(qk_done.sem, qk_done.at(t, h + 1))
                act.copy(raw[:, h % 2, :, :].rearrange("p a b -> p (a b)"), ps[:, 2, :]).then_inc(raw_ready.sem, 1)

            def gates(h):
                act.wait_ge(vg_done.sem, vg_done.at(t, h + 1))
                vg = ps[:, 3, :].rearrange("p (c w d) -> p c w d", c=ST, w=2)
                act.copy(v1[:, h % 4, :, :], vg[:, :, 0, :]).then_inc(v1_ready.sem, 1)
                if h >= 4 and h % 2 == 0:
                    act.wait_ge(og_ready.sem, og_ready.at(t, h // 2 - 1))
                act.activation(gate[:, h % 4, :, :], vg[:, :, 1, :], ACT.Tanh, scale=0.5).then_inc(gate_tanh.sem, 1)

            if part == "before":
                act.wait_ge(moe0.gate_up_done.sem, moe0.gate_up_done.at(TURNS - 1, NT0))
                next_tokens(0)
                upper_qk(0)
                return
            for pp in (-1, 0) if part == "first" else range(1, PAIR1 + 1):
                further, ahead, now, behind = steps(pp, part)
                if pp == LAST and ahead:
                    slot_rank(t + 1)
                elif pp < 0:
                    slot_rank(0, RANK_BANK)
                    upper_vg(0)
                if behind:
                    act.wait_ge(rs_ready.sem, rs_ready.at(t, pp))
                    act.wait_ge(o_done.sem, o_done.at(t, 2 * pp))
                    for hh in range(2):
                        for c in range(ST):
                            at = hh * SEQ + c * P
                            last = act.activation(squares[:, hh, c, :], ps[:, 6, at:at + P], ACT.Square, scale=rs[:, c, hh:hh + 1],
                                                  accum_out=ssq[:, c, hh:hh + 1])
                        last.then_inc(ssq_ready.sem, 1)
                if ahead:
                    exp_scores(pp + 1)
                    copy_qk(2 * pp + 2)
                    upper_qk(2 * pp + 3)
                if now:
                    act.wait_ge(oks_ready.sem, oks_ready.at(t, pp + 1))
                    act.activation(okp, oks, ACT.Exp).then_inc(okp_ready.sem, 1)
                if pp > LAST and not now:
                    moe1.act_logits(act, 0, 0)
                    moe1.act_tokens(act, 0, 0)
                if behind:
                    act.wait_ge(og_turned.sem, og_turned.at(t, pp))
                    act.copy(og_split[:, 0, :, :].rearrange("p a b -> p (a b)"), ps[:, 1, :]).then_inc(og_upper.sem, 1)
                if pp > LAST and not now:
                    moe1.act_exp(act, 0)
                    act.wait_ge(f1_loaded[0], 16)
                    moe1.act_upper_gu(act, 0, 0)
                    act.wait_ge(f1_loaded[1], 16)
                    moe1.act_upper_gu(act, 0, 1)
                    moe1.act_upper_down(act, 0, 0)
                if ahead:
                    gates(2 * pp + 2)
                    upper_vg(2 * pp + 3)
                    copy_qk(2 * pp + 3)
                if further:
                    upper_qk(2 * pp + 4)
                if now:
                    act.wait_ge(qe_turned.sem, qe_turned.at(t, pp + 1))
                    act.copy(qeT, ps[:, 1, 0:SEQ]).then_inc(qeT_ready.sem, 1)
                    upper_wo(pp)
                if pp == LAST and not ahead:
                    for kc in range(KC):
                        norm2.act_copy(act, 0, kc, idle_banks)
                    moe1.act_split_x(act, 0, norm2)
                if ahead:
                    gates(2 * pp + 3)
                if pp == LAST - 1 and part != "last":
                    next_tokens(t + 1)
                if further:
                    upper_vg(2 * pp + 4)
            if part == "first":
                return
            act.wait_ge(out1_done.sem, out1_done.at(t, 1))
            act.copy(sT1[:, :, bass.ds(t * SEQ, SEQ)], ps[:, 7, :].rearrange("p (k n) -> p k n", k=KC))\
               .then_inc(sT1_ready.sem, 1)

        def dve_slots(dve, t, x_next, part):
            def first_tokens(c, n):
                return x_res[:, c:c + n, :]

            def rotate(h):
                dve.wait_ge(raw_ready.sem, raw_ready.at(t, h + 1))
                H = DK // 2
                for dst, src in ((0, H), (H, 0)):
                    last = dve.tensor_tensor(rot_s[dst:dst + H, h % 2, :, :], raw[src:src + H, h % 2, :, :],
                                             rope[src:src + H, 1, :].unsqueeze(1).broadcast_to([H, 2, SEQ]), ALU.mult)
                last.then_inc(rot_s_ready.sem, 1)

            def gates(h):
                dve.wait_ge(gate_tanh.sem, gate_tanh.at(t, h + 1))
                g = ps[:, 3, :].rearrange("p (c w d) -> p c w d", c=ST, w=2)[:, :, 1, :]
                dve.scalar_tensor_tensor(gate[:, h % 4, :, :], gate[:, h % 4, :, :], 1.0, g, ALU.add, ALU.mult)\
                   .then_inc(gate_ready.sem, 1)

            def keep(h, src_done, dst, mask, ready):
                dve.wait_ge(src_done.sem, src_done.at(t, h + 1))
                dve.tensor_tensor(dst[:, h % 2, :], ps[:, 4 + h % 2, 0:BLK], mask[:, :], ALU.mult).then_inc(ready.sem, 1)

            def lower_vg(h):
                dve.wait_ge(vg_upper.sem, vg_upper.at(t, h + 1))
                dve.tensor_tensor(w_vg[:, 1, :], w1(h, 2 * KC * DK, 2 * KC * DK), w_vg[:, 0, :], ALU.subtract)\
                   .then_inc(vg_lower.sem, 1)

            def lower_og(pp):
                dve.wait_ge(og_upper.sem, og_upper.at(t, pp + 1))
                dve.tensor_tensor(og_split[:, 1, :, :].rearrange("p a b -> p (a b)"), ps[:, 1, :],
                                  og_split[:, 0, :, :].rearrange("p a b -> p (a b)"), ALU.subtract).then_inc(ogT_ready.sem, 1)

            def lower_wo(pp):
                n = pp % PAIR1
                dve.wait_ge(wo_upper.sem, wo_upper.at(t, pp + 1))
                dve.scalar_tensor_tensor(w_out[:, 1, :, :].rearrange("p a b -> p (a b)"),
                                         weights[:, W1O + 2 * n * D:W1O + 2 * (n + 1) * D], g_half[:, 0:1],
                                         w_out[:, 0, :, :].rearrange("p a b -> p (a b)"), ALU.mult, ALU.subtract)\
                   .then_inc(wo_lower.sem, 1)

            def lower_x(turn):
                dve.wait_ge(x1_upper.sem, x1_upper.at(turn, 1))
                dve.tensor_tensor(x1_split[:, 1, :, :], norm1.xT, x1_split[:, 0, :, :], ALU.subtract).then_inc(x1_lower.sem, 1)

            def lower_s1(turn, bank=0):
                dve.wait_ge(s1_upper.sem, s1_upper.at(turn, 1))
                rows = slice(2 * RG, RS)
                dve.tensor_tensor(s1_split[rows, :], ps[rows, bank, 0:SEQ], s1_split[rows, :], ALU.subtract).then_inc(s1_ready.sem, 1)

            if part == "before":
                lower_x(0)
                return
            if part == "first":
                lower_s1(0, RANK_BANK)
                lower_vg(0)

            def gated(pp):
                dve.wait_ge(comb_ready.sem, comb_ready.at(t, pp + 1))
                for hh in range(2):
                    for c in range(ST):
                        at = hh * SEQ + c * P
                        last = dve.scalar_tensor_tensor(og[:, hh, c, :], ps[:, 6, at:at + P], comb[:, c, hh:hh + 1],
                                                        gate[:, (2 * pp + hh) % 4, c, :], ALU.mult, ALU.mult)
                last.then_inc(og_ready.sem, 1)

            for pp in (-1, 0) if part == "first" else range(1, PAIR1 + 1):
                further, ahead, now, behind = steps(pp, part)
                n = pp + 1
                if pp == LAST and ahead:
                    lower_s1(t + 1)
                if now:
                    keep(2 * pp, a_done, aT, keep_a, aT_ready)
                    keep(2 * pp + 1, a_done, aT, keep_a, aT_ready)
                if ahead:
                    dve.wait_ge(s_done.sem, s_done.at(t, n + 1))
                    dve.tensor_scalar(s_clip, ps[:, 0, :], -CLAMP, CLAMP, ALU.max, ALU.min).then_inc(s_clipped.sem, 1)
                if behind:
                    lower_wo(pp - 1)
                    gated(pp - 1)
                if now:
                    dve.wait_ge(ok_done.sem, ok_done.at(t, pp + 1))
                    for hh in range(2):
                        last = dve.tensor_tensor(okz[:, :, hh, :], ps[:, 4 + hh, BLK:512].rearrange("p (c m) -> p c m", c=ST),
                                                 enz[:, pp % 2, :, hh * M:(hh + 1) * M], ALU.mult)
                    last.then_inc(ok_step.sem, 1)
                    dve.wait_ge(ok_step.sem, ok_step.at(t, 2 * pp + 1))
                    dve.tensor_reduce(okmax, okz, AX.X, ALU.max).then_inc(ok_step.sem, 1)
                    dve.wait_ge(ok_step.sem, ok_step.at(t, 2 * pp + 2))
                    flat = "p c h m -> p (c h) m"
                    dve.tensor_tensor(oks.rearrange(flat), okz.rearrange(flat),
                                      okmax.rearrange("p c h -> p (c h)").unsqueeze(2).broadcast_to([P, ST * 2, M]), ALU.subtract)\
                       .then_inc(oks_ready.sem, 1)
                if pp > LAST and not now:
                    moe1.dve_router_scores(dve, 0)
                if ahead:
                    rotate(2 * n)
                if behind:
                    lower_og(pp - 1)
                if ahead:
                    gates(2 * n)
                    lower_vg(2 * n + 1)
                    rotate(2 * n + 1)
                if pp == LAST and not ahead:
                    norm2.dve_stats(dve, 0, first_tokens)
                if now:
                    dve.wait_ge(okp_ready.sem, okp_ready.at(t, pp + 1))
                    dve.tensor_reduce(oksum, okp, AX.X, ALU.add).then_inc(sum_step.sem, 1)
                    dve.wait_ge(sum_step.sem, sum_step.at(t, pp + 1))
                    dve.reciprocal(rs, oksum).then_inc(rs_ready.sem, 1)
                if pp == LAST and not ahead:
                    norm2.dve_scale(dve, 0, first_tokens)
                if now:
                    keep(2 * pp, w2_done, w2T, keep_w, w2T_ready)
                    keep(2 * pp + 1, w2_done, w2T, keep_w, w2T_ready)
                if ahead:
                    dve.wait_ge(cum_done.sem, cum_done.at(t, n + 1))
                    dve.reciprocal(enz[:, n % 2, :, :].rearrange("p c n -> p (c n)"), ps[:, 0, SEQ:2 * SEQ])\
                       .then_inc(enz_ready.sem, 1)
                if part != "last":
                    if pp == LAST - 3:
                        norm1.dve_stats(dve, t + 1, x_next)
                    if pp == LAST - 2:
                        norm1.dve_scale(dve, t + 1, x_next)
                    if pp == LAST - 1:
                        lower_x(t + 1)
                if ahead:
                    gates(2 * n + 1)

        def pool_slots(pool, t, part):
            def rotate(h):
                pool.wait_ge(raw_ready.sem, raw_ready.at(t, h + 1))
                pool.tensor_tensor(qk[:, h % 4, :, :], raw[:, h % 2, :, :],
                                   rope[:, 0, :].unsqueeze(1).broadcast_to([P, 2, SEQ]), ALU.mult).then_inc(rot_c_ready.sem, 1)

            def rotate_end(h):
                pool.wait_ge(rot_c_ready.sem, rot_c_ready.at(t, h + 1))
                pool.wait_ge(rot_s_ready.sem, rot_s_ready.at(t, h + 1))
                pool.tensor_tensor(qk[:, h % 4, :, :], qk[:, h % 4, :, :], rot_s[:, h % 2, :, :], ALU.add)\
                    .then_inc(qk_ready.sem, 1)

            def lower_qk(h):
                pool.wait_ge(qk_upper.sem, qk_upper.at(t, h + 1))
                pool.tensor_tensor(w_qk[:, 1, :], w1(h, 0, 2 * KC * DK), w_qk[:, 0, :], ALU.subtract).then_inc(qk_lower.sem, 1)

            def lower_vg(h):
                pool.wait_ge(vg_upper.sem, vg_upper.at(t, h + 1))
                pool.tensor_tensor(w_vg[:, 1, :], w1(h, 2 * KC * DK, 2 * KC * DK), w_vg[:, 0, :], ALU.subtract)\
                    .then_inc(vg_lower.sem, 1)

            if part == "first":
                lower_qk(0)

            def lower_es(pp):
                pool.wait_ge(es_ready.sem, es_ready.at(t, pp + 1))
                pool.tensor_tensor(es_split[:, 1, :], es_both[:, pp % 2, 0:SEQ], es_split[:, 0, :], ALU.subtract)\
                    .then_inc(es_lower.sem, 1)

            def rms(pp):
                pool.wait_ge(ssq_ready.sem, ssq_ready.at(t, 2 * pp + 2))
                four = "p c h -> p (c h)"
                pool.tensor_tensor(ms.rearrange(four), ssq.rearrange(four), eps_dk, ALU.add).then_inc(rms_step.sem, 1)
                pool.wait_ge(rms_step.sem, rms_step.at(t, 2 * pp + 1))
                pool.tensor_tensor(rstd1.rearrange(four), ms.rearrange(four), minus_half[:, 0:ST * 2], ALU.pow)\
                    .then_inc(rms_step.sem, 1)
                pool.wait_ge(rms_step.sem, rms_step.at(t, 2 * pp + 2))
                pool.tensor_tensor(comb.rearrange(four), rstd1.rearrange(four), rs.rearrange(four), ALU.mult)\
                    .then_inc(comb_ready.sem, 1)

            for pp in (-1, 0) if part == "first" else range(1, PAIR1 + 1):
                further, ahead, now, behind = steps(pp, part)
                if pp == LAST - 2 and part != "last":
                    norm1.pool_all(pool, t + 1)
                if behind:
                    rms(pp - 1)
                if ahead:
                    lower_es(pp + 1)
                    lower_qk(2 * pp + 3)
                    rotate(2 * pp + 2)
                if now:
                    pool.wait_ge(okp_ready.sem, okp_ready.at(t, pp + 1))
                    pool.tensor_tensor(qe, okp.rearrange("p c h m -> p c (h m)"), enz[:, pp % 2, :, :], ALU.mult)\
                        .then_inc(qe_ready.sem, 1)
                if pp == LAST and not ahead:
                    norm2.pool_all(pool, 0)
                if ahead:
                    rotate_end(2 * pp + 2)
                    rotate(2 * pp + 3)
                    rotate_end(2 * pp + 3)
                if further:
                    lower_qk(2 * pp + 4)
                    lower_vg(2 * pp + 4)

        used["experts"] = RAW_AT
        norm2 = Norm("experts", CT, [ps[:, kc, :] for kc in range(KC)])
        moe1 = MoE("experts", E1, K1, NT1, sel1, lower1, 2, None, before=moe0)

        block = ctx.enter_context(nc.Block())
        first_loads = [(ident, "ident"), (cols, "cols")]
        const_loads = [(causal, "causal"), (router0, "router0"),
                       (lower0, "lower0"), (lower1, "lower1"), (router1, "router1"), (rope, "rope"), (tri, "tri"),
                       (keep_a, "keep_a"), (keep_w, "keep_w"), (s1w, "s1w"),
                       (weights[0:RS, W0S:W0S + NH1 * M], "s2w")]
        row_loads = [(expert_rows[:, 0, :], "extra_scale"),
                     (expert_rows[:, 1, :], "extra_bias")]
        NCONST = 16 * (len(const_loads) + len(row_loads))
        MOE_LOT = [0, 1, 3, 8, 16, NT1]
        MOE_LOTS = len(MOE_LOT) - 1
        w1_loaded = [sem(f"w1_loaded{n}") for n in range(PAIR1)]
        wo1_loaded = sem("wo1_loaded")
        f1_loaded = [sem(f"f1_loaded{n}") for n in range(MOE_LOTS)]
        stored = sem("stored")

        @block.sync
        def _(sp):
            def load_pair(pp):
                at = w1_head(2 * pp + 1)
                sp.dma_start(weights[:, at:at + 2 * HW], A["w1"][:, at:at + 2 * HW]).then_inc(w1_loaded[pp], 16)

            x_tiles = A["x"].rearrange("b (c p) d -> p (b c) d", p=P)
            sp.dma_start(x_res[:, 0:CT, :], x_tiles[:, 0:CT, :]).then_inc(x_first, 16)
            for dst, name in first_loads:
                sp.dma_start(dst[tuple(slice(None) for _ in dst.shape)], A[name]).then_inc(first_loaded, 16)
            for dst, name in const_loads:
                sp.dma_start(dst[tuple(slice(None) for _ in dst.shape)], A[name]).then_inc(consts_loaded, 16)
            for dst, name in row_loads:
                sp.dma_start(dst, A[name].partition_broadcast(P)).then_inc(consts_loaded, 16)
            sp.dma_start(x_res[:, CT:TILES, :], x_tiles[:, CT:TILES, :]).then_inc(x_loaded, 16)
            sp.dma_start(weights[:, W0F:W0F + NT0 * WT].rearrange("p (j w) -> p j w", w=WT),
                         A["f0"].rearrange("j p w -> p j w")).then_inc(f0_loaded, 16)
            load_pair(0)
            sp.wait_ge(moe0.x_ready.sem, 2 * TURNS)
            for pp in range(1, PAIR1):
                load_pair(pp)
                if pp == 1:
                    sp.dma_start(weights[:, W1O:WCOLS], A["wo1"]).then_inc(wo1_loaded, 16)
            sp.wait_ge(qk_lower.sem, qk_lower.at(SEQ_END, NH1))
            sp.wait_ge(vg_lower.sem, vg_lower.at(SEQ_END, NH1))
            for n in range(MOE_LOTS):
                j0, j1 = MOE_LOT[n], MOE_LOT[n + 1]
                if j0 * WT < W1O < j1 * WT:
                    slots_over(sp)
                sp.dma_start(weights[:, j0 * WT:j1 * WT].rearrange("p (j w) -> p j w", w=WT),
                             A["f1"][j0:j1].rearrange("j p w -> p j w")).then_inc(f1_loaded[n], 16)
            with sp.Fori(0, TURNS) as t:
                sp.wait_ge(moe1.x_ready.sem, moe1.x_ready.at(t, 2))
                sp.dma_start(out.rearrange("b (c p) d -> p (b c) d", p=P)[:, bass.ds(t * CT, CT), :],
                             x_res[:, bass.ds(t * CT, CT), :]).then_inc(stored, 16)
            sp.wait_ge(stored, 16 * TURNS)

        @block.gpsimd
        def _(pool):
            pool.dma_start(sel0[:, :], A["sel0"]).then_inc(casts_done, 16)
            pool.dma_start(sel1[:, :], A["sel1"]).then_inc(casts_done, 16)
            for n, value in enumerate((-0.5, EPS, DK * EPS, 0.0)):
                pool.memset(minus_half[:, 16 * n:16 * n + 16], value).then_inc(pow_rows, 1)
            pool.memset(ones_r[:, :].bitcast(F32), 1.0).then_inc(pow_rows, 1)
            pool.wait_ge(pow_rows, 5)
            norm0.pool_all(pool, 0)
            pool.memset(v0, 0.0).then_inc(pow_rows, 1)
            pool.wait_ge(consts_loaded, NCONST)
            pool.wait_ge(s2_upper, 1)
            rows = slice(RG, 2 * RG)
            pool.tensor_tensor(s2_split[rows, :], weights[rows, W0S:W0S + NH1 * M], s2_split[rows, :], ALU.subtract).then_inc(s2_lower, 1)
            pool.wait_ge(s2_lower, 1)

            def layer0(t, more):
                def ahead(j):
                    if j == NORM_TILE:
                        norm0.pool_all(pool, t + 1) if more else norm1.pool_all(pool, 0)

                moe0.ties(pool, t, 0)
                moe0.ties(pool, t, 1)
                moe0.split_coef(pool, t)
                moe0.split_x(pool, t, norm0)
                moe0.pool_lower_gu(pool, t, 0)
                moe0.pool_lower_gu(pool, t, 1)
                moe0.pool_lower_down(pool, t, 0)
                moe0.pool_tiles(pool, t, ahead)
                moe0.pool_lower_down(pool, t, NT0 - 1)

            with pool.Fori(0, TURNS - 1) as t:
                layer0(t, True)
            layer0(TURNS - 1, False)
            pool_slots(pool, 0, "first")
            with pool.Fori(0, SEQ_END) as t:
                pool_slots(pool, t, "middle")
            pool_slots(pool, SEQ_END, "last")
            moe1.pool_lower_gu(pool, 0, 0)
            moe1.pool_lower_gu(pool, 0, 1)
            moe1.pool_lower_down(pool, 0, 0)

            def experts(t, more):
                def ahead(j):
                    if not more:
                        return
                    if j == NORM_TILE:
                        norm2.pool_all(pool, t + 1)
                    if RANK_TILE <= j < RANK_TILE + 2:
                        moe1.ties(pool, t + 1, j - RANK_TILE)
                    if j == COEF_TILE:
                        moe1.split_coef(pool, t + 1)

                moe1.pool_tiles(pool, t, ahead)
                if more:
                    moe1.pool_lower_gu(pool, t + 1, 0)
                moe1.pool_lower_down(pool, t, NT1 - 1)
                if more:
                    moe1.pool_lower_gu(pool, t + 1, 1)
                    moe1.pool_lower_down(pool, t + 1, 0)

            with pool.Fori(0, TURNS - 1) as t:
                experts(t, True)
            experts(TURNS - 1, False)

        @block.vector
        def _(dve):
            dve.wait_ge(x_first, 16)
            norm0.dve_stats(dve, 0, lambda c, n: x_res[:, c:c + n, :])
            dve.wait_ge(first_loaded, 16 * len(first_loads))
            dve.tensor_scalar(bqs[:, :], BQ, HD0 ** -0.5, None, ALU.mult).then_inc(bias_done, 1)
            norm0.dve_scale(dve, 0, lambda c, n: x_res[:, c:c + n, :])
            dve.tensor_copy(ident_b[:, :], ident[:, :]).then_inc(bias_done, 1)
            dve.wait_ge(consts_loaded, NCONST)
            dve.tensor_scalar(g_half[:, :], G_NORM, 0.5 * DK ** 0.5, None, ALU.mult).then_inc(bias_done, 1)
            dve.tensor_copy(causal_b[:, :].rearrange("p (a n) -> p a n", a=2), causal[:, :].unsqueeze(1).broadcast_to([P, 2, P])).then_inc(bias_done, 1)
            dve.memset(s1_split[0:2 * RG, :].bitcast(F32), 1.0).then_inc(bias_done, 1)
            dve.memset(s1_split[2 * RG:RS, :].bitcast(F32), 0.0).then_inc(bias_done, 1)
            dve.wait_ge(x_loaded, 16)

            def layer0(t, more):
                def x_now(c, n):
                    return x_res[:, bass.ds(t * CT + c, n), :]

                def x_next(c, n):
                    return x_res[:, bass.ds((t + 1) * CT + c, n), :]

                def first_tokens(c, n):
                    return x_res[:, c:c + n, :]

                def ahead(j):
                    norm, turn, tokens = (norm0, t + 1, x_next) if more else (norm1, 0, first_tokens)
                    if j == NORM_TILE:
                        norm.dve_stats(dve, turn, tokens)
                    if j == NORM_TILE + 1:
                        norm.dve_scale(dve, turn, tokens)

                dve_layer0(dve, t)
                moe0.dve_tiles(dve, t, ahead)
                if not more:
                    dve_slots(dve, 0, None, "before")
                dve.wait_ge(sT_ready.sem, sT_ready.at(t, KC))
                moe0.dve_out(dve, t, sT0, x_now)

            with dve.Fori(0, TURNS - 1) as t:
                layer0(t, True)
            layer0(TURNS - 1, False)
            dve.wait_ge(moe0.x_ready.sem, 2 * TURNS)
            dve_slots(dve, 0, None, "first")
            with dve.Fori(0, SEQ_END) as t:
                dve_slots(dve, t, lambda c, n: x_res[:, bass.ds((t + 1) * ST + c, n), :], "middle")
            dve_slots(dve, SEQ_END, None, "last")
            moe1.split_x(dve, 0, norm2)
            moe1.dve_router_probs(dve, 0)
            moe1.dve_router_compare(dve, 0, 0)
            moe1.dve_router_compare(dve, 0, 1)
            moe1.ties(dve, 0, 0)
            moe1.ties(dve, 0, 1)
            moe1.dve_router_choose(dve, 0)
            moe1.split_coef(dve, 0)
            slots_over(dve)

            def experts(t, more):
                def x_now(c, n):
                    return x_res[:, bass.ds(t * CT + c, n), :]

                def x_next(c, n):
                    return x_res[:, bass.ds((t + 1) * CT + c, n), :]

                def ahead(j):
                    if not more:
                        return
                    if j == NORM_TILE:
                        norm2.dve_stats(dve, t + 1, x_next)
                    if j == NORM_TILE + 1:
                        norm2.dve_scale(dve, t + 1, x_next)
                    if j == TOKENS_TILE + 1:
                        moe1.dve_router_scores(dve, t + 1)
                    if j == EXP_TILE + 1:
                        moe1.dve_router_probs(dve, t + 1)
                    if RANK_TILE - 2 <= j < RANK_TILE:
                        moe1.dve_router_compare(dve, t + 1, j - RANK_TILE + 2)
                    if j == COEF_TILE - 2:
                        moe1.dve_router_choose(dve, t + 1)

                moe1.dve_tiles(dve, t, ahead)
                if more:
                    moe1.split_x(dve, t + 1, norm2)
                moe1.dve_out(dve, t, sT1[:, :, bass.ds(t * CH, CH)], x_now)

            with dve.Fori(0, TURNS - 1) as t:
                experts(t, True)
            experts(TURNS - 1, False)

        @block.scalar
        def _(act):
            act.dma_start(weights[:, W0Q:W0F], A["w0"]).then_inc(w0_loaded, 16)
            norm0.act_all(act, 0)
            act.wait_ge(bias_done, 6)
            act.wait_ge(pow_rows, 6)
            act.wait_ge(consts_loaded, NCONST)
            act.copy(tri_r[:, :], tri[:, :])
            act.copy(s2_split[:, :], weights[0:RS, W0S:W0S + NH1 * M]).then_inc(s2_upper, 1)

            def layer0(t, more):
                def ahead(j):
                    if TURN_TILE <= j < TURN_TILE + KC:
                        if more:
                            norm0.act_copy(act, t + 1, j - TURN_TILE)
                        else:
                            norm1.act_copy(act, 0, j - TURN_TILE, spread_banks)

                act_layer0(act, t)
                moe0.act_upper_down(act, t, 1)
                moe0.act_upper_gu(act, t, 3)
                moe0.act_tiles(act, t, ahead, lambda j: None)
                moe0.act_upper_down(act, t, NT0 - 1)
                if not more:
                    act_slots(act, 0, "before")
                moe0.act_out(act, t)
                act.wait_ge(moe0.delta_turned.sem, moe0.delta_turned.at(t, 1))

            with act.Fori(0, TURNS - 1) as t:
                layer0(t, True)
            layer0(TURNS - 1, False)
            act_slots(act, 0, "first")
            with act.Fori(0, SEQ_END) as t:
                act_slots(act, t, "middle")

            def loaded(j):
                if j in MOE_LOT:
                    act.wait_ge(f1_loaded[MOE_LOT.index(j)], 16)

            act_slots(act, SEQ_END, "last")
            moe1.act_coef(act, 0, 1)

            def experts(t, more):
                def ahead(j):
                    if not more:
                        return
                    if TURN_TILE <= j < TURN_TILE + KC:
                        norm2.act_copy(act, t + 1, j - TURN_TILE)
                    if j == LOGITS_TILE:
                        moe1.act_logits(act, t + 1, j % 2)
                    if j == TOKENS_TILE:
                        moe1.act_tokens(act, t + 1, j % 2)
                    if j == EXP_TILE:
                        moe1.act_exp(act, t + 1)

                moe1.act_upper_down(act, t, 1)
                moe1.act_tanh(act, t, 0)
                moe1.act_upper_gu(act, t, 2)
                moe1.act_tanh(act, t, 1)
                loaded(3)
                moe1.act_upper_gu(act, t, 3)
                moe1.act_tiles(act, t, ahead, loaded)
                act.wait_ge(moe1.gate_up_done.sem, moe1.gate_up_done.at(t, NT1))
                if more:
                    moe1.act_split_x(act, t + 1, norm2)
                    moe1.act_upper_gu(act, t + 1, 0)
                moe1.act_upper_down(act, t, NT1 - 1)
                if more:
                    moe1.act_upper_gu(act, t + 1, 1)
                    moe1.act_coef(act, t + 1, 1)
                moe1.act_out(act, t)
                if more:
                    moe1.act_upper_down(act, t + 1, 0)

            with act.Fori(0, TURNS - 1) as t:
                experts(t, True)
            experts(TURNS - 1, False)

        @block.tensor
        def _(pe):
            pe.wait_ge(first_loaded, 16 * len(first_loads))
            norm0.pe_all(pe, 0)
            pe.wait_ge(w0_loaded, 16)
            pe_queries_keys(pe, 0, 0)
            pe_queries_keys(pe, 0, 1)
            pe_values(pe, 0, 0)
            pe.wait_ge(consts_loaded, NCONST)
            pe.wait_ge(bias_done, 4)
            pe.wait_ge(pow_rows, 6)
            pe.wait_ge(casts_done, 32)

            def layer0(t, more):
                def ahead(j):
                    if TURN_TILE <= j < TURN_TILE + KC:
                        if more:
                            norm0.pe_turn(pe, t + 1, j - TURN_TILE)
                        else:
                            norm1.pe_turn(pe, 0, j - TURN_TILE, spread_banks)

                def bank_read(j):
                    if j == 2:
                        pe.wait_ge(sT_ready.sem, sT_ready.at(t, KC))
                    if TURN_TILE <= j < TURN_TILE + KC:
                        norm, turn = (norm0, t + 1) if more else (norm1, 0)
                        pe.wait_ge(norm.xT_ready.sem, norm.xT_ready.at(turn, j - TURN_TILE + 1))

                pe_layer0(pe, t)
                moe0.pe_tiles(pe, t, ahead, bank_read)
                if more:
                    pe_queries_keys(pe, t + 1, 0)
                moe0.pe_down(pe, t, NT0 - 1)
                if more:
                    pe_queries_keys(pe, t + 1, 1)
                else:
                    pe_slots(pe, 0, "before")
                moe0.pe_delta(pe, t)
                if more:
                    pe_values(pe, t + 1, 0)
                pe.wait_ge(moe0.x_ready.sem, moe0.x_ready.at(t, 2))

            with pe.Fori(0, TURNS - 1) as t:
                layer0(t, True)
            layer0(TURNS - 1, False)
            pe_slots(pe, 0, "first")
            with pe.Fori(0, SEQ_END) as t:
                pe_slots(pe, t, "middle")
            pe_slots(pe, SEQ_END, "last")
            moe1.pe_gate_up(pe, 0, 0)
            moe1.pe_gate_up(pe, 0, 1)
            moe1.pe_coef(pe, 0, 1)
            slots_over(pe)

            def experts(t, more):
                def ahead(j):
                    if not more:
                        return
                    if TURN_TILE <= j < TURN_TILE + KC:
                        norm2.pe_turn(pe, t + 1, j - TURN_TILE)
                    if j == LOGITS_TILE:
                        moe1.pe_logits(pe, t + 1, norm2.xT, router1, j % 2)
                    if j == TOKENS_TILE:
                        moe1.pe_router(pe, t + 1, j % 2)

                def bank_read(j):
                    if not more:
                        return
                    if TURN_TILE <= j < TURN_TILE + KC:
                        pe.wait_ge(norm2.xT_ready.sem, norm2.xT_ready.at(t + 1, j - TURN_TILE + 1))
                    if j == LOGITS_TILE:
                        pe.wait_ge(moe1.logits_copied.sem, moe1.logits_copied.at(t + 1, 1))
                    if j == TOKENS_TILE:
                        pe.wait_ge(moe1.tokens_copied.sem, moe1.tokens_copied.at(t + 1, 1))

                moe1.pe_spread(pe, t, 0)
                moe1.pe_spread(pe, t, 1)
                moe1.pe_tiles(pe, t, ahead, bank_read)
                if more:
                    moe1.pe_coef(pe, t + 1, 1)
                moe1.pe_down(pe, t, NT1 - 1)
                if more:
                    moe1.pe_gate_up(pe, t + 1, 0)
                moe1.pe_delta(pe, t)
                if more:
                    moe1.pe_gate_up(pe, t + 1, 1)
                pe.wait_ge(moe1.x_ready.sem, moe1.x_ready.at(t, 2))

            with pe.Fori(0, TURNS - 1) as t:
                experts(t, True)
            experts(TURNS - 1, False)


def _constants():
    p = np.arange(P)
    tri_jt = (p[:, None] <= p[None, :]).astype(np.float32)
    one = np.ones((P, P), np.float32)
    bias = np.where(p[None, :] > p[:, None], np.float32(NEG), np.float32(0)).astype(np.float32)
    keep = np.concatenate([tri_jt, one, tri_jt], 1)
    inv_freq = 1.0 / np.float32(10000.0) ** (np.arange(0, DK, 2, dtype=np.float32) / np.float32(DK))
    ang = (np.arange(SEQ, dtype=np.float32)[:, None] * inv_freq[None, :].astype(np.float32)).astype(np.float32)
    cos, sin = np.cos(ang).T.astype(np.float32), np.sin(ang).T.astype(np.float32)

    def sel(experts, f, tiles):
        row = np.minimum(np.arange(tiles * P) // f, experts)
        hot = (row[None, :] == np.arange(experts + 1)[:, None]).astype(np.float32)
        return np.concatenate([hot] * 3, 0)

    def lower(e):
        n = np.arange(e)
        return np.ascontiguousarray(np.broadcast_to((n[None, :] < n[:, None]).astype(np.float32).reshape(1, e * e), (P, e * e)))

    return {
        "ident": np.eye(P, dtype=np.float32),
        "causal": bias,
        "sel0": sel(E0, F0, NT0), "sel1": sel(E1, F1, NT1),
        "lower0": lower(E0), "lower1": lower(E1),
        "rope": np.stack([np.concatenate([cos, cos], 0), np.concatenate([sin, -sin], 0)], 1),
        "tri": tri_jt, "keep_a": keep * np.float32(SCALE1), "keep_w": keep,
    }


def _chunks(w_t):
    return w_t.reshape(KC, P, -1).transpose(1, 0, 2)


def _moe_tiles(wg, wu, wd, sg, su, sd, tiles):
    e, f, d = wg.shape
    pad = tiles * P - e * f - sg.shape[0]
    z = np.zeros((pad, d), wg.dtype)
    gate = np.concatenate([wg.reshape(e * f, d), sg, z], 0).reshape(tiles, P, KC, P).transpose(0, 3, 2, 1)
    up = np.concatenate([wu.reshape(e * f, d), su, z], 0).reshape(tiles, P, KC, P).transpose(0, 3, 2, 1)
    down = np.concatenate([wd.transpose(0, 2, 1).reshape(e * f, d), sd.T, z], 0).reshape(tiles, P, d)
    return np.concatenate([gate.reshape(tiles, P, KC * P), up.reshape(tiles, P, KC * P), down], 2)


def layout(i):
    c = _constants()
    p = np.arange(P)
    mask = ((p[:, None] // HD0) % HPQ == np.arange(HPQ)[None, :]).astype(np.float32)
    col = [i["L0_attn_" + n].reshape(KC, P).T for n in ("bq", "bk", "bv", "bo")]
    c["cols"] = np.concatenate([mask, *col, i["L1_attn_g_norm_weight"].reshape(DK, 1), np.zeros((P, 3), np.float32)], 1)
    c["x"] = i["L0_attn_hidden_states"]
    c["w0"] = np.stack([_chunks(i["L0_attn_" + n].T) for n in ("wq", "wk", "wv", "wo")], 1).reshape(P, -1)
    c["f0"] = _moe_tiles(i["L0_ffn_Wg"], i["L0_ffn_Wu"], i["L0_ffn_Wd"], i["L0_ffn_Wsg"], i["L0_ffn_Wsu"],
                         i["L0_ffn_Wsd"], NT0)
    c["router0"] = _chunks(i["L0_ffn_Wr"].T)
    c["f1"] = _moe_tiles(i["L1_ffn_Wg"], i["L1_ffn_Wu"], i["L1_ffn_Wd"], i["L1_ffn_Sg"], i["L1_ffn_Su"],
                         i["L1_ffn_Sd"], NT1)
    c["router1"] = _chunks(np.concatenate([i["L1_ffn_rg_w"], i["L1_ffn_ru_w"]], 0).T)
    pad = np.zeros((RG - R1, D), np.float32)
    c["s1w"] = _chunks(np.concatenate([i["L1_attn_Ws1"], pad] * 3, 0).T)
    pad = np.zeros((RG - R1 - 1, NH1 * M), np.float32)
    c["s2w"] = np.concatenate([i["L1_attn_Ws2"].T, i["L1_attn_bs2"][None, :], pad] * 3, 0)
    c["extra_scale"], c["extra_bias"] = i["L1_ffn_extra_scale"], i["L1_ffn_extra_bias"]
    wq, wk, wv, wg = (i["L1_attn_" + n].T.reshape(KC, P, NH1, DK).transpose(2, 1, 0, 3) for n in ("Wq", "Wk", "Wv", "Wg"))
    vg = np.concatenate([wv, wg], 3)
    heads = np.concatenate([a.reshape(NH1, P, -1) for a in (wq, wk, vg)], 2)
    c["w1"] = heads[::-1].transpose(1, 0, 2).reshape(P, -1)
    c["wo1"] = i["L1_attn_Wo"].T.reshape(NH1, DK, D).transpose(1, 0, 2).reshape(P, -1)
    return {k: np.ascontiguousarray(v) for k, v in c.items()}


def kernel(**inputs):
    import concourse.bacc as bacc
    from concourse.bass_utils import run_bass_kernel_spmd

    arrays = layout({k: np.asarray(v) for k, v in inputs.items()})
    nc = bacc.Bacc("TRN2", target_bir_lowering=False, num_devices=1)
    A = {k: nc.dram_tensor("in_" + k, v.shape, mybir.dt.from_np(v.dtype), kind="ExternalInput").ap()
         for k, v in arrays.items()}
    out = nc.dram_tensor("out_x", (BATCH, SEQ, D), F32, kind="ExternalOutput").ap()
    build(nc, A, out)
    r = run_bass_kernel_spmd(nc, [{"in_" + k: v for k, v in arrays.items()}], core_ids=[0])
    return r.results[0]["out_x"]
```
